# Optimizing a Trainium2 kernel written in Bass

```python
import numpy as np
import jax
import jax.numpy as jnp

def _softmax(x, axis=-1):
    return jax.nn.softmax(x, axis=axis)

def _gelu(x):
    return jax.nn.gelu(x, approximate=True)

def _silu(x):
    return jax.nn.silu(x)

def _sigmoid(x):
    return jax.nn.sigmoid(x)

def _layernorm(x, axis=-1, eps=1e-05):
    m = jnp.mean(x, axis=axis, keepdims=True)
    v = jnp.var(x, axis=axis, keepdims=True)
    return (x - m) / jnp.sqrt(v + eps)

def _scatter_add(tgt, idx, src, axis=0):
    return tgt.at[idx].add(src)

def _segment_sum(src, seg, n):
    return jax.ops.segment_sum(src, seg, n)
kernel_name = 'mk_conv_attn_hybrid_d2_conv_nhwc768_r4_bb84ef'

def setup_inputs(seed: int=0):
    np.random.seed(seed)
    _w = jnp.asarray

    def _rec_inputs():
        import jax
        import jax.numpy as jnp
        _gk = jax.random.key(seed)
        x = -0.0002221 + 1 * jax.random.normal(jax.random.fold_in(_gk, 1), (8, 16, 16, 192), jnp.float32)
        return x
    x = _rec_inputs()

    def _L0_conv_setup():
        import jax, jax.numpy as jnp
        import numpy as np
        B, H, W, D = (8, 16, 16, 192)
        HEADS, WS = (12, 14)
        HD = D // HEADS
        MLP = 4 * D
        LREL = 2 * WS - 1
        EPS = 1e-05

        def _layer_norm(x, w, b):
            mu = jnp.mean(x, axis=-1, keepdims=True)
            var = jnp.mean(jnp.square(x - mu), axis=-1, keepdims=True)
            return (x - mu) * jax.lax.rsqrt(var + EPS) * w + b
        key = jax.random.key(seed)
        ks = jax.random.split(key, 12)
        s = 0.02
        return {'x': jax.random.normal(ks[0], (B, H, W, D), jnp.float32), 'qkv_w': jax.random.normal(ks[1], (D, 3 * D), jnp.float32) * s, 'qkv_b': jax.random.normal(ks[2], (3 * D,), jnp.float32) * s, 'proj_w': jax.random.normal(ks[3], (D, D), jnp.float32) * s, 'proj_b': jax.random.normal(ks[4], (D,), jnp.float32) * s, 'rel_pos_h': jax.random.normal(ks[5], (LREL, HD), jnp.float32) * s, 'rel_pos_w': jax.random.normal(ks[6], (LREL, HD), jnp.float32) * s, 'norm1_w': jnp.ones((D,), jnp.float32), 'norm1_b': jnp.zeros((D,), jnp.float32), 'norm2_w': jnp.ones((D,), jnp.float32), 'norm2_b': jnp.zeros((D,), jnp.float32), 'fc1_w': jax.random.normal(ks[7], (D, MLP), jnp.float32) * s, 'fc1_b': jax.random.normal(ks[8], (MLP,), jnp.float32) * s, 'fc2_w': jax.random.normal(ks[9], (MLP, D), jnp.float32) * s, 'fc2_b': jax.random.normal(ks[10], (D,), jnp.float32) * s}
    _L0_conv_all = _L0_conv_setup()
    _L0_conv_in = {k: v for k, v in _L0_conv_all.items() if k in ('qkv_w', 'qkv_b', 'proj_w', 'proj_b', 'rel_pos_h', 'rel_pos_w', 'norm1_w', 'norm1_b', 'norm2_w', 'norm2_b', 'fc1_w', 'fc1_b', 'fc2_w', 'fc2_b')}
    del _L0_conv_all

    def _L1_attn_setup():
        import jax, jax.numpy as jnp
        import numpy as np
        CONTEXT_LENGTH = 256
        key = jax.random.key(seed)
        ks = jax.random.split(key, 6)
        B, T, C, nh, hs = (4, 256, 192, 12, 16)
        stdv = 1.0 / np.sqrt(C)
        x = jax.random.normal(ks[0], (B, T, C), dtype=jnp.float32)
        W_q = jax.random.uniform(ks[1], (nh, C, hs), minval=-stdv, maxval=stdv, dtype=jnp.float32)
        W_k = jax.random.uniform(ks[2], (nh, C, hs), minval=-stdv, maxval=stdv, dtype=jnp.float32)
        W_v = jax.random.uniform(ks[3], (nh, C, hs), minval=-stdv, maxval=stdv, dtype=jnp.float32)
        lin_w = jax.random.normal(ks[4], (C, C), dtype=jnp.float32) * (1.0 / np.sqrt(C))
        lin_b = jnp.zeros((C,), dtype=jnp.float32)
        return {'x': x, 'W_q': W_q, 'W_k': W_k, 'W_v': W_v, 'lin_w': lin_w, 'lin_b': lin_b}
    _L1_attn_all = _L1_attn_setup()
    _L1_attn_in = {k: v for k, v in _L1_attn_all.items() if k in ('W_q', 'W_k', 'W_v', 'lin_w', 'lin_b')}
    del _L1_attn_all

    def _L1_ffn_setup():
        import jax, jax.numpy as jnp
        import numpy as np
        TOP_K = 2
        TEMP = 1.0
        key = jax.random.key(seed)
        ks = jax.random.split(key, 7)
        B, T, D, E = (2, 512, 192, 8)
        F = 4 * D
        s = 0.02
        return {'x': jax.random.normal(ks[0], (B, T, D), dtype=jnp.float32), 'gate_w': jax.random.normal(ks[1], (D, E), dtype=jnp.float32) * s, 'gate_b': jnp.zeros((E,), dtype=jnp.float32), 'w1': jax.random.normal(ks[2], (E, D, F), dtype=jnp.float32) * s, 'b1': jnp.zeros((E, F), dtype=jnp.float32), 'w2': jax.random.normal(ks[3], (E, F, D), dtype=jnp.float32) * s, 'b2': jnp.zeros((E, D), dtype=jnp.float32)}
    _L1_ffn_all = _L1_ffn_setup()
    _L1_ffn_in = {k: v for k, v in _L1_ffn_all.items() if k in ('gate_w', 'gate_b', 'w1', 'b1', 'w2', 'b2')}
    del _L1_ffn_all
    return {'x': x, 'L0_conv_qkv_w': _L0_conv_in['qkv_w'], 'L0_conv_qkv_b': _L0_conv_in['qkv_b'], 'L0_conv_proj_w': _L0_conv_in['proj_w'], 'L0_conv_proj_b': _L0_conv_in['proj_b'], 'L0_conv_rel_pos_h': _L0_conv_in['rel_pos_h'], 'L0_conv_rel_pos_w': _L0_conv_in['rel_pos_w'], 'L0_conv_norm1_w': _L0_conv_in['norm1_w'], 'L0_conv_norm1_b': _L0_conv_in['norm1_b'], 'L0_conv_norm2_w': _L0_conv_in['norm2_w'], 'L0_conv_norm2_b': _L0_conv_in['norm2_b'], 'L0_conv_fc1_w': _L0_conv_in['fc1_w'], 'L0_conv_fc1_b': _L0_conv_in['fc1_b'], 'L0_conv_fc2_w': _L0_conv_in['fc2_w'], 'L0_conv_fc2_b': _L0_conv_in['fc2_b'], 'L1_attn_W_q': _L1_attn_in['W_q'], 'L1_attn_W_k': _L1_attn_in['W_k'], 'L1_attn_W_v': _L1_attn_in['W_v'], 'L1_attn_lin_w': _L1_attn_in['lin_w'], 'L1_attn_lin_b': _L1_attn_in['lin_b'], 'L1_ffn_gate_w': _L1_ffn_in['gate_w'], 'L1_ffn_gate_b': _L1_ffn_in['gate_b'], 'L1_ffn_w1': _L1_ffn_in['w1'], 'L1_ffn_b1': _L1_ffn_in['b1'], 'L1_ffn_w2': _L1_ffn_in['w2'], 'L1_ffn_b2': _L1_ffn_in['b2']}

def reference(x, L0_conv_qkv_w, L0_conv_qkv_b, L0_conv_proj_w, L0_conv_proj_b, L0_conv_rel_pos_h, L0_conv_rel_pos_w, L0_conv_norm1_w, L0_conv_norm1_b, L0_conv_norm2_w, L0_conv_norm2_b, L0_conv_fc1_w, L0_conv_fc1_b, L0_conv_fc2_w, L0_conv_fc2_b, L1_attn_W_q, L1_attn_W_k, L1_attn_W_v, L1_attn_lin_w, L1_attn_lin_b, L1_ffn_gate_w, L1_ffn_gate_b, L1_ffn_w1, L1_ffn_b1, L1_ffn_w2, L1_ffn_b2):
    import jax
    import jax.numpy as jnp

    def _L0_conv_ref(x, qkv_w, qkv_b, proj_w, proj_b, rel_pos_h, rel_pos_w, norm1_w, norm1_b, norm2_w, norm2_b, fc1_w, fc1_b, fc2_w, fc2_b):
        import jax, jax.numpy as jnp
        import numpy as np
        B, H, W, D = (8, 16, 16, 192)
        HEADS, WS = (12, 14)
        HD = D // HEADS
        MLP = 4 * D
        LREL = 2 * WS - 1
        EPS = 1e-05

        def _layer_norm(x, w, b):
            mu = jnp.mean(x, axis=-1, keepdims=True)
            var = jnp.mean(jnp.square(x - mu), axis=-1, keepdims=True)
            return (x - mu) * jax.lax.rsqrt(var + EPS) * w + b
        shortcut = x
        xn = _layer_norm(x, norm1_w, norm1_b)
        pad_h = (WS - H % WS) % WS
        pad_w = (WS - W % WS) % WS
        Hp, Wp = (H + pad_h, W + pad_w)
        xp = jnp.pad(xn, ((0, 0), (0, pad_h), (0, pad_w), (0, 0)))
        win = xp.reshape(B, Hp // WS, WS, Wp // WS, WS, D)
        win = win.transpose(0, 1, 3, 2, 4, 5).reshape(-1, WS, WS, D)
        Bn = win.shape[0]
        N = WS * WS
        qkv = win.reshape(Bn, N, D) @ qkv_w + qkv_b
        qkv = qkv.reshape(Bn, N, 3, HEADS, HD).transpose(2, 0, 3, 1, 4)
        qkv = qkv.reshape(3, Bn * HEADS, N, HD)
        q, k, v = (qkv[0], qkv[1], qkv[2])
        scale = HD ** (-0.5)
        attn = jnp.einsum('bqc,bkc->bqk', q * scale, k)
        coords = jnp.arange(WS)[:, None] - jnp.arange(WS)[None, :] + (WS - 1)
        Rh = rel_pos_h[coords]
        Rw = rel_pos_w[coords]
        r_q = q.reshape(-1, WS, WS, HD)
        rel_h = jnp.einsum('bhwc,hkc->bhwk', r_q, Rh)
        rel_w = jnp.einsum('bhwc,wkc->bhwk', r_q, Rw)
        attn = (attn.reshape(-1, WS, WS, WS, WS) + rel_h[:, :, :, :, None] + rel_w[:, :, :, None, :]).reshape(-1, N, N)
        attn = jax.nn.softmax(attn, axis=-1)
        out = jnp.einsum('bqk,bkc->bqc', attn, v)
        out = out.reshape(Bn, HEADS, WS, WS, HD).transpose(0, 2, 3, 1, 4).reshape(Bn, WS, WS, D)
        out = out @ proj_w + proj_b
        out = out.reshape(B, Hp // WS, Wp // WS, WS, WS, D)
        out = out.transpose(0, 1, 3, 2, 4, 5).reshape(B, Hp, Wp, D)[:, :H, :W, :]
        x = shortcut + out
        xn2 = _layer_norm(x, norm2_w, norm2_b)
        h = jax.nn.gelu(xn2 @ fc1_w + fc1_b, approximate=False)
        x = x + (h @ fc2_w + fc2_b)
        return x

    def _L1_attn_ref(x, W_q, W_k, W_v, lin_w, lin_b):
        import jax, jax.numpy as jnp
        import numpy as np
        CONTEXT_LENGTH = 256
        B, T, C = x.shape
        Q = jnp.einsum('btc,hcd->bhtd', x, W_q)
        K = jnp.einsum('btc,hcd->bhtd', x, W_k)
        V = jnp.einsum('btc,hcd->bhtd', x, W_v)
        scale = 1.0 / jnp.sqrt(jnp.asarray(CONTEXT_LENGTH, dtype=x.dtype))
        score = jnp.einsum('bhtd,bhsd->bhts', Q, K) * scale
        causal = jnp.tril(jnp.ones((T, T), dtype=bool))
        score = jnp.where(causal[None, None, :, :], score, jnp.asarray(-jnp.inf, dtype=score.dtype))
        attn = jax.nn.softmax(score, axis=-1)
        out = jnp.einsum('bhts,bhsd->bhtd', attn, V)
        res = out.transpose(0, 2, 1, 3).reshape(B, T, C)
        res = jnp.einsum('btc,oc->bto', res, lin_w) + lin_b
        return res

    def _L1_ffn_ref(x, gate_w, gate_b, w1, b1, w2, b2):
        import jax, jax.numpy as jnp
        import numpy as np
        TOP_K = 2
        TEMP = 1.0
        B, T, D = x.shape
        E = gate_w.shape[1]
        x_flat = x.reshape(-1, D)
        logits = x_flat @ gate_w + gate_b
        gates = jax.nn.softmax(logits / TEMP, axis=-1)
        topk_gates, topk_idx = jax.lax.top_k(gates, TOP_K)
        topk_gates = topk_gates / (jnp.sum(topk_gates, axis=-1, keepdims=True) + 1e-09)
        combine = jnp.sum(topk_gates[:, :, None] * jax.nn.one_hot(topk_idx, E, dtype=x.dtype), axis=1)
        out = jnp.zeros_like(x_flat)
        for e in range(E):
            h = jax.nn.gelu(x_flat @ w1[e] + b1[e], approximate=False)
            y = h @ w2[e] + b2[e]
            out = out + combine[:, e:e + 1] * y
        return out.reshape(B, T, D)

    def _gn(v, G=32, eps=1e-05):
        B_, H_, W_, C_ = v.shape
        g = v.reshape(B_, H_, W_, G, C_ // G)
        m = jnp.mean(g, axis=(1, 2, 4), keepdims=True)
        s = jnp.var(g, axis=(1, 2, 4), keepdims=True)
        return ((g - m) / jnp.sqrt(s + eps)).reshape(v.shape)

    def _ln_c(v, eps=1e-06):
        m = jnp.mean(v, axis=-1, keepdims=True)
        s = jnp.var(v, axis=-1, keepdims=True)
        return (v - m) / jnp.sqrt(s + eps)

    def _ln_t(v, eps=1e-05):
        m = jnp.mean(v, axis=-1, keepdims=True)
        s = jnp.var(v, axis=-1, keepdims=True)
        return (v - m) / jnp.sqrt(s + eps)

    def _to_tokens(v):
        B_, H_, W_, C_ = v.shape
        return v.reshape(B_, H_ * W_, C_)

    def _from_tokens(t, like):
        return t.reshape(like.shape)
    x = _L0_conv_ref(x, L0_conv_qkv_w, L0_conv_qkv_b, L0_conv_proj_w, L0_conv_proj_b, L0_conv_rel_pos_h, L0_conv_rel_pos_w, L0_conv_norm1_w, L0_conv_norm1_b, L0_conv_norm2_w, L0_conv_norm2_b, L0_conv_fc1_w, L0_conv_fc1_b, L0_conv_fc2_w, L0_conv_fc2_b)
    t = _to_tokens(x)
    t = t + _L1_attn_ref(_ln_t(t), L1_attn_W_q, L1_attn_W_k, L1_attn_W_v, L1_attn_lin_w, L1_attn_lin_b)
    t = t + _L1_ffn_ref(_ln_t(t), L1_ffn_gate_w, L1_ffn_gate_b, L1_ffn_w1, L1_ffn_b1, L1_ffn_w2, L1_ffn_b2)
    x = _from_tokens(t, x)
    return x

_drawn_inputs = setup_inputs


def setup_inputs(seed=0):
    import zlib

    import numpy as np

    out = dict(_drawn_inputs(seed))
    spreads = {'L0_conv_norm1_w': (1.0, 0.6),
     'L0_conv_norm1_b': (0.0, 0.609),
     'L0_conv_norm2_w': (1.0, 0.6),
     'L0_conv_norm2_b': (0.0, 0.579),
     'L1_attn_lin_b': (0.0, 0.1),
     'L1_ffn_gate_b': (0.0, 0.1),
     'L1_ffn_b1': (0.0, 0.378),
     'L1_ffn_b2': (0.0, 0.1)}
    factors = {'L0_conv_qkv_w': 4.472,
     'L0_conv_qkv_b': 5.341,
     'L0_conv_proj_w': 3.424,
     'L0_conv_rel_pos_h': 8.0,
     'L0_conv_rel_pos_w': 8.0,
     'L0_conv_fc1_b': 6.558,
     'L1_attn_W_q': 5.859,
     'L1_attn_W_k': 5.602,
     'L0_conv_proj_b': 4.074,
     'L0_conv_fc2_b': 3.939}
    for name, (base, spread) in spreads.items():
        noise = np.random.default_rng([zlib.crc32(name.encode()), seed]).standard_normal(out[name].shape)
        drawn = base * np.exp(spread * noise) if base else spread * noise
        out[name] = jnp.asarray(drawn.astype(out[name].dtype))
    for name, factor in factors.items():
        out[name] = (out[name] * factor).astype(out[name].dtype)
    return out
```

```python
from contextlib import ExitStack

import numpy as np

import concourse.bass as bass
from concourse import mybir

F32 = mybir.dt.float32
F32R = mybir.dt.float32r
BF16 = mybir.dt.bfloat16
U32 = mybir.dt.uint32
I32 = mybir.dt.int32
ALU = mybir.AluOpType
ACT = mybir.ActivationFunctionType
AX = mybir.AxisListType

P = 128
B, S, D = 8, 16, 192
TOK = S * S
NT = B * TOK // P
HEADS, HD, WS = 12, 16, 14
PAIRS, GROUPS = HEADS // 2, HEADS // 4
DC = D // 2
MLP = 4 * D
FT = MLP // P
NE = 8
WIN = WS * WS
HALF = WIN // 2
OUT = TOK - WIN
KEYS = TOK + WIN
EDGE = (S - WS) * WS
SLOT = 64
REL = 32
MAXROW = 60
MAXROW_B = 32
BIG = 1.0e30
NTILE = 2 * B * TOK // P + NE
SCALE_A, SCALE_B = 0.25, 0.0625
EPS = 1e-5


def window_pieces(t):
    return t[..., 0:WS, 0:WS], t[..., 0:WS, WS:S], t[..., WS:S, 0:S]


def build(nc, a, out):
    scratch = nc.dram_tensor("qk_scratch", (2, 2, 4, DC, TOK), F32, kind="Internal").ap()
    pad_scratch = nc.dram_tensor("pad_scratch", (2, 2, DC, WIN), F32, kind="Internal").ap()
    max_scratch = nc.dram_tensor("max_scratch", (2, HEADS, TOK), F32, kind="Internal").ap()
    t2_dram = nc.dram_tensor("t2_dram", (NT, P, D), F32, kind="Internal").ap()
    xn_dram = nc.dram_tensor("xn_dram", (NT, P, D), F32, kind="Internal").ap()
    xs_dram = nc.dram_tensor("sorted_dram", (NTILE * P, D), F32, kind="Internal").ap()
    ys_dram = nc.dram_tensor("expert_out_dram", (NTILE * P, D), F32, kind="Internal").ap()
    with ExitStack() as keep:
        logits = keep.enter_context(nc.sbuf_tensor("logits", [P, NT, NE], F32))
        ident = keep.enter_context(nc.sbuf_tensor("ident", [P, P], F32))
        ps = [keep.enter_context(nc.psum_tensor(f"ps{u}", [P, 4, 512], F32)) for u in range(2)]

        def sem(name):
            return keep.enter_context(nc.semaphore(name))

        attention_phase(nc, a, scratch, pad_scratch, max_scratch, t2_dram, xn_dram, xs_dram, logits, ident, ps, sem)
        expert_phase(nc, a, t2_dram, xn_dram, xs_dram, ys_dram, logits, ident, ps, sem, out)


def attention_phase(nc, a, scratch, pad_scratch, max_scratch, t2_dram, xn_dram, xs_dram, logits, ident, ps, sem):
    with ExitStack() as ctx:
        def sb(name, shape, dt=F32):
            return ctx.enter_context(nc.sbuf_tensor(name, shape, dt))

        def two(name, shape, dt=F32):
            return [sb(f"{name}{u}", shape, dt) for u in range(2)]

        def sems(name, n):
            return [sem(f"{name}{i}") for i in range(n)]

        w_qkv_a = sb("w_qkv_a", [DC + 1, 2, 3 * D])
        w_qkv_b = sb("w_qkv_b", [DC, 2, 3 * D])
        w_out_a = sb("w_out_a", [P, GROUPS, D])
        w_out_b = sb("w_out_b", [P, GROUPS, D])
        w_fc1 = sb("w_fc1", [DC, 2, MLP])
        w_fc2 = sb("w_fc2", [P, FT, D])
        b_fc1 = sb("b_fc1", [P, FT])
        b_fc2 = sb("b_fc2", [P, 2 * D])
        norms = sb("norms", [DC, 8])
        k_bias = sb("k_bias", [DC, 2])
        w_gate = sb("w_gate", [DC + 1, 2, NE])
        rel_w = sb("rel_w", [P, 2 * WS, P], F32R)
        part_rows = sb("part_rows", [P, 2])
        mask_q = sb("mask_q", [P, 2, P], BF16)
        mask_k = sb("mask_k", [P, 2, P], BF16)
        ident16 = sb("ident16", [P, P], BF16)
        half_neg = sb("half_neg", [P, 2])
        eps = sb("eps", [P, 2])
        slot_rows = sb("slot_rows", [P, KEYS])
        slot_rows_q = sb("slot_rows_q", [P, TOK])
        v_bias = sb("v_bias", [P, D])

        x_in = two("x_in", [P, 2, D])
        x_n = two("x_n", [P, 2, D])
        stats = two("stats", [P, 2, 6])
        mean_var = two("mean_var", [P, 2, 2])
        var_eps = two("var_eps", [P, 2])
        rstd = two("rstd", [P, 2])
        x_t = two("x_t", [DC + 1, 2, TOK])
        x_tw = two("x_tw", [DC + 1, 2, TOK])
        s_hi = two("s_hi", [P, PAIRS, TOK], F32R)
        s_lo = two("s_lo", [P, PAIRS, TOK], F32R)
        work_all = sb("work", [P, 2, 2048])
        q_hi = two("q_hi", [P, PAIRS, TOK], F32R)
        q_lo = two("q_lo", [P, PAIRS, TOK], F32R)
        k_s = two("k_s", [P, PAIRS, KEYS], F32R)
        k_16 = two("k_16", [P, PAIRS, KEYS], BF16)
        q_16 = two("q_16", [P, PAIRS, TOK], BF16)
        v_s = two("v_s", [P, 4, HEADS, 32])
        o_t = two("o_t", [P, GROUPS, TOK])
        x_2 = two("x_2", [P, 2 * D])
        x_2b = two("x_2b", [P, 2 * D])
        x_3 = two("x_3", [P, 2 * D])
        den = two("den", [P, TOK])
        neg_max = two("neg_max", [P, 3, HEADS])
        neg_max_t = two("neg_max_t", [HEADS, TOK], F32R)

        def yx(t):
            return t.rearrange("p c (y x) -> p c y x", x=S)

        def win_order(t):
            return (t[:, :, 0:WIN].rearrange("p c (y x) -> p c y x", x=WS),
                    t[:, :, WIN:WIN + EDGE].rearrange("p c (y x) -> p c y x", x=S - WS),
                    t[:, :, WIN + EDGE:TOK].rearrange("p c (y x) -> p c y x", x=S))

        work = [work_all[:, u, :] for u in range(2)]
        rel_sum = [w[:, 0:PAIRS * TOK].rearrange("p (g n) -> p g n", g=PAIRS) for w in work]
        probs = [w.rearrange("p (r e n) -> p r e n", r=2, e=2) for w in work]
        hid = [w[:, 0:FT * TOK].rearrange("p (f n) -> p f n", f=FT) for w in work]
        c_hi = [q[0:DC, 0:4, :] for q in q_hi]
        c_lo = [q[0:DC, 0:4, :] for q in q_lo]

        w_in, pool_c, act_c, dve_c, pad_out, pad_in, zero_out = (sem(f"set_{n}") for n in (
            "weights", "pool", "act", "dve", "pad_out", "pad_in", "zeros"))
        tables = work_all[:, :, :].rearrange("p a b -> p (a b)")[:, 0:2 * WS * P].rearrange("p (t m) -> p t m", m=P)
        mask_in = o_t[0][:, :, :].rearrange("p g n -> p (g n)")[:, 0:4 * P]
        zero = o_t[1][:, :, :].rearrange("p g n -> p (g n)")
        loads = ((tables, "rel_tables"), (slot_rows[:, :], "slot_rows"), (slot_rows_q[:, :], "slot_rows_q"),
                 (mask_in, "masks"), (k_bias[:, :], "k_bias"), (v_bias[:, :], "v_bias"),
                 (part_rows[:, :], "part_rows"), (ident[:, :], "ident"), (norms[:, :], "norms"),
                 (w_qkv_a[:, :, :], "w_qkv_a"), (w_out_a[:, :, :], "w_out_a"), (w_fc1[:, :, :], "w_fc1"),
                 (w_fc2[:, :, :], "w_fc2"), (b_fc1[:, :], "b_fc1"), (b_fc2[:, :], "b_fc2"),
                 (w_qkv_b[:, :, :], "w_qkv_b"), (w_out_b[:, :, :], "w_out_b"), (w_gate[:, :, :], "w_gate"))
        ALL_IN = 16 * len(loads)

        with nc.Block("setup") as block:
            @block.sync
            def _(sp):
                for dst, name in loads:
                    sp.dma_start(dst, a[name]).then_inc(w_in, 16)
                sp.wait_ge(dve_c, 4)
                sp.dma_start(pad_scratch[0].rearrange("g r n -> r g n"),
                             q_hi[1][0:DC, 0:2, 0:WIN].bitcast(F32)).then_inc(pad_out, 16)
                sp.dma_start(pad_scratch[1].rearrange("g r n -> r g n"),
                             q_lo[1][0:DC, 0:2, 0:WIN].bitcast(F32)).then_inc(pad_out, 16)
                sp.wait_ge(pad_out, 32)
                sp.wait_ge(pool_c, 2)
                for u in range(2):
                    for e in range(2):
                        for part in range(2):
                            r = SLOT * e + HD * part
                            sp.dma_start(k_s[u][r:r + HD, :, TOK:KEYS].bitcast(F32),
                                         pad_scratch[part].rearrange("g (p e c) n -> e c (g p) n", e=2, c=HD)[e]
                                         ).then_inc(pad_in, 16)
                rows = xs_dram.rearrange("(p r) d -> p (r d)", p=P)
                width = GROUPS * TOK
                for at in range(0, NTILE * D, width):
                    sp.dma_start(rows[:, at:at + width], zero).then_inc(zero_out, 16)
                sp.wait_ge(zero_out, 16 * (NTILE * D // width))
                sp.wait_ge(w_in, ALL_IN)
                sp.wait_ge(pad_in, 16 * 8)

            @block.gpsimd
            def _(gp):
                for u in range(2):
                    gp.memset(k_s[u][:, :, :].bitcast(F32), 0.0).then_inc(pool_c, 1)
                for u in range(2):
                    gp.memset(s_hi[u][:, :, :].bitcast(F32), 0.0).then_inc(pool_c, 1)
                    gp.memset(s_lo[u][:, :, :].bitcast(F32), 0.0).then_inc(pool_c, 1)
                for u in range(2):
                    gp.memset(v_s[u][:, :, :, :], 1.0)
                    gp.memset(x_t[u][:, :, :], 1.0).then_inc(pool_c, 1)
                gp.memset(eps[:, :], EPS)
                gp.memset(half_neg[:, :], -0.5).then_inc(pool_c, 1)

            @block.scalar
            def _(ac):
                ac.wait_ge(w_in, ALL_IN)
                ac.wait_ge(pool_c, 6)
                for u in range(2):
                    for r in (REL, SLOT + REL):
                        for p in range(PAIRS):
                            ac.copy(k_s[u][r:r + 32, p, :], slot_rows[r:r + 32, :]).then_inc(act_c, 1)
                            ac.copy(s_hi[u][r:r + 32, p, :], slot_rows_q[r:r + 32, :])
                ac.wait_ge(pool_c, 8)
                for u in range(2):
                    for t in (2, 3):
                        ac.copy(v_s[u][:, t, :, 0:HD], v_bias[:, :].rearrange("p (h d) -> p h d", h=HEADS))
                ac.wait_ge(act_c, 4 * PAIRS)
                ac.wait_ge(pad_in, 16 * 8)
                for u in range(2):
                    ac.copy(k_16[u][:, :, :], k_s[u][:, :, :].bitcast(F32))

            @block.vector
            def _(dv):
                count = [0]

                def step(ins):
                    count[0] += 1
                    ins.then_inc(dve_c, 1)
                    dv.wait_ge(dve_c, count[0])

                step(dv.memset(zero, 0.0))
                dv.wait_ge(w_in, ALL_IN)
                for c in range(2):
                    ins = dv.tensor_scalar(x_tw[1][0:DC, c, 0:WIN], zero[0:DC, 0:WIN], k_bias[:, c:c + 1], SCALE_A,
                                           ALU.add, ALU.mult)
                step(ins)
                step(dv.tensor_copy(q_hi[1][0:DC, 0:2, 0:WIN], x_tw[1][0:DC, :, 0:WIN]))
                step(dv.tensor_tensor(q_lo[1][0:DC, 0:2, 0:WIN], x_tw[1][0:DC, :, 0:WIN],
                                      q_hi[1][0:DC, 0:2, 0:WIN].bitcast(F32), ALU.subtract))
                step(dv.tensor_copy(rel_w[:, :, :], tables))
                step(dv.tensor_tensor(tables, tables, rel_w[:, :, :].bitcast(F32), ALU.subtract))
                step(dv.tensor_scalar(tables, tables, part_rows[:, 1:2], None, ALU.mult))
                step(dv.scalar_tensor_tensor(out=rel_w[:, :, :], in0=rel_w[:, :, :].bitcast(F32),
                                             scalar=part_rows[:, 0:1], in1=tables, op0=ALU.mult, op1=ALU.add))
                step(dv.tensor_copy(ident16[:, :], ident[:, :]))
                masks = mask_in.rearrange("p (m a k) -> p m a k", m=2, a=2)
                step(dv.tensor_copy(mask_q[:, :, :], masks[:, 0]))
                step(dv.tensor_copy(mask_k[:, :, :], masks[:, 1]))

        x_loaded = sems("x_loaded", 2)
        q_out, k_out, q_slots, k_slots, max_out, max_row = (sems(n, 2) for n in (
            "q_out", "k_out", "q_slots", "k_slots", "max_out", "max_row"))
        t2_out, xn_out = sems("t2_out", 2), sems("xn_out", 2)
        st, ag, ve, rs, xn, xt_ps, xt = (sem(n) for n in (
            "ln_stats", "ln_mean", "ln_var", "ln_rstd", "ln_out", "xt_ps", "xt_sb"))
        xtw = sem("xtw")
        q_ps, k_ps, v_ps, q_h, k_h, q_l, k_l, v_sb, mt_ps, mt_sb, o_ps, res = (sem(n) for n in (
            "q_ps", "k_ps", "v_ps", "q_h", "k_h", "q_l", "k_l", "v_sb", "mt_ps", "mt_sb", "o_ps", "res"))
        m_ps, m_sb, sc_ps, pr_sb = (sems(n, PAIRS) for n in ("m_ps", "m_sb", "sc_ps", "pr_sb"))
        av_ps, dn_sb, rc_sb, ot_sb = (sems(n, GROUPS) for n in ("av_ps", "dn_sb", "rc_sb", "ot_sb"))
        ry_ps, ry_sb, rx_ps = (sems(n, 2) for n in ("ry_ps", "ry_sb", "rx_ps"))
        rel_done, qh_done, ql_done, q16_done, k16_done, q16b_done, k16b_done, ones_b = (sem(n) for n in (
            "rel_done", "qh_done", "ql_done", "q16_done", "k16_done", "q16b_done", "k16b_done", "ones_b"))
        f1_ps, hid_sb, f2_ps, x2b_done, mlp_done, lg_ps, lg_sb = (sem(n) for n in (
            "f1_ps", "hid_sb", "f2_ps", "x2b_done", "mlp_done", "lg_ps", "lg_sb"))

        went_on = sem("went_on")

        def hold(eng):
            eng.sem_inc(went_on, 1)

        block = ctx.enter_context(nc.Block("attention"))

        def numbers(eng, it):
            return [eng.snap(it * 2 + 1), eng.snap(it * 2 + 2)]

        def reached(eng, it, stages="ab"):
            return {k: [eng.snap(it * (2 * len(stages)) + 2 * at + 1 + u) for u in range(2)]
                    for at, k in enumerate(stages)}

        def transfers(eng, it, count):
            return {k: eng.snap(it * (2 * count) + (at + 1) * count) for at, k in enumerate("ab")}

        def slots(t, part, chunk):
            return t[part, chunk:chunk + 2].rearrange("g (p e c) n -> e c (g p) n", e=2, c=HD)

        @block.sync
        def _(sp):
            for u in range(2):
                sp.dma_start(x_in[u][:, :, :], a["x"][u]).then_inc(x_loaded[u], 16)
                sp.sem_inc(t2_out[u], 16)
                sp.sem_inc(xn_out[u], 16)
            with sp.Fori(0, B // 2) as it:
                n = numbers(sp, it)
                ab, ambg = reached(sp, it), reached(sp, it, "ambg")
                c16, c32 = transfers(sp, it, 16), transfers(sp, it, 32)
                nxt = [sp.snap((it * 2 + 2 + u) % B) for u in range(2)]
                row = [sp.snap(it * 4 + 2 * u) for u in range(2)]

                def to_dram(k):
                    for u in range(2):
                        for ready, src, part, chunk, out in (
                                (q_h, c_hi, 0, 0, q_out), (q_l, c_lo, 1, 0, q_out),
                                (k_h, c_hi, 0, 2, k_out), (k_l, c_lo, 1, 2, k_out)):
                            sp.wait_ge(ready, ab[k][u])
                            sp.dma_start(scratch[u, part, chunk:chunk + 2].rearrange("g r n -> r g n"),
                                         src[u][:, chunk:chunk + 2, :].bitcast(F32)).then_inc(out[u], 16)

                def to_slots(k, keys):
                    for u in range(2):
                        sp.wait_ge(q_out[u], c32[k])
                        for e in range(2):
                            for part, dst in ((0, s_hi[u]), (1, s_lo[u])):
                                for twice in range(2):
                                    r = SLOT * e + HD * twice
                                    sp.dma_start(dst[r:r + HD, :, :].bitcast(F32),
                                                 slots(scratch[u], part, 0)[e]).then_inc(q_slots[u], 16)
                        sp.wait_ge(k_out[u], c32[k])
                        for e in range(2):
                            for part in range(2):
                                r = SLOT * e + HD * part
                                sp.dma_start(keys[u][r:r + HD, :, 0:TOK].bitcast(F32),
                                             slots(scratch[u], part, 2)[e]).then_inc(k_slots[u], 16)

                def max_rows(k, dst, at):
                    for u in range(2):
                        if k == "a":
                            sp.wait_ge(ql_done, n[u])
                        sp.wait_ge(mt_sb, ab[k][u])
                        sp.dma_start(max_scratch[u], neg_max_t[u][:, :].bitcast(F32)).then_inc(max_out[u], 16)
                    for u in range(2):
                        sp.wait_ge(max_out[u], c16[k])
                        for e in range(2):
                            r = SLOT * e + at
                            sp.dma_start(dst[u][r:r + 1, :, :].bitcast(F32),
                                         max_scratch[u:u + 1, e:HEADS:2, :]).then_inc(max_row[u], 16)

                to_dram("a")
                to_slots("a", k_s)
                max_rows("a", q_hi, MAXROW)
                for u in range(2):
                    sp.wait_ge(res, ab["a"][u])
                    sp.dma_start(x_in[u][:, :, :], a["x"][nxt[u]]).then_inc(x_loaded[u], 16)
                to_dram("b")
                to_slots("b", q_lo)
                max_rows("b", s_hi, MAXROW_B)
                for u in range(2):
                    sp.wait_ge(res, ab["b"][u])
                    sp.dma_start(t2_dram[bass.ds(row[u], 2)].rearrange("t p d -> p t d"),
                                 x_2[u][:, :].rearrange("p (t d) -> p t d", t=2)).then_inc(t2_out[u], 16)
                for u in range(2):
                    sp.wait_ge(xn, ambg["g"][u])
                    sp.dma_start(xn_dram[bass.ds(row[u], 2)].rearrange("t p d -> p t d"),
                                 x_n[u][:, :, :]).then_inc(xn_out[u], 16)
            for u in range(2):
                sp.wait_ge(t2_out[u], 16 * (B // 2 + 1))
                sp.wait_ge(xn_out[u], 16 * (B // 2 + 1))
                sp.wait_ge(x_loaded[u], 16 * (B // 2 + 1))

        @block.gpsimd
        def _(gp):
            with gp.Fori(0, B // 2) as it:
                n = numbers(gp, it)
                ab, ambg = reached(gp, it), reached(gp, it, "ambg")
                c64 = transfers(gp, it, 64)

                def rstds(k):
                    for u in range(2):
                        gp.wait_ge(ag, ambg[k][u])
                        gp.tensor_tensor(var_eps[u][:, :], mean_var[u][:, :, 1], eps[:, :],
                                         ALU.add).then_inc(ve, 1)
                        gp.wait_ge(ve, ambg[k][u])
                        gp.tensor_tensor(rstd[u][:, :], var_eps[u][:, :], half_neg[:, :],
                                         ALU.pow).then_inc(rs, 1)

                rstds("a")
                for u in range(2):
                    gp.wait_ge(xt, ambg["a"][u])
                    hold(gp)
                    for c in range(2):
                        for dst, src in zip(win_order(x_tw[u][:, c:c + 1, :]),
                                            window_pieces(yx(x_t[u][:, c:c + 1, :]))):
                            ins = gp.tensor_copy(dst[:, 0], src[:, 0])
                    ins.then_inc(xtw, 1)
                for u in range(2):
                    gp.wait_ge(qh_done, n[u])
                    for dst, src, hi in zip(win_order(q_lo[u][:, :, :]), window_pieces(yx(rel_sum[u])),
                                            win_order(q_hi[u][:, :, :].bitcast(F32))):
                        ins = gp.tensor_tensor(dst, src, hi, ALU.subtract)
                    ins.then_inc(ql_done, 1)
                for u in range(2):
                    gp.wait_ge(res, ab["a"][u])
                    gp.tensor_tensor(x_2b[u][:, :], x_2[u][:, :], b_fc2[:, :], ALU.add).then_inc(x2b_done, 1)
                rstds("m")
                rstds("b")
                for u in range(2):
                    gp.wait_ge(k_slots[u], c64["b"])
                    hold(gp)
                    for e in range(2):
                        r = SLOT * e + MAXROW_B
                        ins = gp.memset(q_lo[u][r:r + 1, :, :].bitcast(F32), 1.0)
                    ins.then_inc(ones_b, 1)
                rstds("g")

        @block.scalar
        def _(ac):
            with ac.Fori(0, B // 2) as it:
                n, ab, ambg = numbers(ac, it), reached(ac, it), reached(ac, it, "ambg")
                c64, c128 = transfers(ac, it, 64), transfers(ac, it, 128)

                def channels(k, scale, shift):
                    for u in range(2):
                        ac.wait_ge(xt_ps, ambg[k][u])
                        for c in range(2):
                            src = ps[u][0:DC, 0, c * TOK:(c + 1) * TOK]
                            if scale is None:
                                ins = ac.copy(x_t[u][0:DC, c, :], src)
                            else:
                                ins = ac.activation(x_t[u][0:DC, c, :], src, ACT.Identity,
                                                    bias=norms[:, shift + c:shift + c + 1],
                                                    scale=norms[:, scale + c:scale + c + 1])
                        ins.then_inc(xt, 1)

                def high_parts(k, scale):
                    for u in range(2):
                        ac.wait_ge(q_ps, ab[k][u])
                        ac.activation(c_hi[u][:, 0:2, :].rearrange("p g n -> p (g n)"), ps[u][0:DC, 1, :],
                                      ACT.Copy).then_inc(q_h, 1)
                    for u in range(2):
                        ac.wait_ge(k_ps, ab[k][u])
                        ac.activation(c_hi[u][:, 2:4, :].rearrange("p g n -> p (g n)"), ps[u][0:DC, 2, :],
                                      ACT.Copy, scale=scale).then_inc(k_h, 1)

                channels("a", 0, 2)
                high_parts("a", SCALE_A)
                for u in range(2):
                    ac.wait_ge(v_ps, ab["a"][u])
                    ac.copy(v_s[u][0:HALF, 0:2, :, 0:HD],
                            ps[u][0:HALF, 3, 0:2 * D].rearrange("p (t h d) -> p t h d", t=2, h=HEADS))
                    ac.copy(v_s[u][0:OUT, 2, :, 0:HD],
                            ps[u][0:OUT, 0, 0:D].rearrange("p (h d) -> p h d", h=HEADS)).then_inc(v_sb, 1)
                for half in range(2):
                    for u in range(2):
                        ac.wait_ge(ry_ps[half], n[u])
                        for b in range(2):
                            y = 8 * half + 4 * b
                            ins = ac.copy(
                                yx(rel_sum[u])[:, :, y:y + 4, :].rearrange("p g y x -> p y g x"),
                                ps[u][:, 2 * half + b, 0:384].rearrange("p (y g x) -> p y g x", y=4, g=PAIRS))
                        ins.then_inc(ry_sb[half], 1)
                for u in range(2):
                    ac.wait_ge(k_slots[u], c64["a"])
                    ac.copy(k_16[u][:, :, 0:TOK], k_s[u][:, :, 0:TOK].bitcast(F32)).then_inc(k16_done, 1)
                for u in range(2):
                    ac.wait_ge(rel_done, n[u])
                    for dst, src in zip(win_order(q_16[u][:, :, :]), window_pieces(yx(rel_sum[u]))):
                        ins = ac.copy(dst, src)
                    ins.then_inc(q16_done, 1)
                for u in range(2):
                    ac.wait_ge(mt_ps, ab["a"][u])
                    ac.copy(neg_max_t[u][:, :], ps[u][0:HEADS, 0, 0:TOK]).then_inc(mt_sb, 1)
                for p in range(PAIRS):
                    for u in range(2):
                        if p == 0:
                            ac.wait_ge(ql_done, n[u])
                        ac.wait_ge(sc_ps[p], ab["a"][u])
                        ac.activation(probs[u][0:HALF, p % 2, :, 0:2 * WIN], ps[u][0:HALF, 0:2, 0:2 * WIN],
                                      ACT.Exp)
                        ac.activation(probs[u][:, p % 2, :, 2 * WIN:512], ps[u][:, 0:2, 2 * WIN:512],
                                      ACT.Exp).then_inc(pr_sb[p], 1)
                channels("m", 4, 6)
                for u in range(2):
                    ac.wait_ge(f1_ps, n[u])
                    for f in range(FT):
                        ins = ac.activation(hid[u][:, f, :],
                                            ps[u][:, 1 + f // 2, (f % 2) * TOK:(f % 2 + 1) * TOK],
                                            ACT.Gelu, bias=b_fc1[:, f:f + 1])
                    ins.then_inc(hid_sb, 1)
                channels("b", None, None)
                high_parts("b", SCALE_B)
                for u in range(2):
                    ac.wait_ge(v_ps, ab["b"][u])
                    ac.copy(v_s[u][:, 0:2, :, 0:HD],
                            ps[u][:, 3, 0:2 * D].rearrange("p (t h d) -> p t h d", t=2, h=HEADS)
                            ).then_inc(v_sb, 1)
                for u in range(2):
                    ac.wait_ge(q_slots[u], c128["b"])
                    for r in (0, SLOT):
                        ins = ac.copy(q_16[u][r:r + 32, :, :], s_hi[u][r:r + 32, :, :].bitcast(F32))
                    ins.then_inc(q16b_done, 1)
                    ac.wait_ge(k_slots[u], c64["b"])
                    for r in (0, SLOT):
                        ins = ac.copy(k_16[u][r:r + 32, :, 0:TOK], q_lo[u][r:r + 32, :, :].bitcast(F32))
                    ins.then_inc(k16b_done, 1)
                for u in range(2):
                    ac.wait_ge(mt_ps, ab["b"][u])
                    ac.copy(neg_max_t[u][:, :], ps[u][0:HEADS, 0, 0:TOK]).then_inc(mt_sb, 1)
                for p in range(PAIRS):
                    for u in range(2):
                        ac.wait_ge(sc_ps[p], ab["b"][u])
                        ac.activation(probs[u][:, p % 2, :, 0:384], ps[u][:, 0:2, 0:384],
                                      ACT.Exp).then_inc(pr_sb[p], 1)
                channels("g", None, None)

        @block.vector
        def _(dv):
            with dv.Fori(0, B // 2) as it:
                n, ab, ambg = numbers(dv, it), reached(dv, it), reached(dv, it, "ambg")
                c16, c64 = dv.snap(it * 16 + 16), transfers(dv, it, 64)
                tile = [dv.snap(it * 4 + 2 * u) for u in range(2)]

                def norm(k, src, ready, count):
                    for u in range(2):
                        dv.wait_ge(ready[u], count[u])
                        for t in range(2):
                            ins = dv.bn_stats(stats[u][:, t, :], src[u][:, t * D:(t + 1) * D])
                        ins.then_inc(st, 1)
                    for u in range(2):
                        dv.wait_ge(st, ambg[k][u])
                        hold(dv)
                        for t in range(2):
                            ins = dv.bn_aggr(mean_var[u][:, t, :], stats[u][:, t, :])
                        ins.then_inc(ag, 1)
                    for u in range(2):
                        dv.wait_ge(rs, ambg[k][u])
                        if k == "a":
                            dv.wait_ge(xn_out[u], c16)
                        for t in range(2):
                            ins = dv.tensor_scalar(x_n[u][:, t, :], src[u][:, t * D:(t + 1) * D],
                                                   mean_var[u][:, t, 0:1], rstd[u][:, t:t + 1],
                                                   ALU.subtract, ALU.mult)
                        ins.then_inc(xn, 1)

                def low_parts(k, scale):
                    for u in range(2):
                        dv.wait_ge(q_h, ab[k][u])
                        dv.tensor_tensor(c_lo[u][:, 0:2, :].rearrange("p g n -> p (g n)"), ps[u][0:DC, 1, :],
                                         c_hi[u][:, 0:2, :].rearrange("p g n -> p (g n)").bitcast(F32),
                                         ALU.subtract).then_inc(q_l, 1)
                    for u in range(2):
                        dv.wait_ge(k_h, ab[k][u])
                        dv.scalar_tensor_tensor(out=c_lo[u][:, 2:4, :].rearrange("p g n -> p (g n)"),
                                                in0=ps[u][0:DC, 2, :], scalar=scale,
                                                in1=c_hi[u][:, 2:4, :].rearrange("p g n -> p (g n)").bitcast(F32),
                                                op0=ALU.mult, op1=ALU.subtract).then_inc(k_l, 1)

                def normalise(k):
                    for g in range(GROUPS):
                        bank = 2 + g % 2
                        for u in range(2):
                            dv.wait_ge(av_ps[g], ab[k][u])
                            if g:
                                dv.wait_ge(ot_sb[g - 1], ab[k][u])
                            hold(dv)
                            dv.stream_shuffle(den[u][:, :], ps[u][:, bank, 0:TOK], [HD] * 32).then_inc(dn_sb[g], 1)
                        for u in range(2):
                            dv.wait_ge(dn_sb[g], ab[k][u])
                            dv.reciprocal(den[u][:, :], den[u][:, :]).then_inc(rc_sb[g], 1)
                        for u in range(2):
                            dv.wait_ge(rc_sb[g], ab[k][u])
                            if k == "a":
                                for dst, src, d in zip(window_pieces(yx(o_t[u][:, g:g + 1, :])),
                                                       win_order(ps[u][:, bank:bank + 1, 0:TOK]),
                                                       win_order(den[u][:, :].unsqueeze(1))):
                                    ins = dv.tensor_tensor(dst[:, 0], src[:, 0], d[:, 0], ALU.mult)
                            else:
                                ins = dv.tensor_tensor(o_t[u][:, g, :], ps[u][:, bank, 0:TOK], den[u][:, :],
                                                       ALU.mult)
                            ins.then_inc(ot_sb[g], 1)

                norm("a", [x[:, :, :].rearrange("p t d -> p (t d)") for x in x_in], x_loaded, [c16, c16])
                low_parts("a", SCALE_A)
                for half in range(2):
                    for u in range(2):
                        dv.wait_ge(ry_sb[0], n[u])
                        dv.wait_ge(ry_sb[1], n[u])
                        dv.wait_ge(rx_ps[half], n[u])
                        for b in range(2):
                            x = 8 * half + 4 * b
                            part = yx(rel_sum[u])[:, :, :, x:x + 4].rearrange("p g y x -> p x g y")
                            ins = dv.tensor_tensor(
                                part, ps[u][:, 2 * half + b, 0:384].rearrange("p (x g y) -> p x g y", x=4, g=PAIRS),
                                part, ALU.add)
                        if half:
                            ins.then_inc(rel_done, 1)
                for u in range(2):
                    dv.wait_ge(rel_done, n[u])
                    dv.wait_ge(k_slots[u], c64["a"])
                    for dst, src in zip(win_order(q_hi[u][:, :, :]), window_pieces(yx(rel_sum[u]))):
                        ins = dv.tensor_copy(dst, src)
                    ins.then_inc(qh_done, 1)
                for p in range(PAIRS):
                    for u in range(2):
                        dv.wait_ge(m_ps[p], ab["a"][u])
                        dv.tensor_reduce(neg_max[u][0:HALF, 0:2, 2 * p:2 * p + 2].rearrange("p q e -> p e q"),
                                         ps[u][0:HALF, 0:2, 0:2 * WIN].rearrange("p e (q k) -> p e q k", q=2),
                                         AX.X, ALU.max, negate=True)
                        dv.tensor_reduce(neg_max[u][0:OUT, 2, 2 * p:2 * p + 2], ps[u][0:OUT, 2:4, 0:TOK],
                                         AX.X, ALU.max, negate=True).then_inc(m_sb[p], 1)
                normalise("a")
                for u in range(2):
                    dv.wait_ge(o_ps, ab["a"][u])
                    dv.wait_ge(t2_out[u], c16)
                    dv.tensor_tensor(x_2[u][:, :], ps[u][:, 0, 0:2 * D],
                                     x_in[u][:, :, :].rearrange("p t d -> p (t d)"), ALU.add).then_inc(res, 1)
                norm("m", x_2, [res] * 2, ab["a"])
                for u in range(2):
                    dv.wait_ge(f2_ps, n[u])
                    dv.wait_ge(x2b_done, n[u])
                    dv.tensor_tensor(x_3[u][:, :], ps[u][:, 0, 0:2 * D], x_2b[u][:, :], ALU.add).then_inc(mlp_done, 1)
                norm("b", x_3, [mlp_done] * 2, n)
                low_parts("b", SCALE_B)
                for p in range(PAIRS):
                    bank = 2 * (p % 2)
                    for u in range(2):
                        dv.wait_ge(m_ps[p], ab["b"][u])
                        dv.tensor_reduce(neg_max[u][:, 0, 2 * p:2 * p + 2], ps[u][:, bank:bank + 2, 0:P],
                                         AX.X, ALU.max, negate=True)
                        dv.tensor_reduce(neg_max[u][:, 1, 2 * p:2 * p + 2], ps[u][:, bank:bank + 2, P:3 * P],
                                         AX.X, ALU.max, negate=True).then_inc(m_sb[p], 1)
                normalise("b")
                for u in range(2):
                    dv.wait_ge(o_ps, ab["b"][u])
                    dv.tensor_tensor(x_2[u][:, :], ps[u][:, 0, 0:2 * D], x_3[u][:, :], ALU.add).then_inc(res, 1)
                norm("g", x_2, [res] * 2, ab["b"])
                for u in range(2):
                    dv.wait_ge(lg_ps, n[u])
                    dv.tensor_copy(logits[:, bass.ds(tile[u], 2), :],
                                   ps[u][:, 1, 0:2 * NE].rearrange("p (t e) -> p t e", t=2)).then_inc(lg_sb, 1)

        @block.tensor
        def _(pe):
            with pe.Fori(0, B // 2) as it:
                n, ab, ambg = numbers(pe, it), reached(pe, it), reached(pe, it, "ambg")
                c32, c128 = transfers(pe, it, 32), transfers(pe, it, 128)

                def transpose_norm(k):
                    for u in range(2):
                        pe.wait_ge(xn, ambg[k][u])
                        for t in range(2):
                            for c in range(2):
                                ins = pe.transpose(ps[u][0:DC, 0, c * TOK + t * P:c * TOK + (t + 1) * P],
                                                   x_n[u][:, t, c * DC:(c + 1) * DC], ident[:, :])
                        ins.then_inc(xt_ps, 1)

                def chunks(dst, w, cols, x, toks, ones):
                    pe.matmul(dst, w[0:DC + ones, 0, cols], x[0:DC + ones, 0, toks], start=True, stop=False)
                    return pe.matmul(dst, w[0:DC, 1, cols], x[0:DC, 1, toks], start=False, stop=True)

                def tokens(dst, x, toks, w, cols, ones):
                    pe.matmul(dst, x[0:DC + ones, 0, toks], w[0:DC + ones, 0, cols], start=True, stop=False)
                    return pe.matmul(dst, x[0:DC, 1, toks], w[0:DC, 1, cols], start=False, stop=True)

                def output(k, w):
                    for u in range(2):
                        for g in range(GROUPS):
                            pe.wait_ge(ot_sb[g], ab[k][u])
                        for t in range(2):
                            for g in range(GROUPS):
                                ins = pe.matmul(ps[u][:, 0, t * D:(t + 1) * D], o_t[u][:, g, t * P:(t + 1) * P],
                                                w[:, g, :], start=(g == 0), stop=(g == GROUPS - 1))
                        ins.then_inc(o_ps, 1)

                transpose_norm("a")
                for u in range(2):
                    pe.wait_ge(xt, ambg["a"][u])
                    for g in range(2):
                        ins = chunks(ps[u][0:DC, 1, g * TOK:(g + 1) * TOK], w_qkv_a, slice(g * DC, (g + 1) * DC),
                                     x_t[u], slice(0, TOK), 1)
                    ins.then_inc(q_ps, 1)
                for u in range(2):
                    pe.wait_ge(xtw, n[u])
                    for g in range(2):
                        ins = chunks(ps[u][0:DC, 2, g * TOK:(g + 1) * TOK], w_qkv_a,
                                     slice(D + g * DC, D + (g + 1) * DC), x_tw[u], slice(0, TOK), 1)
                    ins.then_inc(k_ps, 1)
                for u in range(2):
                    for t in range(2):
                        tokens(ps[u][0:HALF, 3, t * D:(t + 1) * D], x_tw[u], slice(t * HALF, (t + 1) * HALF),
                               w_qkv_a, slice(2 * D, 3 * D), 1)
                    tokens(ps[u][0:OUT, 0, 0:D], x_tw[u], slice(WIN, TOK), w_qkv_a,
                           slice(2 * D, 3 * D), 1).then_inc(v_ps, 1)

                def rel(u, bank, at, table, toks):
                    dst = ps[u][:, bank, at * 96:(at + 1) * 96].rearrange("p (g x) -> p g x", g=PAIRS)
                    pe.matmul(dst, rel_w[:, table, :], toks(s_hi[u]), start=True, stop=False)
                    return pe.matmul(dst, rel_w[:, table, :], toks(s_lo[u]), start=False, stop=True)

                for half in range(2):
                    for u in range(2):
                        pe.wait_ge(q_slots[u], c128["a"])
                        pe.wait_ge(v_sb, ab["a"][u])
                        pe.wait_ge(k_l, ab["a"][u])
                        for y in range(8 * half, 8 * half + 8):
                            ins = rel(u, y // 4, y % 4, y % WS, lambda s: s[:, :, y * S:(y + 1) * S])
                        ins.then_inc(ry_ps[half], 1)
                for half in range(2):
                    for u in range(2):
                        pe.wait_ge(ry_sb[half], n[u])
                        for x in range(8 * half, 8 * half + 8):
                            ins = rel(u, x // 4, x % 4, WS + x % WS, lambda s: s[:, :, x:TOK:S])
                        ins.then_inc(rx_ps[half], 1)
                for p in range(PAIRS):
                    for u in range(2):
                        if p == 0:
                            pe.wait_ge(q16_done, n[u])
                            pe.wait_ge(k16_done, n[u])
                        else:
                            pe.wait_ge(m_sb[p - 1], ab["a"][u])
                        for e in range(2):
                            slot = slice(SLOT * e, SLOT * (e + 1))
                            for q in range(2):
                                pe.matmul(ps[u][0:HALF, e, q * WIN:(q + 1) * WIN],
                                          q_16[u][slot, p, q * HALF:(q + 1) * HALF], k_16[u][slot, p, 0:WIN],
                                          start=True, stop=True)
                            ins = pe.matmul(ps[u][0:OUT, 2 + e, 0:TOK], q_16[u][slot, p, WIN:TOK],
                                            k_16[u][slot, p, WIN:KEYS], start=True, stop=True)
                        ins.then_inc(m_ps[p], 1)
                for u in range(2):
                    pe.wait_ge(m_sb[PAIRS - 1], ab["a"][u])
                    for t, (rows, at) in enumerate(((HALF, 0), (HALF, HALF), (OUT, WIN))):
                        ins = pe.transpose(ps[u][0:HEADS, 0, at:at + rows], neg_max[u][0:rows, t, :],
                                           ident[0:rows, 0:rows])
                    ins.then_inc(mt_ps, 1)

                def scores_a(p, u):
                    for e in range(2):
                        slot = slice(SLOT * e, SLOT * (e + 1))
                        for k in range(2):
                            for q, start in ((q_hi[u], True), (q_lo[u], False)):
                                pe.matmul(ps[u][0:HALF, e, k * WIN:(k + 1) * WIN],
                                          k_s[u][slot, p, k * HALF:(k + 1) * HALF], q[slot, p, 0:WIN],
                                          start=start, stop=not start)
                        for k in range(2):
                            for q, start in ((q_hi[u], True), (q_lo[u], False)):
                                ins = pe.matmul(ps[u][:, e, 2 * WIN + k * OUT:2 * WIN + (k + 1) * OUT],
                                                k_s[u][slot, p, WIN + k * P:WIN + (k + 1) * P], q[slot, p, WIN:TOK],
                                                start=start, stop=not start)
                    ins.then_inc(sc_ps[p], 1)

                def values_a(p, u):
                    pe.wait_ge(pr_sb[p], ab["a"][u])
                    g = p // 2
                    for e in range(2):
                        h = 2 * p + e
                        rows = slice(32 * (h % 4), 32 * (h % 4) + 32)
                        for k in range(2):
                            pe.matmul(ps[u][rows, 2 + g % 2, 0:WIN], v_s[u][0:HALF, k, h, :],
                                      probs[u][0:HALF, p % 2, e, k * WIN:(k + 1) * WIN],
                                      start=(k == 0), stop=(k == 1))
                        for k in range(2):
                            ins = pe.matmul(ps[u][rows, 2 + g % 2, WIN:TOK], v_s[u][:, 2 + k, h, :],
                                            probs[u][:, p % 2, e, 2 * WIN + k * OUT:2 * WIN + (k + 1) * OUT],
                                            start=(k == 0), stop=(k == 1))
                    if p % 2:
                        ins.then_inc(av_ps[g], 1)

                def attend(k, scores, values):
                    for p in range(PAIRS + 1):
                        for u in range(2):
                            if p < PAIRS:
                                if p:
                                    pe.wait_ge(pr_sb[p - 1], ab[k][u])
                                scores(p, u)
                        for u in range(2):
                            if p:
                                if p == 5:
                                    pe.wait_ge(ot_sb[0], ab[k][u])
                                values(p - 1, u)

                for u in range(2):
                    pe.wait_ge(max_row[u], c32["a"])
                pe.wait_ge(ql_done, n[1])
                attend("a", scores_a, values_a)
                output("a", w_out_a)

                transpose_norm("m")
                for u in range(2):
                    pe.wait_ge(xt, ambg["m"][u])
                    for f in range(FT):
                        ins = chunks(ps[u][:, 1 + f // 2, (f % 2) * TOK:(f % 2 + 1) * TOK], w_fc1,
                                     slice(f * P, (f + 1) * P), x_t[u], slice(0, TOK), 0)
                    ins.then_inc(f1_ps, 1)
                for u in range(2):
                    pe.wait_ge(hid_sb, n[u])
                    for t in range(2):
                        for f in range(FT):
                            ins = pe.matmul(ps[u][:, 0, t * D:(t + 1) * D], hid[u][:, f, t * P:(t + 1) * P],
                                            w_fc2[:, f, :], start=(f == 0), stop=(f == FT - 1))
                    ins.then_inc(f2_ps, 1)

                transpose_norm("b")
                for u in range(2):
                    pe.wait_ge(xt, ambg["b"][u])
                    for part, done in ((0, q_ps), (1, k_ps)):
                        for g in range(2):
                            at = part * D + g * DC
                            ins = chunks(ps[u][0:DC, 1 + part, g * TOK:(g + 1) * TOK], w_qkv_b,
                                         slice(at, at + DC), x_t[u], slice(0, TOK), 0)
                        ins.then_inc(done, 1)
                    for t in range(2):
                        ins = tokens(ps[u][:, 3, t * D:(t + 1) * D], x_t[u], slice(t * P, (t + 1) * P),
                                     w_qkv_b, slice(2 * D, 3 * D), 0)
                    ins.then_inc(v_ps, 1)

                def masked(u, bank, mask):
                    pe.matmul(ps[u][:, bank, 0:512].rearrange("p (a k) -> p a k", a=2)[:, :, 0:P], ident16[:, :],
                              mask[:, :, :], start=True, stop=False, skip_group_check=True)

                for p in range(PAIRS):
                    for u in range(2):
                        if p == 0:
                            pe.wait_ge(q16b_done, n[u])
                            pe.wait_ge(k16b_done, n[u])
                            pe.wait_ge(v_sb, ab["b"][u])
                            pe.wait_ge(k_l, ab["b"][u])
                        if p >= 2:
                            pe.wait_ge(m_sb[p - 2], ab["b"][u])
                        for e in range(2):
                            bank = 2 * (p % 2) + e
                            rows = slice(SLOT * e, SLOT * e + 32)
                            masked(u, bank, mask_q)
                            pe.matmul(ps[u][:, bank, 0:P], q_16[u][rows, p, 0:P], k_16[u][rows, p, 0:P],
                                      start=False, stop=True, skip_group_check=True)
                            ins = pe.matmul(ps[u][:, bank, P:3 * P], q_16[u][rows, p, P:2 * P],
                                            k_16[u][rows, p, 0:2 * P], start=False, stop=True,
                                            skip_group_check=True)
                        ins.then_inc(m_ps[p], 1)
                for u in range(2):
                    pe.wait_ge(m_sb[PAIRS - 1], ab["b"][u])
                    for t in range(2):
                        ins = pe.transpose(ps[u][0:HEADS, 0, t * P:(t + 1) * P], neg_max[u][:, t, :], ident[:, :])
                    ins.then_inc(mt_ps, 1)

                def scores_b(p, u):
                    for e in range(2):
                        rows = slice(SLOT * e, SLOT * e + MAXROW_B + 1)
                        masked(u, e, mask_k)
                        for k in range(2):
                            for q in (s_hi[u], s_lo[u]):
                                ins = pe.matmul(ps[u][:, e, k * TOK:TOK + k * P], q_lo[u][rows, p, k * P:(k + 1) * P],
                                                q[rows, p, k * P:TOK], start=False,
                                                stop=(q is s_lo[u]), skip_group_check=True)
                    ins.then_inc(sc_ps[p], 1)

                def values_b(p, u):
                    pe.wait_ge(pr_sb[p], ab["b"][u])
                    g = p // 2
                    for e in range(2):
                        h = 2 * p + e
                        rows = slice(32 * (h % 4), 32 * (h % 4) + 32)
                        pe.matmul(ps[u][rows, 2 + g % 2, 0:TOK], v_s[u][:, 0, h, :],
                                  probs[u][:, p % 2, e, 0:TOK], start=True, stop=True)
                        ins = pe.matmul(ps[u][rows, 2 + g % 2, P:TOK], v_s[u][:, 1, h, :],
                                        probs[u][:, p % 2, e, TOK:3 * P], start=False, stop=True,
                                        skip_group_check=True)
                    if p % 2:
                        ins.then_inc(av_ps[g], 1)

                for u in range(2):
                    pe.wait_ge(max_row[u], c32["b"])
                pe.wait_ge(ones_b, n[1])
                attend("b", scores_b, values_b)
                output("b", w_out_b)

                transpose_norm("g")
                for u in range(2):
                    pe.wait_ge(xt, ambg["g"][u])
                    for t in range(2):
                        ins = tokens(ps[u][:, 1, t * NE:(t + 1) * NE], x_t[u], slice(t * P, (t + 1) * P), w_gate,
                                     slice(0, NE), 1)
                    ins.then_inc(lg_ps, 1)


def expert_phase(nc, a, t2_dram, xn_dram, xs_dram, ys_dram, logits, ident, ps, sem, out):
    with ExitStack() as ctx:
        def sb(name, shape, dt=F32):
            return ctx.enter_context(nc.sbuf_tensor(name, shape, dt))

        def two(name, shape, dt=F32):
            return [sb(f"{name}{u}", shape, dt) for u in range(2)]

        def sems(name, n=2):
            return [sem(f"{name}{i}") for i in range(n)]

        w1 = sb("w1", [DC + 1, NE, 2, MLP])
        w2 = sb("w2", [P, NE, FT, D])
        b2 = sb("b2", [1, NE, D])
        xn_all = sb("xn_all", [P, NT, D])
        t2_all = sb("t2_all", [P, NT, D])
        y_sel = sb("y_sel", [P, 2, NT, D])
        before = sb("before", [P, P])
        ones = sb("ones", [P, P])
        numbers = sb("numbers", [P, NTILE])
        starts = sb("starts", [P, NT])

        top = sb("top", [P, NT, 8])
        top_at = sb("top_at", [P, NT, 8], U32)
        row = sb("row", [P, NT])
        row2 = sb("row2", [P, NT])
        gates = sb("gates", [P, NT, NE])
        chosen = sb("chosen", [P, NT, 2])
        hot = sb("hot", [P, 2, NT, NE])
        both = sb("both", [P, NT, NE])
        counts = sb("counts", [P, 2, NT * NE])
        seen = sb("seen", [P, NT + 1, NE])
        full = sb("full", [P, NE, NT])
        tiles_of = sb("tiles_of", [P, NE])
        first = sb("first", [P, NE + 1])
        place = sb("place", [P, NT, NE])
        place_s = sb("place_s", [P, NT, NE])
        pos_f = sb("pos_f", [P, 2, NT])
        pos = sb("pos", [P, 2 * NT], U32)
        weight = sb("weight", [P, 2, NT])
        past = sb("past", [P, NTILE, NE - 1])
        expert_f = sb("expert_f", [P, NTILE])
        expert = sb("expert", [P, NTILE], I32)

        rows_in = two("rows_in", [P, D])
        rows_t = two("rows_t", [DC + 1, 2, P])
        hid = two("hid_e", [P, MLP])
        hid_t = two("hid_t", [P, FT, P])
        y_out = two("y_out", [P, D])

        c_in, w_loaded, rows_loaded, pool_c, exp_in, exp_out, choice, counted, routed, experts_known = (
            sem(n) for n in ("c_in", "w_loaded", "rows_loaded", "pool_c", "exp_in", "exp_out", "choice",
                             "counted", "routed", "experts_known"))
        dve_c, scattered, gathered, mixed, stored = (sem(n) for n in (
            "dve_c", "scattered", "gathered", "mixed", "stored"))
        in_loaded, in_ps, in_t, h_ps, h_sb, ht_ps, ht_sb, y_ps, y_sb, y_stored = (sems(n) for n in (
            "in_loaded", "in_ps", "in_t", "h_ps", "h_sb", "ht_ps", "ht_sb", "y_ps", "y_sb", "y_stored"))
        STEPS = NTILE // 2
        HM = MLP // 2

        block = ctx.enter_context(nc.Block("experts"))

        @block.sync
        def _(sp):
            for dst, name in ((before[:, :], "before"), (starts[:, :], "starts"), (numbers[:, :], "numbers")):
                sp.dma_start(dst, a[name]).then_inc(c_in, 16)
            sp.dma_start(xn_all[:, :, :], xn_dram.rearrange("t p d -> p t d")).then_inc(rows_loaded, 16)
            for e in range(NE):
                sp.dma_start(w1[:, e], a["e_w1"][:, e]).then_inc(w_loaded, 16)
                sp.dma_start(w2[:, e], a["e_w2"][:, e]).then_inc(w_loaded, 16)
            sp.dma_start(b2[:, :, :], a["e_b2"]).then_inc(w_loaded, 16)
            sp.dma_start(t2_all[:, :, :], t2_dram.rearrange("t p d -> p t d")).then_inc(rows_loaded, 16)
            sorted_rows = xs_dram.rearrange("(t p) d -> t p d", p=P)
            result = ys_dram.rearrange("(t p) d -> t p d", p=P)
            sp.wait_ge(scattered, 16 * 2 * NT)
            for u in range(2):
                sp.dma_start(rows_in[u][:, :], sorted_rows[u]).then_inc(in_loaded[u], 16)
                sp.sem_inc(y_stored[u], 16)
            with sp.Fori(0, STEPS) as it:
                done = sp.snap(it + 1)
                tile = [sp.snap(it * 2 + u) for u in range(2)]
                nxt = [sp.snap((it * 2 + 2 + u) % NTILE) for u in range(2)]
                for u in range(2):
                    sp.wait_ge(in_ps[u], done)
                    sp.dma_start(rows_in[u][:, :], sorted_rows[nxt[u]]).then_inc(in_loaded[u], 16)
                for u in range(2):
                    sp.wait_ge(y_sb[u], done)
                    sp.dma_start(result[tile[u]], y_out[u][:, :]).then_inc(y_stored[u], 16)
            for u in range(2):
                sp.wait_ge(in_loaded[u], 16 * (STEPS + 1))
            for t in range(NT):
                sp.wait_ge(mixed, t + 1)
                sp.dma_start(out[t], t2_all[:, t, :]).then_inc(stored, 16)
            sp.wait_ge(stored, 16 * NT)

        @block.gpsimd
        def _(gp):
            gp.memset(ones[:, :], 1.0)
            for u in range(2):
                ins = gp.memset(rows_t[u][:, :, :], 1.0)
            ins.then_inc(pool_c, 1)
            gp.wait_ge(routed, 1)
            gp.wait_ge(rows_loaded, 32)
            for t in range(NT):
                for s in range(2):
                    gp.indirect_dma_start(
                        out=xs_dram, out_offset=bass.IndirectOffsetOnAxis(ap=pos[:, s * NT + t:s * NT + t + 1], axis=0),
                        in_=xn_all[:, t, :], in_offset=None).then_inc(scattered, 16)
            for u in range(2):
                gp.wait_ge(y_stored[u], 16 * (STEPS + 1))
            for t in range(NT):
                for s in range(2):
                    gp.indirect_dma_start(
                        out=y_sel[:, s, t, :], out_offset=None, in_=ys_dram,
                        in_offset=bass.IndirectOffsetOnAxis(ap=pos[:, s * NT + t:s * NT + t + 1], axis=0)
                        ).then_inc(gathered, 16)

        @block.scalar
        def _(ac):
            ac.wait_ge(exp_in, 1)
            ac.activation(gates[:, :, :], place[:, :, :], ACT.Exp).then_inc(exp_out, 1)
            with ac.Fori(0, STEPS) as it:
                done = ac.snap(it + 1)
                for u in range(2):
                    ac.wait_ge(h_ps[u], done)
                    for i in range(2):
                        ins = ac.activation(hid[u][:, i * HM:(i + 1) * HM], ps[u][:, 1 + i, 0:HM], ACT.Gelu)
                    ins.then_inc(h_sb[u], 1)
                for u in range(2):
                    ac.wait_ge(ht_ps[u], done)
                    ac.copy(hid_t[u][:, 3:6, :], ps[u][:, 2, 0:HM].rearrange("p (f n) -> p f n", f=3)
                            ).then_inc(ht_sb[u], 1)

        @block.vector
        def _(dv):
            count = [0]

            def step(ins):
                count[0] += 1
                ins.then_inc(dve_c, 1)
                dv.wait_ge(dve_c, count[0])

            def over(x, shape, axis):
                return x.unsqueeze(axis).to_broadcast(shape)

            TE = [P, NT, NE]
            dv.wait_ge(c_in, 48)
            step(dv.tensor_reduce(row[:, :], logits[:, :, :], AX.X, ALU.max))
            dv.tensor_tensor(place[:, :, :], logits[:, :, :], over(row[:, :], TE, 2), ALU.subtract).then_inc(exp_in, 1)
            dv.wait_ge(exp_out, 1)
            step(dv.tensor_reduce(row[:, :], gates[:, :, :], AX.X, ALU.add))
            step(dv.reciprocal(row[:, :], row[:, :]))
            step(dv.tensor_tensor(gates[:, :, :], gates[:, :, :], over(row[:, :], TE, 2), ALU.mult))
            for t in range(NT):
                ins = dv.max(top[:, t, :], gates[:, t, :])
            step(ins)
            for t in range(NT):
                ins = dv.max_index(top_at[:, t, :], top[:, t, :], gates[:, t, :])
            step(ins)
            step(dv.tensor_copy(chosen[:, :, :], top_at[:, :, 0:2]))
            for s in range(2):
                ins = dv.tensor_tensor(hot[:, s], numbers[:, 0:NE].unsqueeze(1).to_broadcast(TE),
                                       over(chosen[:, :, s], TE, 2), ALU.is_equal)
            step(ins)
            dv.tensor_tensor(both[:, :, :], hot[:, 0], hot[:, 1], ALU.add).then_inc(choice, 1)
            step(dv.tensor_tensor(row2[:, :], top[:, :, 0], top[:, :, 1], ALU.add))
            step(dv.tensor_scalar(row2[:, :], row2[:, :], 1e-9, None, ALU.add))
            step(dv.reciprocal(row2[:, :], row2[:, :]))
            for s in range(2):
                ins = dv.tensor_tensor(weight[:, s, :], top[:, :, s], row2[:, :], ALU.mult)
            step(ins)
            dv.wait_ge(counted, 1)
            step(dv.tensor_copy(counts[:, :, :], ps[0][:, 0:2, 0:NT * NE]))
            step(dv.memset(seen[:, 0, :], 0.0))
            total = counts[:, 1, :].rearrange("p (t e) -> p t e", e=NE)
            for t in range(NT):
                step(dv.tensor_tensor(seen[:, t + 1, :], seen[:, t, :], total[:, t, :], ALU.add))
            step(dv.tensor_tensor(full[:, :, :], over(seen[:, NT, :], [P, NE, NT], 2),
                                  starts[:, :].unsqueeze(1).to_broadcast([P, NE, NT]), ALU.is_gt))
            step(dv.tensor_reduce(tiles_of[:, :], full[:, :, :], AX.X, ALU.add))
            step(dv.memset(first[:, :], 0.0))
            for e in range(NE):
                step(dv.tensor_tensor(first[:, e + 1:e + 2], first[:, e:e + 1], tiles_of[:, e:e + 1], ALU.add))
            TL = [P, NTILE, NE - 1]
            step(dv.tensor_tensor(past[:, :, :], over(numbers[:, :], TL, 2),
                                  first[:, 1:NE].unsqueeze(1).to_broadcast(TL), ALU.is_ge))
            step(dv.tensor_reduce(expert_f[:, :], past[:, :, :], AX.X, ALU.add))
            dv.tensor_copy(expert[:, :], expert_f[:, :]).then_inc(experts_known, 1)
            step(dv.tensor_tensor(place[:, :, :], counts[:, 0, :].rearrange("p (t e) -> p t e", e=NE),
                                  seen[:, 0:NT, :], ALU.add))
            step(dv.scalar_tensor_tensor(out=place[:, :, :], in0=first[:, 0:NE].unsqueeze(1).to_broadcast(TE),
                                         scalar=float(P), in1=place[:, :, :], op0=ALU.mult, op1=ALU.add))
            for s in range(2):
                step(dv.tensor_tensor(place_s[:, :, :], place[:, :, :], hot[:, s], ALU.mult))
                step(dv.tensor_reduce(pos_f[:, s, :], place_s[:, :, :], AX.X, ALU.add))
            dv.tensor_copy(pos[:, :], pos_f[:, :, :].rearrange("p s t -> p (s t)")).then_inc(routed, 1)

            def rows_to_channels(u, reached):
                dv.wait_ge(in_ps[u], reached)
                dv.tensor_copy(rows_t[u][0:DC, :, :], ps[u][0:DC, 0, 0:2 * P].rearrange("p (c n) -> p c n", c=2)
                               ).then_inc(in_t[u], 1)

            dv.wait_ge(pool_c, 1)
            for u in range(2):
                rows_to_channels(u, 1)
            with dv.Fori(0, STEPS) as it:
                done, two_done, stored_before = dv.snap(it + 1), dv.snap(it + 2), dv.snap(it * 16 + 16)
                for u in range(2):
                    dv.wait_ge(ht_ps[u], done)
                    dv.tensor_copy(hid_t[u][:, 0:3, :], ps[u][:, 1, 0:HM].rearrange("p (f n) -> p f n", f=3)
                                   ).then_inc(ht_sb[u], 1)
                for u in range(2):
                    rows_to_channels(u, two_done)
                for u in range(2):
                    dv.wait_ge(y_ps[u], done)
                    dv.wait_ge(y_stored[u], stored_before)
                    dv.tensor_copy(y_out[u][:, :], ps[u][:, 3, 0:D]).then_inc(y_sb[u], 1)
            dv.wait_ge(rows_loaded, 32)
            for t in range(NT):
                dv.wait_ge(gathered, 32 * NT)
                step(dv.scalar_tensor_tensor(out=t2_all[:, t, :], in0=y_sel[:, 0, t, :], scalar=weight[:, 0, t:t + 1],
                                             in1=t2_all[:, t, :], op0=ALU.mult, op1=ALU.add))
                dv.scalar_tensor_tensor(out=t2_all[:, t, :], in0=y_sel[:, 1, t, :], scalar=weight[:, 1, t:t + 1],
                                        in1=t2_all[:, t, :], op0=ALU.mult, op1=ALU.add).then_inc(mixed, 1)

        @block.tensor
        def _(pe):
            pe.wait_ge(pool_c, 1)
            pe.wait_ge(c_in, 48)
            pe.wait_ge(choice, 1)
            pairs = both[:, :, :].rearrange("p t e -> p (t e)")
            pe.matmul(ps[0][:, 0, 0:NT * NE], before[:, :], pairs, start=True, stop=True)
            pe.matmul(ps[0][:, 1, 0:NT * NE], ones[:, :], pairs, start=True, stop=True).then_inc(counted, 1)
            pe.wait_ge(routed, 1)
            pe.wait_ge(w_loaded, 16 * (2 * NE + 1))
            pe.wait_ge(experts_known, 1)

            def transpose_rows(u, reached):
                pe.wait_ge(in_loaded[u], reached)
                for c in range(2):
                    ins = pe.transpose(ps[u][0:DC, 0, c * P:(c + 1) * P], rows_in[u][:, c * DC:(c + 1) * DC],
                                       ident[:, :])
                ins.then_inc(in_ps[u], 1)

            for u in range(2):
                transpose_rows(u, 16)
            with pe.Fori(0, STEPS) as it:
                done, loaded = pe.snap(it + 1), pe.snap(it * 16 + 32)
                two_done = pe.snap(it * 2 + 2)
                e = [pe.value_load(expert[0:1, bass.ds(it * 2 + u, 1)], min_val=0, max_val=NE - 1) for u in range(2)]
                for u in range(2):
                    pe.wait_ge(in_t[u], done)
                    for i in range(2):
                        cols = slice(i * HM, (i + 1) * HM)
                        pe.matmul(ps[u][:, 1 + i, 0:HM], rows_t[u][:, 0, :], w1[:, bass.ds(e[u], 1), 0, cols],
                                  start=True, stop=False)
                        ins = pe.matmul(ps[u][:, 1 + i, 0:HM], rows_t[u][0:DC, 1, :],
                                        w1[0:DC, bass.ds(e[u], 1), 1, cols], start=False, stop=True)
                    ins.then_inc(h_ps[u], 1)
                for u in range(2):
                    pe.wait_ge(h_sb[u], done)
                    for f in range(FT):
                        ins = pe.transpose(ps[u][:, 1 + f // 3, (f % 3) * P:(f % 3 + 1) * P],
                                           hid[u][:, f * P:(f + 1) * P], ident[:, :])
                    ins.then_inc(ht_ps[u], 1)
                for u in range(2):
                    transpose_rows(u, loaded)
                for u in range(2):
                    pe.wait_ge(ht_sb[u], two_done)
                    for f in range(FT):
                        pe.matmul(ps[u][:, 3, 0:D], hid_t[u][:, f, :], w2[:, bass.ds(e[u], 1), f, :],
                                  start=(f == 0), stop=False)
                    pe.matmul(ps[u][:, 3, 0:D], ones[0:1, :], b2[:, bass.ds(e[u], 1), :],
                              start=False, stop=True).then_inc(y_ps[u], 1)


def _layouts(i):
    f = np.float32

    def rows(w, bias=None):
        out = np.zeros((DC + (bias is not None), 2, w.shape[1]), f)
        out[:DC, 0], out[:DC, 1] = w[:DC], w[DC:]
        if bias is not None:
            out[DC, 0] = bias
        return out

    def head_rows(w, bias):
        out = np.zeros((P, GROUPS, w.shape[1]), f)
        for h in range(HEADS):
            r = 32 * (h % 4)
            out[r:r + HD, h // 4] = w[h * HD:(h + 1) * HD]
        out[HD, 0] = bias
        return out

    tables = np.zeros((P, 2 * WS, P), f)
    for e in range(2):
        s = SLOT * e
        for at in range(WS):
            for c in range(HD):
                tables[s + c, at, s + c] = 1.0
                tables[s + c, at, s + HD + c] = 1.0
            for r in range(MAXROW + 1, SLOT):
                tables[s + r, at, s + r] = 1.0
            for key in range(WS):
                for half in range(2):
                    r = s + HD * half
                    tables[r:r + HD, at, s + REL + key] = i["L0_conv_rel_pos_h"][at - key + WS - 1]
                    tables[r:r + HD, WS + at, s + REL + WS + key] = i["L0_conv_rel_pos_w"][at - key + WS - 1]
    part = np.zeros((P, 2), f)
    slot_rows = np.zeros((P, KEYS), f)
    slot_rows_q = np.zeros((P, TOK), f)
    for e in range(2):
        s = SLOT * e
        part[s:s + HD, 0] = 1.0
        part[s + HD:s + 2 * HD, 1] = 1.0
        part[s + MAXROW:s + SLOT, 0] = 1.0
        keys = [(y, x, -1) for y in range(WS) for x in range(WS)]
        keys += [(y, x - WS, 0) for y in range(WS) for x in range(WS, S)]
        keys += [(y - WS, x % WS, 1 + x // WS) for y in range(WS, S) for x in range(S)]
        keys += [(y, x, 3) for y in range(WS) for x in range(WS)]
        left = S - WS
        for n, (y, x, w) in enumerate(keys):
            slot_rows[s + REL + y, n] = 1.0
            slot_rows[s + REL + WS + x, n] = 1.0
            slot_rows[s + MAXROW, n] = 1.0
            if w >= 0:
                ok = (x >= left, y >= left, y >= left or x >= left) if w == 3 else (w == 0, w == 1, w == 2)
                for m in range(3):
                    slot_rows[s + MAXROW + 1 + m, n] = 0.0 if ok[m] else -BIG
        for y in range(S):
            for x in range(S):
                if y >= WS or x >= WS:
                    m = 0 if y < WS else 1 if x < WS else 2
                    slot_rows_q[s + MAXROW + 1 + m, y * S + x] = 1.0
    later = np.where(np.arange(P)[None, :] > np.arange(P)[:, None], f(-BIG), f(0))
    masks = np.stack([later, later, later.T, later.T], 1).reshape(P, 4 * P)
    qkv_b = i["L0_conv_qkv_b"]
    heads = [i[f"L1_attn_W_{n}"].transpose(1, 0, 2).reshape(D, D) for n in "qkv"]
    norms = np.zeros((DC, 8), f)
    for n, name in enumerate(("norm1_w", "norm1_b", "norm2_w", "norm2_b")):
        norms[:, 2 * n:2 * n + 2] = i[f"L0_conv_{name}"].reshape(2, DC).T
    e_w1 = np.zeros((DC + 1, NE, 2, MLP), f)
    e_w1[:DC] = i["L1_ffn_w1"].reshape(NE, 2, DC, MLP).transpose(2, 0, 1, 3)
    e_w1[DC, :, 0] = i["L1_ffn_b1"]
    return {
        "x": i["x"].reshape(B, 2, P, D).transpose(0, 2, 1, 3),
        "w_qkv_a": rows(i["L0_conv_qkv_w"], qkv_b),
        "w_qkv_b": rows(np.concatenate(heads, 1)),
        "w_out_a": head_rows(i["L0_conv_proj_w"], i["L0_conv_proj_b"]),
        "w_out_b": head_rows(i["L1_attn_lin_w"].T, i["L1_attn_lin_b"]),
        "w_fc1": rows(i["L0_conv_fc1_w"]),
        "w_fc2": i["L0_conv_fc2_w"].reshape(FT, P, D).transpose(1, 0, 2),
        "b_fc1": i["L0_conv_fc1_b"].reshape(FT, P).T,
        "b_fc2": np.tile(i["L0_conv_fc2_b"], (P, 2)),
        "norms": norms,
        "w_gate": rows(i["L1_ffn_gate_w"], i["L1_ffn_gate_b"]),
        "k_bias": qkv_b[D:2 * D].reshape(2, DC).T,
        "v_bias": np.tile(qkv_b[2 * D:], (P, 1)),
        "rel_tables": tables,
        "part_rows": part,
        "slot_rows": slot_rows,
        "slot_rows_q": slot_rows_q,
        "masks": masks,
        "ident": np.eye(P, dtype=f),
        "before": np.triu(np.ones((P, P), f), 1),
        "starts": np.tile(np.arange(NT, dtype=f) * P, (P, 1)),
        "numbers": np.tile(np.arange(NTILE, dtype=f), (P, 1)),
        "e_w1": e_w1,
        "e_w2": i["L1_ffn_w2"].reshape(NE, FT, P, D).transpose(2, 0, 1, 3),
        "e_b2": i["L1_ffn_b2"].reshape(1, NE, D),
    }


def kernel(**inputs):
    import concourse.bacc as bacc
    from concourse.bass_utils import run_bass_kernel_spmd

    nc = bacc.Bacc("TRN2", target_bir_lowering=False, num_devices=1)
    arrays, aps = {}, {}
    for name, value in _layouts({k: np.asarray(v) for k, v in inputs.items()}).items():
        value = np.ascontiguousarray(value)
        arrays[f"in_{name}"] = value
        aps[name] = nc.dram_tensor(f"in_{name}", value.shape, mybir.dt.from_np(value.dtype),
                                   kind="ExternalInput").ap()
    result = nc.dram_tensor("result", (NT, P, D), F32, kind="ExternalOutput").ap()
    build(nc, aps, result)
    run = run_bass_kernel_spmd(nc, [arrays], core_ids=[0])
    return run.results[0]["result"].reshape(B, S, S, D)
```

```python
from contextlib import ExitStack

import numpy as np

import concourse.bass as bass
from concourse import mybir

F32 = mybir.dt.float32
F32R = mybir.dt.float32r
BF16 = mybir.dt.bfloat16
U32 = mybir.dt.uint32
I32 = mybir.dt.int32
ALU = mybir.AluOpType
ACT = mybir.ActivationFunctionType
AX = mybir.AxisListType

P = 128
B, S, D = 8, 16, 192
TOK = S * S
NT = B * TOK // P
HEADS, HD, WS = 12, 16, 14
PAIRS, GROUPS = HEADS // 2, HEADS // 4
DC = D // 2
MLP = 4 * D
FT = MLP // P
NE = 8
WIN = WS * WS
HALF = WIN // 2
OUT = TOK - WIN
KEYS = TOK + WIN
EDGE = (S - WS) * WS
SLOT = 64
REL = 32
MAXROW = 60
WIDE = 66
BIG = 1.0e30
NTILE = 2 * B * TOK // P + NE
SCALE_A, SCALE_B = 0.25, 0.0625
EPS = 1e-5


def window_pieces(t):
    return t[..., 0:WS, 0:WS], t[..., 0:WS, WS:S], t[..., WS:S, 0:S]


def build(nc, a, out):
    q_scratch = nc.dram_tensor("q_scratch", (2, 2, 2, DC, 2, TOK), F32, kind="Internal").ap()
    k_scratch = nc.dram_tensor("k_scratch", (2, 2, DC, 2, TOK), F32, kind="Internal").ap()
    pad_scratch = nc.dram_tensor("pad_scratch", (2, DC, 2, WIN), F32, kind="Internal").ap()
    max_scratch = nc.dram_tensor("max_scratch", (2, HEADS, TOK), F32, kind="Internal").ap()
    t2_dram = nc.dram_tensor("t2_dram", (NT, P, D), F32, kind="Internal").ap()
    xn_dram = nc.dram_tensor("xn_dram", (NT, P, D), F32, kind="Internal").ap()
    xs_dram = nc.dram_tensor("sorted_dram", (NTILE * P, D), F32, kind="Internal").ap()
    ys_dram = nc.dram_tensor("expert_out_dram", (NTILE * P, D), F32, kind="Internal").ap()
    with ExitStack() as keep:
        logits = keep.enter_context(nc.sbuf_tensor("logits", [P, NT, NE], F32))
        ident = keep.enter_context(nc.sbuf_tensor("ident", [P, P], F32))
        ps = [keep.enter_context(nc.psum_tensor(f"ps{u}", [P, 4, 512], F32)) for u in range(2)]

        def sem(name):
            return keep.enter_context(nc.semaphore(name))

        attention_phase(nc, a, q_scratch, k_scratch, pad_scratch, max_scratch, t2_dram, xn_dram, xs_dram, logits, ident, ps, sem)
        expert_phase(nc, a, t2_dram, xn_dram, xs_dram, ys_dram, logits, ident, ps, sem, out)


def attention_phase(nc, a, q_scratch, k_scratch, pad_scratch, max_scratch, t2_dram, xn_dram, xs_dram, logits, ident, ps, sem):
    with ExitStack() as ctx:
        def sb(name, shape, dt=F32):
            return ctx.enter_context(nc.sbuf_tensor(name, shape, dt))

        def two(name, shape, dt=F32):
            return [sb(f"{name}{u}", shape, dt) for u in range(2)]

        def sems(name, n):
            return [sem(f"{name}{i}") for i in range(n)]

        w_qkv_a = sb("w_qkv_a", [DC + 1, 2, 3 * D])
        w_qkv_b = sb("w_qkv_b", [DC, 2, 3 * D])
        w_out_a = sb("w_out_a", [P, GROUPS, D])
        w_out_b = sb("w_out_b", [P, GROUPS, D])
        w_fc1 = sb("w_fc1", [DC, 2, MLP])
        w_fc2 = sb("w_fc2", [P, FT, D])
        b_fc1 = sb("b_fc1", [P, FT])
        b_fc2 = sb("b_fc2", [P, 2 * D])
        norms = sb("norms", [DC, 8])
        k_bias = sb("k_bias", [DC, 2])
        w_gate = sb("w_gate", [DC + 1, 2, NE])
        rel_w = sb("rel_w", [P, 2 * WS, P])
        mask_q = sb("mask_q", [P, 2, P], BF16)
        mask_k = sb("mask_k", [P, 2, P], BF16)
        ident16 = sb("ident16", [P, P], BF16)
        half_neg = sb("half_neg", [P, 2])
        eps = sb("eps", [P, 2])
        slot_rows = sb("slot_rows", [P, KEYS])
        v_bias = sb("v_bias", [P, D])

        ZEROS = NTILE * D // 16
        zero = sb("zero", [P, ZEROS])

        x_in = two("x_in", [P, 2, D])
        x_n = two("x_n", [P, 2, D])
        stats = two("stats", [P, 2, 6])
        mean_var = two("mean_var", [P, 2, 2])
        var_eps = two("var_eps", [P, 2])
        rstd = two("rstd", [P, 2])
        x_t = two("x_t", [DC + 1, 2, TOK])
        x_tw = two("x_tw", [DC + 1, 2, TOK])
        s_q = two("s_q", [P, PAIRS, TOK])
        work_all = sb("work", [P, 2, 4096])
        q_s = two("q_s", [P, HEADS * TOK + WIDE - OUT], F32R)
        k_s = two("k_s", [P, HEADS, KEYS], F32R)
        v_s = two("v_s", [P, 4, HEADS, 32])
        o_t = two("o_t", [P, GROUPS, TOK])
        x_2 = two("x_2", [P, 2 * D])
        x_2b = two("x_2b", [P, 2 * D])
        x_3 = two("x_3", [P, 2 * D])
        den = two("den", [P, TOK])
        neg_max = two("neg_max", [P, 3, HEADS])
        neg_max_t = two("neg_max_t", [HEADS, TOK])

        def yx(t):
            return t.rearrange("p c (y x) -> p c y x", x=S)

        def win_order(t):
            return (t[:, :, 0:WIN].rearrange("p c (y x) -> p c y x", x=WS),
                    t[:, :, WIN:WIN + EDGE].rearrange("p c (y x) -> p c y x", x=S - WS),
                    t[:, :, WIN + EDGE:TOK].rearrange("p c (y x) -> p c y x", x=S))

        work = [work_all[:, u, :] for u in range(2)]
        rel_sum = [w[:, 0:PAIRS * TOK].rearrange("p (g n) -> p g n", g=PAIRS) for w in work]
        probs = [w.rearrange("p (r e n) -> p r e n", r=4, e=2) for w in work]
        hid = [w[:, 0:FT * TOK].rearrange("p (f n) -> p f n", f=FT) for w in work]
        staged = [w[0:DC, 0:8 * TOK].rearrange("p (c n) -> p c n", n=TOK) for w in work]
        q_heads = [t[:, 0:HEADS * TOK].rearrange("p (h n) -> p h n", n=TOK) for t in q_s]

        def slot_order(t):
            return t.rearrange("g (h c) s n -> (c s) (g h) n", c=HD)

        w_in, late_in, pool_c, dve_c, pad_out, pad_in, zero_out = (sem(f"set_{n}") for n in (
            "first_in", "late_in", "pool", "dve", "pad_out", "pad_in", "zeros"))
        x_loaded = sems("x_loaded", 2)
        mask_in = o_t[0][:, :, :].rearrange("p g n -> p (g n)")[:, 0:4 * P]
        loads = ((k_bias[:, :], "k_bias"), (slot_rows[:, :], "slot_rows"), (v_bias[:, :], "v_bias"),
                 (mask_in, "masks"), (ident[:, :], "ident"), (norms[:, :], "norms"),
                 (w_qkv_a[:, :, :], "w_qkv_a"))
        late_loads = ((rel_w[:, :, :], "rel_tables"), (w_out_a[:, :, :], "w_out_a"), (w_fc1[:, :, :], "w_fc1"),
                      (w_fc2[:, :, :], "w_fc2"), (b_fc1[:, :], "b_fc1"), (b_fc2[:, :], "b_fc2"),
                      (w_qkv_b[:, :, :], "w_qkv_b"), (w_out_b[:, :, :], "w_out_b"), (w_gate[:, :, :], "w_gate"))
        FIRST_IN = 16 * len(loads)
        LATE_IN = 16 * (len(late_loads) + 2)

        def key_rows(r):
            return slot_rows[r:r + SLOT - REL, :].unsqueeze(1).to_broadcast([SLOT - REL, HEADS, KEYS])

        with nc.Block("setup") as block:
            @block.sync
            def _(sp):
                for dst, name in loads:
                    sp.dma_start(dst, a[name]).then_inc(w_in, 16)
                for u in range(2):
                    sp.dma_start(x_in[u][:, :, :], a["x"][u]).then_inc(x_loaded[u], 16)
                sp.wait_ge(dve_c, 3)
                for part in range(2):
                    sp.dma_start(pad_scratch[:, :, part].rearrange("g r n -> r g n"),
                                 staged[1][:, 4 * part:4 * part + 2, 0:WIN]).then_inc(pad_out, 16)
                for u in range(2):
                    sp.dma_start(s_q[u][:, :, :], a["slot_rows_q"].unsqueeze(1).to_broadcast([P, PAIRS, TOK])
                                 ).then_inc(late_in, 16)
                for dst, name in late_loads:
                    sp.dma_start(dst, a[name]).then_inc(late_in, 16)
                sp.wait_ge(pad_out, 32)
                for u in range(2):
                    for r in (0, SLOT):
                        sp.dma_start(k_s[u][r:r + 2 * HD, :, TOK:KEYS].bitcast(F32),
                                     slot_order(pad_scratch)).then_inc(pad_in, 16)
                sp.wait_ge(pool_c, 3)
                rows = xs_dram.rearrange("(p r) d -> p (r d)", p=P)
                for at in range(0, NTILE * D, ZEROS):
                    sp.dma_start(rows[:, at:at + ZEROS], zero[:, :]).then_inc(zero_out, 16)
                sp.wait_ge(w_in, FIRST_IN)

            @block.gpsimd
            def _(gp):
                for u in range(2):
                    gp.memset(v_s[u][:, :, :, :], 1.0)
                    gp.memset(x_t[u][:, :, :], 1.0).then_inc(pool_c, 1)
                for u in range(2):
                    gp.memset(q_s[u][:, HEADS * TOK:].bitcast(F32), 0.0)
                gp.memset(eps[:, :], EPS)
                gp.memset(half_neg[:, :], -0.5)
                gp.memset(zero[:, :], 0.0).then_inc(pool_c, 1)

            @block.scalar
            def _(ac):
                ac.wait_ge(w_in, FIRST_IN)
                ac.copy(k_s[0][REL:SLOT, :, :], key_rows(REL))
                ac.copy(k_s[1][REL:SLOT, :, :], key_rows(REL))
                ac.wait_ge(pool_c, 2)
                for u in range(2):
                    for t in (2, 3):
                        ac.copy(v_s[u][:, t, :, 0:HD], v_bias[:, :].rearrange("p (h d) -> p h d", h=HEADS))

            @block.vector
            def _(dv):
                count = [0]

                def step(ins):
                    count[0] += 1
                    ins.then_inc(dve_c, 1)
                    dv.wait_ge(dve_c, count[0])

                dv.wait_ge(w_in, FIRST_IN)
                for c in range(2):
                    ins = dv.tensor_scalar(x_tw[1][0:DC, c, 0:WIN], k_bias[:, c:c + 1].to_broadcast([DC, WIN]),
                                           SCALE_A, None, ALU.mult)
                step(ins)
                step(dv.tensor_copy(staged[1][:, 0:2, 0:WIN].bitcast(F32R), x_tw[1][0:DC, :, 0:WIN]))
                step(dv.tensor_tensor(staged[1][:, 4:6, 0:WIN].bitcast(F32R), x_tw[1][0:DC, :, 0:WIN],
                                      staged[1][:, 0:2, 0:WIN], ALU.subtract))
                for u in range(2):
                    dv.tensor_copy(k_s[u][SLOT + REL:P, :, :], key_rows(SLOT + REL))
                step(dv.tensor_copy(ident16[:, :], ident[:, :]))
                masks = mask_in.rearrange("p (m a k) -> p m a k", m=2, a=2)
                step(dv.tensor_copy(mask_q[:, :, :], masks[:, 0]))
                step(dv.tensor_copy(mask_k[:, :, :], masks[:, 1]))

        q_out, k_out, q_slots, k_slots, max_out, max_row = (sems(n, 2) for n in (
            "q_out", "k_out", "q_slots", "k_slots", "max_out", "max_row"))
        t2_out, xn_out = sems("t2_out", 2), sems("xn_out", 2)
        st, ag, ve, rs, xn, xt_ps, xt = (sem(n) for n in (
            "ln_stats", "ln_mean", "ln_var", "ln_rstd", "ln_out", "xt_ps", "xt_sb"))
        xtw = sem("xtw")
        q_ps, k_ps, v_ps, q_h, k_h, q_l, k_l, v_sb, mt_ps, mt_sb, o_ps, res = (sem(n) for n in (
            "q_ps", "k_ps", "v_ps", "q_h", "k_h", "q_l", "k_l", "v_sb", "mt_ps", "mt_sb", "o_ps", "res"))
        m_ps, m_sb, sc_ps, pr_sb = (sems(n, PAIRS) for n in ("m_ps", "m_sb", "sc_ps", "pr_sb"))
        av_ps, dn_sb, rc_sb, ot_sb = (sems(n, GROUPS) for n in ("av_ps", "dn_sb", "rc_sb", "ot_sb"))
        ry_ps, ry_sb, rx_ps = (sems(n, 2) for n in ("ry_ps", "ry_sb", "rx_ps"))
        rel_done, q_even, q_odd, q_done, cleared = (sem(n) for n in (
            "rel_done", "q_even", "q_odd", "q_done", "cleared"))
        f1_ps, hid_sb, f2_ps, x2b_done, mlp_done, lg_ps, lg_sb = (sem(n) for n in (
            "f1_ps", "hid_sb", "f2_ps", "x2b_done", "mlp_done", "lg_ps", "lg_sb"))

        went_on = sem("went_on")

        def hold(eng):
            eng.sem_inc(went_on, 1)

        block = ctx.enter_context(nc.Block("attention"))

        def numbers(eng, it):
            return [eng.snap(it * 2 + 1), eng.snap(it * 2 + 2)]

        def reached(eng, it, stages="ab"):
            return {k: [eng.snap(it * (2 * len(stages)) + 2 * at + 1 + u) for u in range(2)]
                    for at, k in enumerate(stages)}

        def transfers(eng, it, in_a, in_b=None):
            in_b = in_b or in_a
            return {"a": eng.snap(it * (16 * (in_a + in_b)) + 16 * in_a),
                    "b": eng.snap(it * (16 * (in_a + in_b)) + 16 * (in_a + in_b))}

        @block.sync
        def _(sp):
            for u in range(2):
                sp.sem_inc(t2_out[u], 16)
                sp.sem_inc(xn_out[u], 16)
            sp.wait_ge(late_in, LATE_IN)
            sp.wait_ge(pad_in, 16 * 4)
            with sp.Fori(0, B // 2) as it:
                n = numbers(sp, it)
                ab, ambg = reached(sp, it), reached(sp, it, "ambg")
                one, two_in, q_four = transfers(sp, it, 1), transfers(sp, it, 2), transfers(sp, it, 1, 4)
                nxt = [sp.snap((it * 2 + 2 + u) % B) for u in range(2)]
                row = [sp.snap(it * 4 + 2 * u) for u in range(2)]

                def to_dram(k):
                    for u in range(2):
                        sp.wait_ge(q_h, ab[k][u])
                        if k == "a":
                            sp.dma_start(q_scratch[u, 0, :, :, 0].rearrange("g r n -> r g n"),
                                         staged[u][:, 0:2, :]).then_inc(q_out[u], 16)
                        else:
                            for part in range(2):
                                if part:
                                    sp.wait_ge(q_l, n[u])
                                for twice in range(2):
                                    sp.dma_start(q_scratch[u, part, :, :, twice].rearrange("g r n -> r g n"),
                                                 staged[u][:, 4 * part:4 * part + 2, :]).then_inc(q_out[u], 16)
                        for ready, part in ((k_h, 0), (k_l, 1)):
                            sp.wait_ge(ready, ab[k][u])
                            sp.dma_start(k_scratch[u, :, :, part].rearrange("g r n -> r g n"),
                                         staged[u][:, 2 + 4 * part:4 + 4 * part, :]).then_inc(k_out[u], 16)

                def to_slots(k):
                    for u in range(2):
                        sp.wait_ge(q_out[u], q_four[k])
                        for e in range(2):
                            if k == "a":
                                dst = s_q[u][SLOT * e:SLOT * e + HD, :, :]
                                src = q_scratch[u, 0, :, :, 0].rearrange("g (p e c) n -> e c (g p) n", e=2, c=HD)[e]
                            else:
                                dst = q_heads[u][SLOT * e:SLOT * e + 2 * HD, :, :].bitcast(F32)
                                src = slot_order(q_scratch[u, e])
                            sp.dma_start(dst, src).then_inc(q_slots[u], 16)
                        sp.wait_ge(k_out[u], two_in[k])
                        for r in (0, SLOT):
                            sp.dma_start(k_s[u][r:r + 2 * HD, :, 0:TOK].bitcast(F32),
                                         slot_order(k_scratch[u])).then_inc(k_slots[u], 16)

                def max_rows(k):
                    for u in range(2):
                        sp.wait_ge(mt_sb, ab[k][u])
                        sp.dma_start(max_scratch[u], neg_max_t[u][:, :]).then_inc(max_out[u], 16)
                    for u in range(2):
                        sp.wait_ge(max_out[u], one[k])
                        sp.dma_start(q_heads[u][MAXROW:MAXROW + 1, :, :].bitcast(F32),
                                     max_scratch[u:u + 1]).then_inc(max_row[u], 16)

                to_dram("a")
                to_slots("a")
                max_rows("a")
                for u in range(2):
                    sp.wait_ge(res, ab["a"][u])
                    sp.dma_start(x_in[u][:, :, :], a["x"][nxt[u]]).then_inc(x_loaded[u], 16)
                to_dram("b")
                to_slots("b")
                max_rows("b")
                for u in range(2):
                    sp.wait_ge(res, ab["b"][u])
                    sp.dma_start(t2_dram[bass.ds(row[u], 2)].rearrange("t p d -> p t d"),
                                 x_2[u][:, :].rearrange("p (t d) -> p t d", t=2)).then_inc(t2_out[u], 16)
                for u in range(2):
                    sp.wait_ge(xn, ambg["g"][u])
                    sp.dma_start(xn_dram[bass.ds(row[u], 2)].rearrange("t p d -> p t d"),
                                 x_n[u][:, :, :]).then_inc(xn_out[u], 16)
            for u in range(2):
                sp.wait_ge(t2_out[u], 16 * (B // 2 + 1))
                sp.wait_ge(xn_out[u], 16 * (B // 2 + 1))
                sp.wait_ge(x_loaded[u], 16 * (B // 2 + 1))
            sp.wait_ge(zero_out, 16 * 16)

        @block.gpsimd
        def _(gp):
            with gp.Fori(0, B // 2) as it:
                n = numbers(gp, it)
                ab, ambg = reached(gp, it), reached(gp, it, "ambg")
                clears = [gp.snap(it * 4 + i + 1) for i in range(3)]

                def rstds(k, images=(0, 1)):
                    for u in images:
                        gp.wait_ge(ag, ambg[k][u])
                        gp.tensor_tensor(var_eps[u][:, :], mean_var[u][:, :, 1], eps[:, :],
                                         ALU.add).then_inc(ve, 1)
                        gp.wait_ge(ve, ambg[k][u])
                        gp.tensor_tensor(rstd[u][:, :], var_eps[u][:, :], half_neg[:, :],
                                         ALU.pow).then_inc(rs, 1)

                rstds("a")
                for u in range(2):
                    gp.wait_ge(xt, ambg["a"][u])
                    hold(gp)
                    for c in range(2):
                        for dst, src in zip(win_order(x_tw[u][:, c:c + 1, :]),
                                            window_pieces(yx(x_t[u][:, c:c + 1, :]))):
                            ins = gp.tensor_copy(dst[:, 0], src[:, 0])
                    ins.then_inc(xtw, 1)
                for u in range(2):
                    rstds("m", [u])
                    gp.wait_ge(res, ab["a"][u])
                    gp.tensor_tensor(x_2b[u][:, :], x_2[u][:, :], b_fc2[:, :], ALU.add).then_inc(x2b_done, 1)
                rstds("b")
                for u in range(2):
                    for half, r in enumerate((REL, SLOT + REL)):
                        if u == half == 0:
                            gp.wait_ge(rs, ambg["b"][1])
                        else:
                            gp.wait_ge(cleared, clears[2 * u + half - 1])
                        hold(gp)
                        gp.memset(q_heads[u][r:r + SLOT - REL, :, :].bitcast(F32), 0.0).then_inc(cleared, 1)
                rstds("g")

        @block.scalar
        def _(ac):
            with ac.Fori(0, B // 2) as it:
                n, ab, ambg = numbers(ac, it), reached(ac, it), reached(ac, it, "ambg")
                k_sent = transfers(ac, it, 2)

                def channels(k, scale, shift):
                    for u in range(2):
                        ac.wait_ge(xt_ps, ambg[k][u])
                        for c in range(2):
                            src = ps[u][0:DC, 0, c * TOK:(c + 1) * TOK]
                            if scale is None:
                                ins = ac.copy(x_t[u][0:DC, c, :], src)
                            else:
                                ins = ac.activation(x_t[u][0:DC, c, :], src, ACT.Identity,
                                                    bias=norms[:, shift + c:shift + c + 1],
                                                    scale=norms[:, scale + c:scale + c + 1])
                        ins.then_inc(xt, 1)

                def high_parts(k, scale):
                    for u in range(2):
                        ac.wait_ge(q_ps, ab[k][u])
                        dst = staged[u][:, 0:2, :].rearrange("p g n -> p (g n)")
                        ac.activation(dst if k == "a" else dst.bitcast(F32R), ps[u][0:DC, 1, :],
                                      ACT.Copy).then_inc(q_h, 1)
                    for u in range(2):
                        ac.wait_ge(k_ps, ab[k][u])
                        ac.activation(staged[u][:, 2:4, :].rearrange("p g n -> p (g n)").bitcast(F32R),
                                      ps[u][0:DC, 2, :], ACT.Copy, scale=scale).then_inc(k_h, 1)

                channels("a", 0, 2)
                high_parts("a", SCALE_A)
                for u in range(2):
                    ac.wait_ge(v_ps, ab["a"][u])
                    ac.copy(v_s[u][0:HALF, 0:2, :, 0:HD],
                            ps[u][0:HALF, 3, 0:2 * D].rearrange("p (t h d) -> p t h d", t=2, h=HEADS))
                    ac.copy(v_s[u][0:OUT, 2, :, 0:HD],
                            ps[u][0:OUT, 0, 0:D].rearrange("p (h d) -> p h d", h=HEADS)).then_inc(v_sb, 1)
                for half in range(2):
                    for u in range(2):
                        ac.wait_ge(ry_ps[half], n[u])
                        if half == 0:
                            ac.wait_ge(k_out[u], k_sent["a"])
                        for b in range(2):
                            y = 8 * half + 4 * b
                            ins = ac.copy(
                                yx(rel_sum[u])[:, :, y:y + 4, :].rearrange("p g y x -> p y g x"),
                                ps[u][:, 2 * half + b, 0:384].rearrange("p (y g x) -> p y g x", y=4, g=PAIRS))
                        ins.then_inc(ry_sb[half], 1)
                for u in range(2):
                    ac.wait_ge(rel_done, n[u])
                    for dst, src in zip(win_order(q_heads[u][0:SLOT, 0:HEADS:2, :]),
                                        window_pieces(yx(rel_sum[u][0:SLOT]))):
                        ins = ac.copy(dst, src)
                    ins.then_inc(q_even, 1)
                for u in range(2):
                    ac.wait_ge(mt_ps, ab["a"][u])
                    ac.copy(neg_max_t[u][:, :], ps[u][0:HEADS, 0, 0:TOK]).then_inc(mt_sb, 1)
                for p in range(PAIRS):
                    for u in range(2):
                        if p == 0:
                            ac.wait_ge(q_done, n[u])
                        ac.wait_ge(sc_ps[p], ab["a"][u])
                        ac.activation(probs[u][0:HALF, p % 4, :, 0:2 * WIN], ps[u][0:HALF, 0:2, 0:2 * WIN],
                                      ACT.Exp)
                        ac.activation(probs[u][:, p % 4, :, 2 * WIN:512], ps[u][:, 0:2, 2 * WIN:512],
                                      ACT.Exp).then_inc(pr_sb[p], 1)
                channels("m", 4, 6)
                for u in range(2):
                    ac.wait_ge(f1_ps, n[u])
                    for f in range(FT):
                        ins = ac.activation(hid[u][:, f, :],
                                            ps[u][:, 1 + f // 2, (f % 2) * TOK:(f % 2 + 1) * TOK],
                                            ACT.Gelu, bias=b_fc1[:, f:f + 1])
                    ins.then_inc(hid_sb, 1)
                channels("b", None, None)
                high_parts("b", SCALE_B)
                for u in range(2):
                    ac.wait_ge(v_ps, ab["b"][u])
                    ac.copy(v_s[u][:, 0:2, :, 0:HD],
                            ps[u][:, 3, 0:2 * D].rearrange("p (t h d) -> p t h d", t=2, h=HEADS)
                            ).then_inc(v_sb, 1)
                for u in range(2):
                    ac.wait_ge(mt_ps, ab["b"][u])
                    ac.copy(neg_max_t[u][:, :], ps[u][0:HEADS, 0, 0:TOK]).then_inc(mt_sb, 1)
                for p in range(PAIRS):
                    for u in range(2):
                        ac.wait_ge(sc_ps[p], ab["b"][u])
                        ac.activation(probs[u][:, p % 4, :, 0:384], ps[u][:, 0:2, 0:384],
                                      ACT.Exp).then_inc(pr_sb[p], 1)
                channels("g", None, None)

        @block.vector
        def _(dv):
            with dv.Fori(0, B // 2) as it:
                n, ab, ambg = numbers(dv, it), reached(dv, it), reached(dv, it, "ambg")
                c16 = dv.snap(it * 16 + 16)
                tile = [dv.snap(it * 4 + 2 * u) for u in range(2)]

                def norm(k, u, src):
                    for t in range(2):
                        ins = dv.bn_stats(stats[u][:, t, :], src[:, t * D:(t + 1) * D])
                    ins.then_inc(st, 1)
                    dv.wait_ge(st, ambg[k][u])
                    hold(dv)
                    for t in range(2):
                        ins = dv.bn_aggr(mean_var[u][:, t, :], stats[u][:, t, :])
                    ins.then_inc(ag, 1)
                    dv.wait_ge(rs, ambg[k][u])
                    if k == "a":
                        dv.wait_ge(xn_out[u], c16)
                    for t in range(2):
                        ins = dv.tensor_scalar(x_n[u][:, t, :], src[:, t * D:(t + 1) * D],
                                               mean_var[u][:, t, 0:1], rstd[u][:, t:t + 1],
                                               ALU.subtract, ALU.mult)
                    ins.then_inc(xn, 1)

                def low_parts(k, scale):
                    if k == "b":
                        for u in range(2):
                            dv.wait_ge(q_h, ab[k][u])
                            dv.tensor_tensor(staged[u][:, 4:6, :].rearrange("p g n -> p (g n)").bitcast(F32R),
                                             ps[u][0:DC, 1, :], staged[u][:, 0:2, :].rearrange("p g n -> p (g n)"),
                                             ALU.subtract).then_inc(q_l, 1)
                    for u in range(2):
                        dv.wait_ge(k_h, ab[k][u])
                        dv.scalar_tensor_tensor(
                            out=staged[u][:, 6:8, :].rearrange("p g n -> p (g n)").bitcast(F32R),
                            in0=ps[u][0:DC, 2, :], scalar=scale,
                            in1=staged[u][:, 2:4, :].rearrange("p g n -> p (g n)"),
                            op0=ALU.mult, op1=ALU.subtract).then_inc(k_l, 1)

                def normalise(k):
                    for g in range(GROUPS):
                        bank = 2 + g % 2
                        for u in range(2):
                            dv.wait_ge(av_ps[g], ab[k][u])
                            if g:
                                dv.wait_ge(ot_sb[g - 1], ab[k][u])
                            hold(dv)
                            dv.stream_shuffle(den[u][:, :], ps[u][:, bank, 0:TOK], [HD] * 32).then_inc(dn_sb[g], 1)
                            dv.wait_ge(dn_sb[g], ab[k][u])
                            dv.reciprocal(den[u][:, :], den[u][:, :]).then_inc(rc_sb[g], 1)
                            dv.wait_ge(rc_sb[g], ab[k][u])
                            if k == "a":
                                for dst, src, d in zip(window_pieces(yx(o_t[u][:, g:g + 1, :])),
                                                       win_order(ps[u][:, bank:bank + 1, 0:TOK]),
                                                       win_order(den[u][:, :].unsqueeze(1))):
                                    ins = dv.tensor_tensor(dst[:, 0], src[:, 0], d[:, 0], ALU.mult)
                            else:
                                ins = dv.tensor_tensor(o_t[u][:, g, :], ps[u][:, bank, 0:TOK], den[u][:, :],
                                                       ALU.mult)
                            ins.then_inc(ot_sb[g], 1)

                for u in range(2):
                    dv.wait_ge(x_loaded[u], c16)
                    norm("a", u, x_in[u][:, :, :].rearrange("p t d -> p (t d)"))
                low_parts("a", SCALE_A)
                for half in range(2):
                    for u in range(2):
                        dv.wait_ge(ry_sb[0], n[u])
                        dv.wait_ge(ry_sb[1], n[u])
                        dv.wait_ge(rx_ps[half], n[u])
                        for b in range(2):
                            x = 8 * half + 4 * b
                            part = yx(rel_sum[u])[:, :, :, x:x + 4].rearrange("p g y x -> p x g y")
                            ins = dv.tensor_tensor(
                                part, ps[u][:, 2 * half + b, 0:384].rearrange("p (x g y) -> p x g y", x=4, g=PAIRS),
                                part, ALU.add)
                        if half:
                            ins.then_inc(rel_done, 1)
                for u in range(2):
                    dv.wait_ge(rel_done, n[u])
                    even, odd = slice(0, SLOT), slice(SLOT, P)
                    for dst, src in zip(win_order(q_heads[u][odd, 1:HEADS:2, :]), window_pieces(yx(rel_sum[u][odd]))):
                        ins = dv.tensor_copy(dst, src)
                    ins.then_inc(q_odd, 1)
                    for ready, rows, to, first in ((q_odd, odd, even, 1), (q_even, even, odd, 0)):
                        dv.wait_ge(ready, n[u])
                        for dst, src, hi in zip(win_order(q_heads[u][to, first:HEADS:2, :]),
                                                window_pieces(yx(rel_sum[u][rows])),
                                                win_order(q_heads[u][rows, first:HEADS:2, :].bitcast(F32))):
                            ins = dv.tensor_tensor(dst, src, hi, ALU.subtract)
                    ins.then_inc(q_done, 1)
                for p in range(PAIRS):
                    for u in range(2):
                        dv.wait_ge(m_ps[p], ab["a"][u])
                        dv.tensor_reduce(neg_max[u][0:HALF, 0:2, 2 * p:2 * p + 2].rearrange("p q e -> p e q"),
                                         ps[u][0:HALF, 0:2, 0:2 * WIN].rearrange("p e (q k) -> p e q k", q=2),
                                         AX.X, ALU.max, negate=True)
                        dv.tensor_reduce(neg_max[u][0:OUT, 2, 2 * p:2 * p + 2], ps[u][0:OUT, 2:4, 0:TOK],
                                         AX.X, ALU.max, negate=True).then_inc(m_sb[p], 1)
                normalise("a")
                for u in range(2):
                    dv.wait_ge(o_ps, ab["a"][u])
                    dv.wait_ge(t2_out[u], c16)
                    dv.tensor_tensor(x_2[u][:, :], ps[u][:, 0, 0:2 * D],
                                     x_in[u][:, :, :].rearrange("p t d -> p (t d)"), ALU.add).then_inc(res, 1)
                    dv.wait_ge(res, ab["a"][u])
                    norm("m", u, x_2[u])
                for u in range(2):
                    dv.wait_ge(f2_ps, n[u])
                    dv.wait_ge(x2b_done, n[u])
                    dv.tensor_tensor(x_3[u][:, :], ps[u][:, 0, 0:2 * D], x_2b[u][:, :], ALU.add).then_inc(mlp_done, 1)
                    dv.wait_ge(mlp_done, n[u])
                    norm("b", u, x_3[u])
                low_parts("b", SCALE_B)
                for p in range(PAIRS):
                    bank = 2 * (p % 2)
                    for u in range(2):
                        dv.wait_ge(m_ps[p], ab["b"][u])
                        dv.tensor_reduce(neg_max[u][:, 0, 2 * p:2 * p + 2], ps[u][:, bank:bank + 2, 0:P],
                                         AX.X, ALU.max, negate=True)
                        dv.tensor_reduce(neg_max[u][:, 1, 2 * p:2 * p + 2], ps[u][:, bank:bank + 2, P:3 * P],
                                         AX.X, ALU.max, negate=True).then_inc(m_sb[p], 1)
                normalise("b")
                for u in range(2):
                    dv.wait_ge(o_ps, ab["b"][u])
                    dv.tensor_tensor(x_2[u][:, :], ps[u][:, 0, 0:2 * D], x_3[u][:, :], ALU.add).then_inc(res, 1)
                    dv.wait_ge(res, ab["b"][u])
                    norm("g", u, x_2[u])
                for u in range(2):
                    dv.wait_ge(lg_ps, n[u])
                    dv.tensor_copy(logits[:, bass.ds(tile[u], 2), :],
                                   ps[u][:, 1, 0:2 * NE].rearrange("p (t e) -> p t e", t=2)).then_inc(lg_sb, 1)

        @block.tensor
        def _(pe):
            with pe.Fori(0, B // 2) as it:
                n, ab, ambg = numbers(pe, it), reached(pe, it), reached(pe, it, "ambg")
                one, two_in = transfers(pe, it, 1), transfers(pe, it, 2)
                clears = [pe.snap(it * 4 + 2 * u + 2) for u in range(2)]

                def transpose_norm(k):
                    for u in range(2):
                        pe.wait_ge(xn, ambg[k][u])
                        for t in range(2):
                            for c in range(2):
                                ins = pe.transpose(ps[u][0:DC, 0, c * TOK + t * P:c * TOK + (t + 1) * P],
                                                   x_n[u][:, t, c * DC:(c + 1) * DC], ident[:, :])
                        ins.then_inc(xt_ps, 1)

                def chunks(dst, w, cols, x, toks, ones):
                    pe.matmul(dst, w[0:DC + ones, 0, cols], x[0:DC + ones, 0, toks], start=True, stop=False)
                    return pe.matmul(dst, w[0:DC, 1, cols], x[0:DC, 1, toks], start=False, stop=True)

                def tokens(dst, x, toks, w, cols, ones):
                    pe.matmul(dst, x[0:DC + ones, 0, toks], w[0:DC + ones, 0, cols], start=True, stop=False)
                    return pe.matmul(dst, x[0:DC, 1, toks], w[0:DC, 1, cols], start=False, stop=True)

                def output(k, w):
                    for u in range(2):
                        for g in range(GROUPS):
                            pe.wait_ge(ot_sb[g], ab[k][u])
                        for t in range(2):
                            for g in range(GROUPS):
                                ins = pe.matmul(ps[u][:, 0, t * D:(t + 1) * D], o_t[u][:, g, t * P:(t + 1) * P],
                                                w[:, g, :], start=(g == 0), stop=(g == GROUPS - 1))
                        ins.then_inc(o_ps, 1)

                transpose_norm("a")
                for u in range(2):
                    pe.wait_ge(xt, ambg["a"][u])
                    for g in range(2):
                        ins = chunks(ps[u][0:DC, 1, g * TOK:(g + 1) * TOK], w_qkv_a, slice(g * DC, (g + 1) * DC),
                                     x_t[u], slice(0, TOK), 1)
                    ins.then_inc(q_ps, 1)
                for u in range(2):
                    pe.wait_ge(xtw, n[u])
                    for g in range(2):
                        ins = chunks(ps[u][0:DC, 2, g * TOK:(g + 1) * TOK], w_qkv_a,
                                     slice(D + g * DC, D + (g + 1) * DC), x_tw[u], slice(0, TOK), 1)
                    ins.then_inc(k_ps, 1)
                for u in range(2):
                    for t in range(2):
                        tokens(ps[u][0:HALF, 3, t * D:(t + 1) * D], x_tw[u], slice(t * HALF, (t + 1) * HALF),
                               w_qkv_a, slice(2 * D, 3 * D), 1)
                    tokens(ps[u][0:OUT, 0, 0:D], x_tw[u], slice(WIN, TOK), w_qkv_a,
                           slice(2 * D, 3 * D), 1).then_inc(v_ps, 1)

                def rel(u, bank, at, table, toks):
                    dst = ps[u][:, bank, at * 96:(at + 1) * 96].rearrange("p (g x) -> p g x", g=PAIRS)
                    return pe.matmul(dst, rel_w[:, table, :], toks(s_q[u]), start=True, stop=True)

                for half in range(2):
                    for u in range(2):
                        pe.wait_ge(q_slots[u], two_in["a"])
                        pe.wait_ge(v_sb, ab["a"][u])
                        pe.wait_ge(k_l, ab["a"][u])
                        for y in range(8 * half, 8 * half + 8):
                            ins = rel(u, y // 4, y % 4, y % WS, lambda s: s[:, :, y * S:(y + 1) * S])
                        ins.then_inc(ry_ps[half], 1)
                for half in range(2):
                    for u in range(2):
                        pe.wait_ge(ry_sb[half], n[u])
                        for x in range(8 * half, 8 * half + 8):
                            ins = rel(u, x // 4, x % 4, WS + x % WS, lambda s: s[:, :, x:TOK:S])
                        ins.then_inc(rx_ps[half], 1)
                for p in range(PAIRS):
                    for u in range(2):
                        if p == 0:
                            pe.wait_ge(q_done, n[u])
                            pe.wait_ge(k_slots[u], two_in["a"])
                        else:
                            pe.wait_ge(m_sb[p - 1], ab["a"][u])
                        for e in range(2):
                            h = 2 * p + e
                            for q in range(2):
                                pe.matmul(ps[u][0:HALF, e, q * WIN:(q + 1) * WIN],
                                          q_heads[u][:, h, q * HALF:(q + 1) * HALF], k_s[u][:, h, 0:WIN],
                                          start=True, stop=True)
                            ins = pe.matmul(ps[u][0:WIDE, 2 + e, 0:TOK],
                                            q_s[u][:, h * TOK + WIN:h * TOK + WIN + WIDE],
                                            k_s[u][:, h, WIN:KEYS], start=True, stop=True)
                        ins.then_inc(m_ps[p], 1)
                for u in range(2):
                    pe.wait_ge(m_sb[PAIRS - 1], ab["a"][u])
                    for t, (rows, at) in enumerate(((HALF, 0), (HALF, HALF), (OUT, WIN))):
                        ins = pe.transpose(ps[u][0:HEADS, 0, at:at + rows], neg_max[u][0:rows, t, :],
                                           ident[0:rows, 0:rows])
                    ins.then_inc(mt_ps, 1)

                def scores_a(p, u):
                    for e in range(2):
                        h = 2 * p + e
                        for k in range(2):
                            pe.matmul(ps[u][0:HALF, e, k * WIN:(k + 1) * WIN],
                                      k_s[u][:, h, k * HALF:(k + 1) * HALF], q_heads[u][:, h, 0:WIN],
                                      start=True, stop=True)
                        for k in range(2):
                            ins = pe.matmul(ps[u][:, e, 2 * WIN + k * OUT:2 * WIN + (k + 1) * OUT],
                                            k_s[u][:, h, WIN + k * P:WIN + (k + 1) * P], q_heads[u][:, h, WIN:TOK],
                                            start=True, stop=True)
                    ins.then_inc(sc_ps[p], 1)

                def values_a(g, u):
                    pe.wait_ge(pr_sb[2 * g + 1], ab["a"][u])
                    for k in range(2):
                        for i in range(4):
                            h = 4 * g + i
                            pe.matmul(ps[u][32 * i:32 * i + 32, 2 + g % 2, 0:WIN], v_s[u][0:HALF, k, h, :],
                                      probs[u][0:HALF, h // 2 % 4, h % 2, k * WIN:(k + 1) * WIN],
                                      start=(k == 0), stop=(k == 1))
                    for k in range(2):
                        for i in range(4):
                            h = 4 * g + i
                            ins = pe.matmul(ps[u][32 * i:32 * i + 32, 2 + g % 2, WIN:TOK], v_s[u][:, 2 + k, h, :],
                                            probs[u][:, h // 2 % 4, h % 2, 2 * WIN + k * OUT:2 * WIN + (k + 1) * OUT],
                                            start=(k == 0), stop=(k == 1))
                    ins.then_inc(av_ps[g], 1)

                def attend(k, scores, values):
                    for p in range(PAIRS + 2):
                        for u in range(2):
                            if p < PAIRS:
                                if p:
                                    pe.wait_ge(pr_sb[p - 1], ab[k][u])
                                scores(p, u)
                            if p >= 2 and u == 0:
                                g, image = p // 2 - 1, p % 2
                                if g == 2:
                                    pe.wait_ge(ot_sb[0], ab[k][image])
                                values(g, image)

                for u in range(2):
                    pe.wait_ge(max_row[u], one["a"])
                attend("a", scores_a, values_a)
                output("a", w_out_a)

                transpose_norm("m")
                for u in range(2):
                    pe.wait_ge(xt, ambg["m"][u])
                    for f in range(FT):
                        ins = chunks(ps[u][:, 1 + f // 2, (f % 2) * TOK:(f % 2 + 1) * TOK], w_fc1,
                                     slice(f * P, (f + 1) * P), x_t[u], slice(0, TOK), 0)
                    ins.then_inc(f1_ps, 1)
                for u in range(2):
                    pe.wait_ge(hid_sb, n[u])
                    for t in range(2):
                        for f in range(FT):
                            ins = pe.matmul(ps[u][:, 0, t * D:(t + 1) * D], hid[u][:, f, t * P:(t + 1) * P],
                                            w_fc2[:, f, :], start=(f == 0), stop=(f == FT - 1))
                    ins.then_inc(f2_ps, 1)

                transpose_norm("b")
                for u in range(2):
                    pe.wait_ge(xt, ambg["b"][u])
                    for part, done in ((0, q_ps), (1, k_ps)):
                        for g in range(2):
                            at = part * D + g * DC
                            ins = chunks(ps[u][0:DC, 1 + part, g * TOK:(g + 1) * TOK], w_qkv_b,
                                         slice(at, at + DC), x_t[u], slice(0, TOK), 0)
                        ins.then_inc(done, 1)
                    for t in range(2):
                        ins = tokens(ps[u][:, 3, t * D:(t + 1) * D], x_t[u], slice(t * P, (t + 1) * P),
                                     w_qkv_b, slice(2 * D, 3 * D), 0)
                    ins.then_inc(v_ps, 1)

                def masked(u, bank, mask):
                    pe.matmul(ps[u][:, bank, 0:512].rearrange("p (a k) -> p a k", a=2)[:, :, 0:P], ident16[:, :],
                              mask[:, :, :], start=True, stop=False, skip_group_check=True)

                for p in range(PAIRS):
                    for u in range(2):
                        if p == 0:
                            pe.wait_ge(q_slots[u], two_in["b"])
                            pe.wait_ge(k_slots[u], two_in["b"])
                            pe.wait_ge(cleared, clears[u])
                            pe.wait_ge(v_sb, ab["b"][u])
                            pe.wait_ge(k_l, ab["b"][u])
                        if p >= 2:
                            pe.wait_ge(m_sb[p - 2], ab["b"][u])
                        for e in range(2):
                            bank = 2 * (p % 2) + e
                            h = 2 * p + e
                            masked(u, bank, mask_q)
                            pe.matmul(ps[u][:, bank, 0:P], q_heads[u][:, h, 0:P], k_s[u][:, h, 0:P],
                                      start=False, stop=True, skip_group_check=True)
                            ins = pe.matmul(ps[u][:, bank, P:3 * P], q_heads[u][:, h, P:2 * P],
                                            k_s[u][:, h, 0:2 * P], start=False, stop=True,
                                            skip_group_check=True)
                        ins.then_inc(m_ps[p], 1)
                for u in range(2):
                    pe.wait_ge(m_sb[PAIRS - 1], ab["b"][u])
                    for t in range(2):
                        ins = pe.transpose(ps[u][0:HEADS, 0, t * P:(t + 1) * P], neg_max[u][:, t, :], ident[:, :])
                    ins.then_inc(mt_ps, 1)

                def scores_b(p, u):
                    for e in range(2):
                        h = 2 * p + e
                        masked(u, e, mask_k)
                        for k in range(2):
                            ins = pe.matmul(ps[u][:, e, k * TOK:TOK + k * P], k_s[u][:, h, k * P:(k + 1) * P],
                                            q_heads[u][:, h, k * P:TOK], start=False, stop=True,
                                            skip_group_check=True)
                    ins.then_inc(sc_ps[p], 1)

                def values_b(g, u):
                    pe.wait_ge(pr_sb[2 * g + 1], ab["b"][u])
                    for k in range(2):
                        for i in range(4):
                            h = 4 * g + i
                            ins = pe.matmul(ps[u][32 * i:32 * i + 32, 2 + g % 2, k * P:TOK], v_s[u][:, k, h, :],
                                            probs[u][:, h // 2 % 4, h % 2, k * TOK:k * TOK + TOK - k * P],
                                            start=(k == 0), stop=True, skip_group_check=(k == 1))
                    ins.then_inc(av_ps[g], 1)

                for u in range(2):
                    pe.wait_ge(max_row[u], one["b"])
                attend("b", scores_b, values_b)
                output("b", w_out_b)

                transpose_norm("g")
                for u in range(2):
                    pe.wait_ge(xt, ambg["g"][u])
                    for t in range(2):
                        ins = tokens(ps[u][:, 1, t * NE:(t + 1) * NE], x_t[u], slice(t * P, (t + 1) * P), w_gate,
                                     slice(0, NE), 1)
                    ins.then_inc(lg_ps, 1)


def expert_phase(nc, a, t2_dram, xn_dram, xs_dram, ys_dram, logits, ident, ps, sem, out):
    with ExitStack() as ctx:
        def sb(name, shape, dt=F32):
            return ctx.enter_context(nc.sbuf_tensor(name, shape, dt))

        def two(name, shape, dt=F32):
            return [sb(f"{name}{u}", shape, dt) for u in range(2)]

        def sems(name, n=2):
            return [sem(f"{name}{i}") for i in range(n)]

        w1 = sb("w1", [DC + 1, NE, 2, MLP])
        w2 = sb("w2", [P, NE, FT, D])
        b2 = sb("b2", [1, NE, D])
        xn_all = sb("xn_all", [P, NT, D])
        t2_all = sb("t2_all", [P, NT, D])
        y_sel = sb("y_sel", [P, 2, NT, D])
        before = sb("before", [P, P])
        ones = sb("ones", [P, P])
        numbers = sb("numbers", [P, NTILE])
        starts = sb("starts", [P, NT])

        top = sb("top", [P, NT, 8])
        top_at = sb("top_at", [P, NT, 8], U32)
        row = sb("row", [P, NT])
        row2 = sb("row2", [P, NT])
        gates = sb("gates", [P, NT, NE])
        chosen = sb("chosen", [P, NT, 2])
        hot = sb("hot", [P, 2, NT, NE])
        both = sb("both", [P, NT, NE])
        counts = sb("counts", [P, 2, NT * NE])
        seen = sb("seen", [P, NT + 1, NE])
        full = sb("full", [P, NE, NT])
        tiles_of = sb("tiles_of", [P, NE])
        first = sb("first", [P, NE + 1])
        place = sb("place", [P, NT, NE])
        place_s = sb("place_s", [P, NT, NE])
        pos_f = sb("pos_f", [P, 2, NT])
        pos = sb("pos", [P, 2 * NT], U32)
        weight = sb("weight", [P, 2, NT])
        past = sb("past", [P, NTILE, NE - 1])
        expert_f = sb("expert_f", [P, NTILE])
        expert = sb("expert", [P, NTILE], I32)

        rows_in = two("rows_in", [P, D])
        rows_t = two("rows_t", [DC + 1, 2, P])
        hid = two("hid_e", [P, MLP])
        hid_t = two("hid_t", [P, FT, P])
        y_out = two("y_out", [P, D])

        gathered = sems("gathered", NT // 4)
        c_in, w_loaded, xn_loaded, t2_loaded, pool_c, exp_in, exp_out, choice, counted, routed, experts_known = (
            sem(n) for n in ("c_in", "w_loaded", "xn_loaded", "t2_loaded", "pool_c", "exp_in", "exp_out", "choice",
                             "counted", "routed", "experts_known"))
        dve_c, scattered, mixed, stored = (sem(n) for n in ("dve_c", "scattered", "mixed", "stored"))
        in_loaded, in_ps, in_t, h_ps, h_sb, ht_ps, ht_sb, y_ps, y_sb, y_stored = (sems(n) for n in (
            "in_loaded", "in_ps", "in_t", "h_ps", "h_sb", "ht_ps", "ht_sb", "y_ps", "y_sb", "y_stored"))
        STEPS = NTILE // 2
        HM = MLP // 2

        block = ctx.enter_context(nc.Block("experts"))

        @block.sync
        def _(sp):
            for dst, name in ((before[:, :], "before"), (starts[:, :], "starts"), (numbers[:, :], "numbers")):
                sp.dma_start(dst, a[name]).then_inc(c_in, 16)
            sp.dma_start(xn_all[:, :, :], xn_dram.rearrange("t p d -> p t d")).then_inc(xn_loaded, 16)
            for e in range(NE):
                sp.dma_start(w1[:, e], a["e_w1"][:, e]).then_inc(w_loaded, 16)
                sp.dma_start(w2[:, e], a["e_w2"][:, e]).then_inc(w_loaded, 16)
            sp.dma_start(b2[:, :, :], a["e_b2"]).then_inc(w_loaded, 16)
            sp.dma_start(t2_all[:, :, :], t2_dram.rearrange("t p d -> p t d")).then_inc(t2_loaded, 16)
            sorted_rows = xs_dram.rearrange("(t p) d -> t p d", p=P)
            result = ys_dram.rearrange("(t p) d -> t p d", p=P)
            sp.wait_ge(scattered, 16 * 2 * NT)
            for u in range(2):
                sp.dma_start(rows_in[u][:, :], sorted_rows[u]).then_inc(in_loaded[u], 16)
                sp.sem_inc(y_stored[u], 16)
            with sp.Fori(0, STEPS) as it:
                done = sp.snap(it + 1)
                tile = [sp.snap(it * 2 + u) for u in range(2)]
                nxt = [sp.snap((it * 2 + 2 + u) % NTILE) for u in range(2)]
                for u in range(2):
                    sp.wait_ge(in_ps[u], done)
                    sp.dma_start(rows_in[u][:, :], sorted_rows[nxt[u]]).then_inc(in_loaded[u], 16)
                for u in range(2):
                    sp.wait_ge(y_sb[u], done)
                    sp.dma_start(result[tile[u]], y_out[u][:, :]).then_inc(y_stored[u], 16)
            for u in range(2):
                sp.wait_ge(in_loaded[u], 16 * (STEPS + 1))
            for t in range(NT):
                sp.wait_ge(mixed, t + 1)
                sp.dma_start(out[t], t2_all[:, t, :]).then_inc(stored, 16)
            sp.wait_ge(stored, 16 * NT)

        @block.gpsimd
        def _(gp):
            gp.memset(ones[:, :], 1.0)
            for u in range(2):
                ins = gp.memset(rows_t[u][:, :, :], 1.0)
            ins.then_inc(pool_c, 1)
            gp.wait_ge(routed, 1)
            gp.wait_ge(xn_loaded, 16)
            for t in range(NT):
                for s in range(2):
                    gp.indirect_dma_start(
                        out=xs_dram, out_offset=bass.IndirectOffsetOnAxis(ap=pos[:, s * NT + t:s * NT + t + 1], axis=0),
                        in_=xn_all[:, t, :], in_offset=None).then_inc(scattered, 16)
            for u in range(2):
                gp.wait_ge(y_stored[u], 16 * (STEPS + 1))
            for t in range(NT):
                for s in range(2):
                    gp.indirect_dma_start(
                        out=y_sel[:, s, t, :], out_offset=None, in_=ys_dram,
                        in_offset=bass.IndirectOffsetOnAxis(ap=pos[:, s * NT + t:s * NT + t + 1], axis=0)
                        ).then_inc(gathered[t // 4], 16)

        @block.scalar
        def _(ac):
            ac.wait_ge(exp_in, 1)
            ac.activation(gates[:, :, :], place[:, :, :], ACT.Exp).then_inc(exp_out, 1)
            with ac.Fori(0, STEPS) as it:
                done = ac.snap(it + 1)
                for u in range(2):
                    ac.wait_ge(h_ps[u], done)
                    for i in range(2):
                        ins = ac.activation(hid[u][:, i * HM:(i + 1) * HM], ps[u][:, 1 + i, 0:HM], ACT.Gelu)
                    ins.then_inc(h_sb[u], 1)
                for u in range(2):
                    ac.wait_ge(ht_ps[u], done)
                    ac.copy(hid_t[u][:, 3:6, :], ps[u][:, 2, 0:HM].rearrange("p (f n) -> p f n", f=3)
                            ).then_inc(ht_sb[u], 1)

        @block.vector
        def _(dv):
            count = [0]

            def step(ins):
                count[0] += 1
                ins.then_inc(dve_c, 1)
                dv.wait_ge(dve_c, count[0])

            def over(x, shape, axis):
                return x.unsqueeze(axis).to_broadcast(shape)

            TE = [P, NT, NE]
            dv.wait_ge(c_in, 48)
            step(dv.tensor_reduce(row[:, :], logits[:, :, :], AX.X, ALU.max))
            dv.tensor_tensor(place[:, :, :], logits[:, :, :], over(row[:, :], TE, 2), ALU.subtract).then_inc(exp_in, 1)
            dv.wait_ge(exp_out, 1)
            step(dv.tensor_reduce(row[:, :], gates[:, :, :], AX.X, ALU.add))
            step(dv.reciprocal(row[:, :], row[:, :]))
            step(dv.tensor_tensor(gates[:, :, :], gates[:, :, :], over(row[:, :], TE, 2), ALU.mult))
            for t in range(NT):
                ins = dv.max(top[:, t, :], gates[:, t, :])
            step(ins)
            for t in range(NT):
                ins = dv.max_index(top_at[:, t, :], top[:, t, :], gates[:, t, :])
            step(ins)
            step(dv.tensor_copy(chosen[:, :, :], top_at[:, :, 0:2]))
            for s in range(2):
                ins = dv.tensor_tensor(hot[:, s], numbers[:, 0:NE].unsqueeze(1).to_broadcast(TE),
                                       over(chosen[:, :, s], TE, 2), ALU.is_equal)
            step(ins)
            dv.tensor_tensor(both[:, :, :], hot[:, 0], hot[:, 1], ALU.add).then_inc(choice, 1)
            step(dv.tensor_tensor(row2[:, :], top[:, :, 0], top[:, :, 1], ALU.add))
            step(dv.tensor_scalar(row2[:, :], row2[:, :], 1e-9, None, ALU.add))
            step(dv.reciprocal(row2[:, :], row2[:, :]))
            for s in range(2):
                ins = dv.tensor_tensor(weight[:, s, :], top[:, :, s], row2[:, :], ALU.mult)
            step(ins)
            dv.wait_ge(counted, 1)
            step(dv.tensor_copy(counts[:, :, :], ps[0][:, 0:2, 0:NT * NE]))
            step(dv.memset(seen[:, 0, :], 0.0))
            total = counts[:, 1, :].rearrange("p (t e) -> p t e", e=NE)
            for t in range(NT):
                step(dv.tensor_tensor(seen[:, t + 1, :], seen[:, t, :], total[:, t, :], ALU.add))
            step(dv.tensor_tensor(full[:, :, :], over(seen[:, NT, :], [P, NE, NT], 2),
                                  starts[:, :].unsqueeze(1).to_broadcast([P, NE, NT]), ALU.is_gt))
            step(dv.tensor_reduce(tiles_of[:, :], full[:, :, :], AX.X, ALU.add))
            step(dv.memset(first[:, :], 0.0))
            for e in range(NE):
                step(dv.tensor_tensor(first[:, e + 1:e + 2], first[:, e:e + 1], tiles_of[:, e:e + 1], ALU.add))
            TL = [P, NTILE, NE - 1]
            step(dv.tensor_tensor(past[:, :, :], over(numbers[:, :], TL, 2),
                                  first[:, 1:NE].unsqueeze(1).to_broadcast(TL), ALU.is_ge))
            step(dv.tensor_reduce(expert_f[:, :], past[:, :, :], AX.X, ALU.add))
            dv.tensor_copy(expert[:, :], expert_f[:, :]).then_inc(experts_known, 1)
            step(dv.tensor_tensor(place[:, :, :], counts[:, 0, :].rearrange("p (t e) -> p t e", e=NE),
                                  seen[:, 0:NT, :], ALU.add))
            step(dv.scalar_tensor_tensor(out=place[:, :, :], in0=first[:, 0:NE].unsqueeze(1).to_broadcast(TE),
                                         scalar=float(P), in1=place[:, :, :], op0=ALU.mult, op1=ALU.add))
            for s in range(2):
                step(dv.tensor_tensor(place_s[:, :, :], place[:, :, :], hot[:, s], ALU.mult))
                step(dv.tensor_reduce(pos_f[:, s, :], place_s[:, :, :], AX.X, ALU.add))
            dv.tensor_copy(pos[:, :], pos_f[:, :, :].rearrange("p s t -> p (s t)")).then_inc(routed, 1)

            def rows_to_channels(u, reached):
                dv.wait_ge(in_ps[u], reached)
                dv.tensor_copy(rows_t[u][0:DC, :, :], ps[u][0:DC, 0, 0:2 * P].rearrange("p (c n) -> p c n", c=2)
                               ).then_inc(in_t[u], 1)

            dv.wait_ge(pool_c, 1)
            for u in range(2):
                rows_to_channels(u, 1)
            with dv.Fori(0, STEPS) as it:
                done, two_done, stored_before = dv.snap(it + 1), dv.snap(it + 2), dv.snap(it * 16 + 16)
                for u in range(2):
                    dv.wait_ge(ht_ps[u], done)
                    dv.tensor_copy(hid_t[u][:, 0:3, :], ps[u][:, 1, 0:HM].rearrange("p (f n) -> p f n", f=3)
                                   ).then_inc(ht_sb[u], 1)
                for u in range(2):
                    rows_to_channels(u, two_done)
                for u in range(2):
                    dv.wait_ge(y_ps[u], done)
                    dv.wait_ge(y_stored[u], stored_before)
                    dv.tensor_copy(y_out[u][:, :], ps[u][:, 3, 0:D]).then_inc(y_sb[u], 1)
            dv.wait_ge(t2_loaded, 16)
            for t in range(NT):
                dv.wait_ge(gathered[t // 4], 16 * 8)
                step(dv.scalar_tensor_tensor(out=t2_all[:, t, :], in0=y_sel[:, 0, t, :], scalar=weight[:, 0, t:t + 1],
                                             in1=t2_all[:, t, :], op0=ALU.mult, op1=ALU.add))
                dv.scalar_tensor_tensor(out=t2_all[:, t, :], in0=y_sel[:, 1, t, :], scalar=weight[:, 1, t:t + 1],
                                        in1=t2_all[:, t, :], op0=ALU.mult, op1=ALU.add).then_inc(mixed, 1)

        @block.tensor
        def _(pe):
            pe.wait_ge(pool_c, 1)
            pe.wait_ge(c_in, 48)
            pe.wait_ge(choice, 1)
            pairs = both[:, :, :].rearrange("p t e -> p (t e)")
            pe.matmul(ps[0][:, 0, 0:NT * NE], before[:, :], pairs, start=True, stop=True)
            pe.matmul(ps[0][:, 1, 0:NT * NE], ones[:, :], pairs, start=True, stop=True).then_inc(counted, 1)
            pe.wait_ge(routed, 1)
            pe.wait_ge(w_loaded, 16 * (2 * NE + 1))
            pe.wait_ge(experts_known, 1)

            def transpose_rows(u, reached):
                pe.wait_ge(in_loaded[u], reached)
                for c in range(2):
                    ins = pe.transpose(ps[u][0:DC, 0, c * P:(c + 1) * P], rows_in[u][:, c * DC:(c + 1) * DC],
                                       ident[:, :])
                ins.then_inc(in_ps[u], 1)

            for u in range(2):
                transpose_rows(u, 16)
            with pe.Fori(0, STEPS) as it:
                done, loaded = pe.snap(it + 1), pe.snap(it * 16 + 32)
                two_done = pe.snap(it * 2 + 2)
                e = [pe.value_load(expert[0:1, bass.ds(it * 2 + u, 1)], min_val=0, max_val=NE - 1) for u in range(2)]
                for u in range(2):
                    pe.wait_ge(in_t[u], done)
                    for i in range(2):
                        cols = slice(i * HM, (i + 1) * HM)
                        pe.matmul(ps[u][:, 1 + i, 0:HM], rows_t[u][:, 0, :], w1[:, bass.ds(e[u], 1), 0, cols],
                                  start=True, stop=False)
                        ins = pe.matmul(ps[u][:, 1 + i, 0:HM], rows_t[u][0:DC, 1, :],
                                        w1[0:DC, bass.ds(e[u], 1), 1, cols], start=False, stop=True)
                    ins.then_inc(h_ps[u], 1)
                for u in range(2):
                    pe.wait_ge(h_sb[u], done)
                    for f in range(FT):
                        ins = pe.transpose(ps[u][:, 1 + f // 3, (f % 3) * P:(f % 3 + 1) * P],
                                           hid[u][:, f * P:(f + 1) * P], ident[:, :])
                    ins.then_inc(ht_ps[u], 1)
                for u in range(2):
                    transpose_rows(u, loaded)
                for u in range(2):
                    pe.wait_ge(ht_sb[u], two_done)
                    for f in range(FT):
                        pe.matmul(ps[u][:, 3, 0:D], hid_t[u][:, f, :], w2[:, bass.ds(e[u], 1), f, :],
                                  start=(f == 0), stop=False)
                    pe.matmul(ps[u][:, 3, 0:D], ones[0:1, :], b2[:, bass.ds(e[u], 1), :],
                              start=False, stop=True).then_inc(y_ps[u], 1)


def _layouts(i):
    f = np.float32

    def rows(w, bias=None):
        out = np.zeros((DC + (bias is not None), 2, w.shape[1]), f)
        out[:DC, 0], out[:DC, 1] = w[:DC], w[DC:]
        if bias is not None:
            out[DC, 0] = bias
        return out

    def head_rows(w, bias):
        out = np.zeros((P, GROUPS, w.shape[1]), f)
        for h in range(HEADS):
            r = 32 * (h % 4)
            out[r:r + HD, h // 4] = w[h * HD:(h + 1) * HD]
        out[HD, 0] = bias
        return out

    tables = np.zeros((P, 2 * WS, P), f)
    for e in range(2):
        s = SLOT * e
        for at in range(WS):
            for c in range(HD):
                tables[s + c, at, s + 2 * c:s + 2 * c + 2] = 1.0
            for r in range(MAXROW + 1, SLOT):
                tables[s + r, at, s + r] = 1.0
            for key in range(WS):
                tables[s:s + HD, at, s + REL + key] = i["L0_conv_rel_pos_h"][at - key + WS - 1]
                tables[s:s + HD, WS + at, s + REL + WS + key] = i["L0_conv_rel_pos_w"][at - key + WS - 1]
    slot_rows = np.zeros((P, KEYS), f)
    slot_rows_q = np.zeros((P, TOK), f)
    for e in range(2):
        s = SLOT * e
        keys = [(y, x, -1) for y in range(WS) for x in range(WS)]
        keys += [(y, x - WS, 0) for y in range(WS) for x in range(WS, S)]
        keys += [(y - WS, x % WS, 1 + x // WS) for y in range(WS, S) for x in range(S)]
        keys += [(y, x, 3) for y in range(WS) for x in range(WS)]
        left = S - WS
        for n, (y, x, w) in enumerate(keys):
            slot_rows[s + REL + y, n] = 1.0
            slot_rows[s + REL + WS + x, n] = 1.0
            slot_rows[s + MAXROW, n] = 1.0
            if w >= 0:
                ok = (x >= left, y >= left, y >= left or x >= left) if w == 3 else (w == 0, w == 1, w == 2)
                for m in range(3):
                    slot_rows[s + MAXROW + 1 + m, n] = 0.0 if ok[m] else -BIG
        for y in range(S):
            for x in range(S):
                if y >= WS or x >= WS:
                    m = 0 if y < WS else 1 if x < WS else 2
                    slot_rows_q[s + MAXROW + 1 + m, y * S + x] = 1.0
    later = np.where(np.arange(P)[None, :] > np.arange(P)[:, None], f(-BIG), f(0))
    masks = np.stack([later, later, later.T, later.T], 1).reshape(P, 4 * P)
    qkv_b = i["L0_conv_qkv_b"]
    heads = [i[f"L1_attn_W_{n}"].transpose(1, 0, 2).reshape(D, D) for n in "qkv"]
    norms = np.zeros((DC, 8), f)
    for n, name in enumerate(("norm1_w", "norm1_b", "norm2_w", "norm2_b")):
        norms[:, 2 * n:2 * n + 2] = i[f"L0_conv_{name}"].reshape(2, DC).T
    e_w1 = np.zeros((DC + 1, NE, 2, MLP), f)
    e_w1[:DC] = i["L1_ffn_w1"].reshape(NE, 2, DC, MLP).transpose(2, 0, 1, 3)
    e_w1[DC, :, 0] = i["L1_ffn_b1"]
    return {
        "x": i["x"].reshape(B, 2, P, D).transpose(0, 2, 1, 3),
        "w_qkv_a": rows(i["L0_conv_qkv_w"], qkv_b),
        "w_qkv_b": rows(np.concatenate(heads, 1)),
        "w_out_a": head_rows(i["L0_conv_proj_w"], i["L0_conv_proj_b"]),
        "w_out_b": head_rows(i["L1_attn_lin_w"].T, i["L1_attn_lin_b"]),
        "w_fc1": rows(i["L0_conv_fc1_w"]),
        "w_fc2": i["L0_conv_fc2_w"].reshape(FT, P, D).transpose(1, 0, 2),
        "b_fc1": i["L0_conv_fc1_b"].reshape(FT, P).T,
        "b_fc2": np.tile(i["L0_conv_fc2_b"], (P, 2)),
        "norms": norms,
        "w_gate": rows(i["L1_ffn_gate_w"], i["L1_ffn_gate_b"]),
        "k_bias": qkv_b[D:2 * D].reshape(2, DC).T,
        "v_bias": np.tile(qkv_b[2 * D:], (P, 1)),
        "rel_tables": tables,
        "slot_rows": slot_rows,
        "slot_rows_q": slot_rows_q,
        "masks": masks,
        "ident": np.eye(P, dtype=f),
        "before": np.triu(np.ones((P, P), f), 1),
        "starts": np.tile(np.arange(NT, dtype=f) * P, (P, 1)),
        "numbers": np.tile(np.arange(NTILE, dtype=f), (P, 1)),
        "e_w1": e_w1,
        "e_w2": i["L1_ffn_w2"].reshape(NE, FT, P, D).transpose(2, 0, 1, 3),
        "e_b2": i["L1_ffn_b2"].reshape(1, NE, D),
    }


def kernel(**inputs):
    import concourse.bacc as bacc
    from concourse.bass_utils import run_bass_kernel_spmd

    nc = bacc.Bacc("TRN2", target_bir_lowering=False, num_devices=1)
    arrays, aps = {}, {}
    for name, value in _layouts({k: np.asarray(v) for k, v in inputs.items()}).items():
        value = np.ascontiguousarray(value)
        arrays[f"in_{name}"] = value
        aps[name] = nc.dram_tensor(f"in_{name}", value.shape, mybir.dt.from_np(value.dtype),
                                   kind="ExternalInput").ap()
    result = nc.dram_tensor("result", (NT, P, D), F32, kind="ExternalOutput").ap()
    build(nc, aps, result)
    run = run_bass_kernel_spmd(nc, [arrays], core_ids=[0])
    return run.results[0]["result"].reshape(B, S, S, D)
```

```python
from contextlib import ExitStack

import numpy as np

import concourse.bass as bass
from concourse import mybir

F32 = mybir.dt.float32
F32R = mybir.dt.float32r
BF16 = mybir.dt.bfloat16
U32 = mybir.dt.uint32
I32 = mybir.dt.int32
ALU = mybir.AluOpType
ACT = mybir.ActivationFunctionType
AX = mybir.AxisListType

P = 128
B, S, D = 8, 16, 192
TOK = S * S
NT = B * TOK // P
HEADS, HD, WS = 12, 16, 14
PAIRS, GROUPS = HEADS // 2, HEADS // 4
DC = D // 2
MLP = 4 * D
FT = MLP // P
NE = 8
WIN = WS * WS
HALF = WIN // 2
OUT = TOK - WIN
KEYS = TOK + WIN
EDGE = (S - WS) * WS
SLOT = 64
REL = 32
MAXROW = 60
WIDE = 66
BIG = 1.0e30
NTILE = 2 * B * TOK // P + NE
SCALE_A, SCALE_B = 0.25, 0.0625
EPS = 1e-5


def window_pieces(t):
    return t[..., 0:WS, 0:WS], t[..., 0:WS, WS:S], t[..., WS:S, 0:S]


def build(nc, a, out):
    q_scratch = nc.dram_tensor("q_scratch", (2, 2, 2, DC, 2, TOK), F32, kind="Internal").ap()
    k_scratch = nc.dram_tensor("k_scratch", (2, 2, DC, 2, TOK), F32, kind="Internal").ap()
    pad_scratch = nc.dram_tensor("pad_scratch", (2, DC, 2, WIN), F32, kind="Internal").ap()
    max_scratch = nc.dram_tensor("max_scratch", (2, HEADS, TOK), F32, kind="Internal").ap()
    t2_dram = nc.dram_tensor("t2_dram", (NT, P, D), F32, kind="Internal").ap()
    xn_dram = nc.dram_tensor("xn_dram", (NT, P, D), F32, kind="Internal").ap()
    xs_dram = nc.dram_tensor("sorted_dram", (NTILE * P, D), F32, kind="Internal").ap()
    ys_dram = nc.dram_tensor("expert_out_dram", (NTILE * P, D), F32, kind="Internal").ap()
    with ExitStack() as keep:
        logits = keep.enter_context(nc.sbuf_tensor("logits", [P, NT, NE], F32))
        ident = keep.enter_context(nc.sbuf_tensor("ident", [P, P], F32))
        ps = [keep.enter_context(nc.psum_tensor(f"ps{u}", [P, 4, 512], F32)) for u in range(2)]

        def sem(name):
            return keep.enter_context(nc.semaphore(name))

        attention_phase(nc, a, q_scratch, k_scratch, pad_scratch, max_scratch, t2_dram, xn_dram, xs_dram, logits, ident, ps, sem)
        expert_phase(nc, a, t2_dram, xn_dram, xs_dram, ys_dram, logits, ident, ps, sem, out)


def attention_phase(nc, a, q_scratch, k_scratch, pad_scratch, max_scratch, t2_dram, xn_dram, xs_dram, logits, ident, ps, sem):
    with ExitStack() as ctx:
        def sb(name, shape, dt=F32):
            return ctx.enter_context(nc.sbuf_tensor(name, shape, dt))

        def two(name, shape, dt=F32):
            return [sb(f"{name}{u}", shape, dt) for u in range(2)]

        def sems(name, n):
            return [sem(f"{name}{i}") for i in range(n)]

        w_qkv_a = sb("w_qkv_a", [DC + 1, 2, 3 * D])
        w_qkv_b = sb("w_qkv_b", [DC, 2, 3 * D])
        w_out_a = sb("w_out_a", [P, GROUPS, D])
        w_out_b = sb("w_out_b", [P, GROUPS, D])
        w_fc1 = sb("w_fc1", [DC, 2, MLP])
        w_fc2 = sb("w_fc2", [P, FT, D])
        b_fc1 = sb("b_fc1", [P, FT])
        b_fc2 = sb("b_fc2", [P, 2 * D])
        norms = sb("norms", [DC, 8])
        k_bias = sb("k_bias", [DC, 2])
        w_gate = sb("w_gate", [DC + 1, 2, NE])
        rel_w = sb("rel_w", [P, 2 * WS, P])
        mask_q = sb("mask_q", [P, 2, P], BF16)
        mask_k = sb("mask_k", [P, 2, P], BF16)
        ident16 = sb("ident16", [P, P], BF16)
        half_neg = sb("half_neg", [P, 2])
        eps = sb("eps", [P, 2])
        slot_rows = sb("slot_rows", [P, KEYS])
        v_bias = sb("v_bias", [P, D])

        ZEROS = NTILE * D // 16
        zero = sb("zero", [P, ZEROS])

        x_in = two("x_in", [P, 2, D])
        x_n = two("x_n", [P, 2, D])
        x_na = two("x_na", [P, 2, D])
        stats = two("stats", [P, 2, 6])
        mean_var = two("mean_var", [P, 2, 2])
        var_eps = two("var_eps", [P, 2])
        rstd = two("rstd", [P, 2])
        x_t = two("x_t", [DC + 1, 2, TOK])
        x_tw = two("x_tw", [DC + 1, 2, TOK])
        s_q = two("s_q", [P, PAIRS, TOK])
        work_all = sb("work", [P, 2, 4096])
        q_s = two("q_s", [P, HEADS * TOK + WIDE - OUT], F32R)
        k_s = two("k_s", [P, HEADS, KEYS], F32R)
        v_s = two("v_s", [P, 4, HEADS, 32])
        o_t = two("o_t", [P, GROUPS, TOK])
        x_2 = two("x_2", [P, 2 * D])
        x_2b = two("x_2b", [P, 2 * D])
        x_3 = two("x_3", [P, 2 * D])
        den = two("den", [P, TOK])
        neg_max = two("neg_max", [P, 3, HEADS])
        neg_max_t = two("neg_max_t", [HEADS, TOK])

        def yx(t):
            return t.rearrange("p c (y x) -> p c y x", x=S)

        def by_tile(t):
            return t[:, :].rearrange("p (t d) -> p t d", t=2)

        def win_order(t):
            return (t[:, :, 0:WIN].rearrange("p c (y x) -> p c y x", x=WS),
                    t[:, :, WIN:WIN + EDGE].rearrange("p c (y x) -> p c y x", x=S - WS),
                    t[:, :, WIN + EDGE:TOK].rearrange("p c (y x) -> p c y x", x=S))

        work = [work_all[:, u, :] for u in range(2)]
        rel_sum = [w[:, 0:PAIRS * TOK].rearrange("p (g n) -> p g n", g=PAIRS) for w in work]
        probs = [w.rearrange("p (r e n) -> p r e n", r=4, e=2) for w in work]
        hid = [w[:, 0:FT * TOK].rearrange("p (f n) -> p f n", f=FT) for w in work]
        staged = [w[0:DC, 0:8 * TOK].rearrange("p (c n) -> p c n", n=TOK) for w in work]
        q_heads = [t[:, 0:HEADS * TOK].rearrange("p (h n) -> p h n", n=TOK) for t in q_s]

        def slot_order(t):
            return t.rearrange("g (h c) s n -> (c s) (g h) n", c=HD)

        w_in, late_in, pool_c, dve_c, pad_out, pad_in, zero_out = (sem(f"set_{n}") for n in (
            "first_in", "late_in", "pool", "dve", "pad_out", "pad_in", "zeros"))
        x_loaded = sems("x_loaded", 2)
        mask_in = o_t[0][:, :, :].rearrange("p g n -> p (g n)")[:, 0:4 * P]
        loads = ((k_bias[:, :], "k_bias"), (slot_rows[:, :], "slot_rows"), (v_bias[:, :], "v_bias"),
                 (mask_in, "masks"), (ident[:, :], "ident"), (norms[:, :], "norms"),
                 (w_qkv_a[:, :, :], "w_qkv_a"))
        late_loads = ((rel_w[:, :, :], "rel_tables"), (w_out_a[:, :, :], "w_out_a"), (w_fc1[:, :, :], "w_fc1"),
                      (w_fc2[:, :, :], "w_fc2"), (b_fc1[:, :], "b_fc1"), (b_fc2[:, :], "b_fc2"),
                      (w_qkv_b[:, :, :], "w_qkv_b"), (w_out_b[:, :, :], "w_out_b"), (w_gate[:, :, :], "w_gate"))
        FIRST_IN = 16 * len(loads)
        LATE_IN = 16 * (len(late_loads) + 2)

        def key_rows(r):
            return slot_rows[r:r + SLOT - REL, :].unsqueeze(1).to_broadcast([SLOT - REL, HEADS, KEYS])

        with nc.Block("setup") as block:
            @block.sync
            def _(sp):
                for dst, name in loads:
                    sp.dma_start(dst, a[name]).then_inc(w_in, 16)
                for u in range(2):
                    sp.dma_start(x_in[u][:, :, :], a["x"][u]).then_inc(x_loaded[u], 16)
                sp.wait_ge(dve_c, 3)
                for part in range(2):
                    sp.dma_start(pad_scratch[:, :, part].rearrange("g r n -> r g n"),
                                 staged[1][:, 4 * part:4 * part + 2, 0:WIN]).then_inc(pad_out, 16)
                for u in range(2):
                    sp.dma_start(s_q[u][:, :, :], a["slot_rows_q"].unsqueeze(1).to_broadcast([P, PAIRS, TOK])
                                 ).then_inc(late_in, 16)
                for dst, name in late_loads:
                    sp.dma_start(dst, a[name]).then_inc(late_in, 16)
                sp.wait_ge(pad_out, 32)
                for u in range(2):
                    for r in (0, SLOT):
                        sp.dma_start(k_s[u][r:r + 2 * HD, :, TOK:KEYS].bitcast(F32),
                                     slot_order(pad_scratch)).then_inc(pad_in, 16)
                sp.wait_ge(pool_c, 3)
                rows = xs_dram.rearrange("(p r) d -> p (r d)", p=P)
                for at in range(0, NTILE * D, ZEROS):
                    sp.dma_start(rows[:, at:at + ZEROS], zero[:, :]).then_inc(zero_out, 16)
                sp.wait_ge(w_in, FIRST_IN)

            @block.gpsimd
            def _(gp):
                for u in range(2):
                    gp.memset(v_s[u][:, :, :, :], 1.0)
                    gp.memset(x_t[u][:, :, :], 1.0).then_inc(pool_c, 1)
                for u in range(2):
                    gp.memset(q_s[u][:, HEADS * TOK:].bitcast(F32), 0.0)
                gp.memset(eps[:, :], EPS)
                gp.memset(half_neg[:, :], -0.5)
                gp.memset(zero[:, :], 0.0).then_inc(pool_c, 1)

            @block.scalar
            def _(ac):
                ac.wait_ge(w_in, FIRST_IN)
                ac.copy(k_s[0][REL:SLOT, :, :], key_rows(REL))
                ac.copy(k_s[1][REL:SLOT, :, :], key_rows(REL))
                ac.wait_ge(pool_c, 2)
                for u in range(2):
                    for t in (2, 3):
                        ac.copy(v_s[u][:, t, :, 0:HD], v_bias[:, :].rearrange("p (h d) -> p h d", h=HEADS))

            @block.vector
            def _(dv):
                count = [0]

                def step(ins):
                    count[0] += 1
                    ins.then_inc(dve_c, 1)
                    dv.wait_ge(dve_c, count[0])

                dv.wait_ge(w_in, FIRST_IN)
                for c in range(2):
                    ins = dv.tensor_scalar(x_tw[1][0:DC, c, 0:WIN], k_bias[:, c:c + 1].to_broadcast([DC, WIN]),
                                           SCALE_A, None, ALU.mult)
                step(ins)
                step(dv.tensor_copy(staged[1][:, 0:2, 0:WIN].bitcast(F32R), x_tw[1][0:DC, :, 0:WIN]))
                step(dv.tensor_tensor(staged[1][:, 4:6, 0:WIN].bitcast(F32R), x_tw[1][0:DC, :, 0:WIN],
                                      staged[1][:, 0:2, 0:WIN], ALU.subtract))
                for u in range(2):
                    dv.tensor_copy(k_s[u][SLOT + REL:P, :, :], key_rows(SLOT + REL))
                step(dv.tensor_copy(ident16[:, :], ident[:, :]))
                masks = mask_in.rearrange("p (m a k) -> p m a k", m=2, a=2)
                step(dv.tensor_copy(mask_q[:, :, :], masks[:, 0]))
                step(dv.tensor_copy(mask_k[:, :, :], masks[:, 1]))

        q_out, k_out, q_slots, k_slots, max_out, max_row, t2_out, xn_out = (sems(n, 2) for n in (
            "q_out", "k_out", "q_slots", "k_slots", "max_out", "max_row", "t2_out", "xn_out"))
        st, ag, ve, rs, xn, xt_ps, xt = (sems(n, 2) for n in (
            "ln_stats", "ln_mean", "ln_var", "ln_rstd", "ln_out", "xt_ps", "xt_sb"))
        q_ps, k_ps, v_ps, q_h, k_h, k_l, v_sb, mt_ps, mt_sb, o_ps, res = (sems(n, 2) for n in (
            "q_ps", "k_ps", "v_ps", "q_h", "k_h", "k_l", "v_sb", "mt_ps", "mt_sb", "o_ps", "res"))
        m_ps, m_sb, sc_ps, pr_sb, av_ps, dn_sb, rc_sb, ot_sb = (sems(n, 2) for n in (
            "m_ps", "m_sb", "sc_ps", "pr_sb", "av_ps", "dn_sb", "rc_sb", "ot_sb"))
        mw_ps, mw_sb = sems("mw_ps", 2), sems("mw_sb", 2)
        s1_ps, p1_sb = sems("s1_ps", 2), sems("p1_sb", 2)
        ry_ps, ry_sb, rx_ps = (sems(n, 2) for n in ("ry_ps", "ry_sb", "rx_ps"))
        xtw, q_l, rel_done, q_even, q_odd, q_done, cleared = (sems(n, 2) for n in (
            "xtw", "q_l", "rel_done", "q_even", "q_odd", "q_done", "cleared"))
        f1_ps, hid_sb, f2_ps, x2b_done, mlp_done, lg_ps = (sems(n, 2) for n in (
            "f1_ps", "hid_sb", "f2_ps", "x2b_done", "mlp_done", "lg_ps"))
        went_on = sem("went_on")

        NORM = {"a": 1, "m": 2, "b": 3, "g": 4}
        ATT = {"a": 0, "b": 1}

        def hold(eng):
            eng.sem_inc(went_on, 1)

        def run(eng, step, bases):
            def image(u, it, later=0, base=None):
                def at(per_image, done):
                    if base is None:
                        return it * per_image + done
                    return base[per_image] + (done + per_image * later)
                return u, at

            step(image(0, 0), None)
            with eng.Fori(0, B // 2 - 1) as it:
                base = {per_image: eng.snap(it * per_image) for per_image in bases}
                step(image(1, it, 0, base), image(0, it, 0, base))
                step(image(0, it, 1, base), image(1, it, 0, base))
            step(image(1, B // 2 - 1), image(0, B // 2 - 1))
            step(None, image(1, B // 2 - 1))

        block = ctx.enter_context(nc.Block("attention"))

        @block.sync
        def _(sp):
            for u in range(2):
                sp.sem_inc(t2_out[u], 16)
                sp.sem_inc(xn_out[u], 16)
            sp.wait_ge(late_in, LATE_IN)
            sp.wait_ge(pad_in, 16 * 4)

            def send_k(k):
                def go(u, at):
                    for ready, part in ((k_h, 0), (k_l, 1)):
                        sp.wait_ge(ready[u], at(2, ATT[k] + 1))
                        sp.dma_start(k_scratch[u, :, :, part].rearrange("g r n -> r g n"),
                                     staged[u][:, 2 + 4 * part:4 + 4 * part, :]).then_inc(k_out[u], 16)
                return go

            def send_q_a(u, at):
                sp.wait_ge(q_h[u], at(2, 1))
                sp.dma_start(q_scratch[u, 0, :, :, 0].rearrange("g r n -> r g n"),
                             staged[u][:, 0:2, :]).then_inc(q_out[u], 16)

            def send_q_b(u, at):
                for part in range(2):
                    if part:
                        sp.wait_ge(q_l[u], at(1, 1))
                    else:
                        sp.wait_ge(q_h[u], at(2, 2))
                    for twice in range(2):
                        sp.dma_start(q_scratch[u, part, :, :, twice].rearrange("g r n -> r g n"),
                                     staged[u][:, 4 * part:4 * part + 2, :]).then_inc(q_out[u], 16)

            def keys_in(k):
                def go(u, at):
                    sp.wait_ge(k_out[u], at(16 * 4, 16 * 2 * (ATT[k] + 1)))
                    for r in (0, SLOT):
                        sp.dma_start(k_s[u][r:r + 2 * HD, :, 0:TOK].bitcast(F32),
                                     slot_order(k_scratch[u])).then_inc(k_slots[u], 16)
                return go

            def queries_in_a(u, at):
                sp.wait_ge(q_out[u], at(16 * 5, 16))
                for e in range(2):
                    sp.dma_start(s_q[u][SLOT * e:SLOT * e + HD, :, :],
                                 q_scratch[u, 0, :, :, 0].rearrange("g (p e c) n -> e c (g p) n", e=2, c=HD)[e]
                                 ).then_inc(q_slots[u], 16)

            def queries_in_b(u, at):
                sp.wait_ge(q_out[u], at(16 * 5, 16 * 5))
                for e in range(2):
                    sp.dma_start(q_heads[u][SLOT * e:SLOT * e + 2 * HD, :, :].bitcast(F32),
                                 slot_order(q_scratch[u, e])).then_inc(q_slots[u], 16)

            def max_rows(k):
                def go(u, at):
                    sp.wait_ge(mt_sb[u], at(2, ATT[k] + 1))
                    sp.dma_start(max_scratch[u], neg_max_t[u][:, :]).then_inc(max_out[u], 16)
                    sp.wait_ge(max_out[u], at(32, 16 * (ATT[k] + 1)))
                    sp.dma_start(q_heads[u][MAXROW:MAXROW + 1, :, :].bitcast(F32),
                                 max_scratch[u:u + 1]).then_inc(max_row[u], 16)
                return go

            def next_x(u, at):
                sp.wait_ge(res[u], at(2, 1))
                sp.dma_start(x_in[u][:, :, :], a["x"][at(2, 2 + u) % B]).then_inc(x_loaded[u], 16)

            def store_t2(u, at):
                sp.wait_ge(res[u], at(2, 2))
                sp.dma_start(t2_dram[bass.ds(at(4, 2 * u), 2)].rearrange("t p d -> p t d"),
                             x_2[u][:, :].rearrange("p (t d) -> p t d", t=2)).then_inc(t2_out[u], 16)

            def store_xn(u, at):
                sp.wait_ge(xn[u], at(4, NORM["g"]))
                sp.dma_start(xn_dram[bass.ds(at(4, 2 * u), 2)].rearrange("t p d -> p t d"),
                             x_n[u][:, :, :]).then_inc(xn_out[u], 16)

            def step(f, g):
                if g:
                    next_x(*g)
                if f:
                    send_q_a(*f)
                    send_k("a")(*f)
                    queries_in_a(*f)
                    keys_in("a")(*f)
                if g:
                    send_q_b(*g)
                    send_k("b")(*g)
                    queries_in_b(*g)
                    keys_in("b")(*g)
                    max_rows("b")(*g)
                if f:
                    max_rows("a")(*f)
                if g:
                    store_t2(*g)
                    store_xn(*g)

            run(sp, step, (1, 2, 4, 32, 64, 80))
            for u in range(2):
                sp.wait_ge(t2_out[u], 16 * (B // 2 + 1))
                sp.wait_ge(xn_out[u], 16 * (B // 2 + 1))
                sp.wait_ge(x_loaded[u], 16 * (B // 2 + 1))
            sp.wait_ge(zero_out, 16 * 16)

        @block.gpsimd
        def _(gp):
            def rstds(k):
                def go(u, at):
                    gp.wait_ge(ag[u], at(4, NORM[k]))
                    gp.tensor_tensor(var_eps[u][:, :], mean_var[u][:, :, 1], eps[:, :], ALU.add).then_inc(ve[u], 1)
                    gp.wait_ge(ve[u], at(4, NORM[k]))
                    gp.tensor_tensor(rstd[u][:, :], var_eps[u][:, :], half_neg[:, :], ALU.pow).then_inc(rs[u], 1)
                return go

            def to_windows(u, at):
                gp.wait_ge(xt[u], at(4, NORM["a"]))
                hold(gp)
                for c in range(2):
                    for dst, src in zip(win_order(x_tw[u][:, c:c + 1, :]), window_pieces(yx(x_t[u][:, c:c + 1, :]))):
                        ins = gp.tensor_copy(dst[:, 0], src[:, 0])
                ins.then_inc(xtw[u], 1)

            def norm_m(u, at):
                rstds("m")(u, at)
                gp.wait_ge(res[u], at(2, 1))
                gp.tensor_tensor(x_2b[u][:, :], x_2[u][:, :], b_fc2[:, :], ALU.add).then_inc(x2b_done[u], 1)

            def clear(u, at):
                for half, r in enumerate((REL, SLOT + REL)):
                    if half:
                        gp.wait_ge(cleared[u], at(2, 1))
                    else:
                        gp.wait_ge(rs[u], at(4, NORM["b"]))
                    hold(gp)
                    gp.memset(q_heads[u][r:r + SLOT - REL, :, :].bitcast(F32), 0.0).then_inc(cleared[u], 1)

            def step(f, g):
                if f:
                    rstds("a")(*f)
                    to_windows(*f)
                if g:
                    norm_m(*g)
                    rstds("b")(*g)
                    clear(*g)
                    rstds("g")(*g)

            run(gp, step, (1, 2, 4))

        @block.scalar
        def _(ac):
            def channels(k, scale, shift):
                def go(u, at):
                    ac.wait_ge(xt_ps[u], at(4, NORM[k]))
                    for c in range(2):
                        src = ps[u][0:DC, 0, c * TOK:(c + 1) * TOK]
                        if scale is None:
                            ins = ac.copy(x_t[u][0:DC, c, :], src)
                        else:
                            ins = ac.activation(x_t[u][0:DC, c, :], src, ACT.Identity,
                                                bias=norms[:, shift + c:shift + c + 1],
                                                scale=norms[:, scale + c:scale + c + 1])
                    ins.then_inc(xt[u], 1)
                return go

            def queries(k):
                def go(u, at):
                    ac.wait_ge(q_ps[u], at(2, ATT[k] + 1))
                    dst = staged[u][:, 0:2, :].rearrange("p g n -> p (g n)")
                    ac.activation(dst if k == "a" else dst.bitcast(F32R), ps[u][0:DC, 1, :],
                                  ACT.Copy).then_inc(q_h[u], 1)
                return go

            def high_keys(k, scale):
                def go(u, at):
                    ac.wait_ge(k_ps[u], at(2, ATT[k] + 1))
                    ac.activation(staged[u][:, 2:4, :].rearrange("p g n -> p (g n)").bitcast(F32R),
                                  ps[u][0:DC, 2, :], ACT.Copy, scale=scale).then_inc(k_h[u], 1)
                return go

            def values_a(u, at):
                ac.wait_ge(v_ps[u], at(2, 1))
                ac.copy(v_s[u][0:HALF, 0:2, :, 0:HD],
                        ps[u][0:HALF, 3, 0:2 * D].rearrange("p (t h d) -> p t h d", t=2, h=HEADS))
                ac.copy(v_s[u][0:OUT, 2, :, 0:HD],
                        ps[u][0:OUT, 0, 0:D].rearrange("p (h d) -> p h d", h=HEADS)).then_inc(v_sb[u], 1)

            def values_b(u, at):
                ac.wait_ge(v_ps[u], at(2, 2))
                ac.copy(v_s[u][:, 0:2, :, 0:HD],
                        ps[u][:, 3, 0:2 * D].rearrange("p (t h d) -> p t h d", t=2, h=HEADS)).then_inc(v_sb[u], 1)

            def rel(u, at):
                for half in range(2):
                    ac.wait_ge(ry_ps[u], at(2, half + 1))
                    if half == 0:
                        ac.wait_ge(k_out[u], at(16 * 4, 16 * 2))
                    for b in range(2):
                        y = 8 * half + 4 * b
                        ins = ac.copy(yx(rel_sum[u])[:, :, y:y + 4, :].rearrange("p g y x -> p y g x"),
                                      ps[u][:, 2 * half + b, 0:384].rearrange("p (y g x) -> p y g x", y=4, g=PAIRS))
                    ins.then_inc(ry_sb[u], 1)

            def split(u, at):
                ac.wait_ge(rel_done[u], at(1, 1))
                for dst, src in zip(win_order(q_heads[u][0:SLOT, 0:HEADS:2, :]),
                                    window_pieces(yx(rel_sum[u][0:SLOT]))):
                    ins = ac.copy(dst, src)
                ins.then_inc(q_even[u], 1)

            def max_rows(k):
                def go(u, at):
                    ac.wait_ge(mt_ps[u], at(2, ATT[k] + 1))
                    ac.copy(neg_max_t[u][:, :], ps[u][0:HEADS, 0, 0:TOK]).then_inc(mt_sb[u], 1)
                return go

            def exp_a(p):
                def go(u, at):
                    if p == 0:
                        ac.wait_ge(q_done[u], at(1, 1))
                    for e, (ready, used) in enumerate(((s1_ps, p1_sb), (sc_ps, pr_sb))):
                        ac.wait_ge(ready[u], at(12, p + 1))
                        ac.activation(probs[u][0:HALF, p % 4, e, 0:2 * WIN], ps[u][0:HALF, e, 0:2 * WIN], ACT.Exp)
                        ac.activation(probs[u][:, p % 4, e, 2 * WIN:512], ps[u][:, e, 2 * WIN:512],
                                      ACT.Exp).then_inc(used[u], 1)
                return go

            def exp_b(p):
                def go(u, at):
                    for e, (ready, used) in enumerate(((s1_ps, p1_sb), (sc_ps, pr_sb))):
                        ac.wait_ge(ready[u], at(12, PAIRS + p + 1))
                        ac.activation(probs[u][:, p % 4, e, 0:384], ps[u][:, e, 0:384], ACT.Exp).then_inc(used[u], 1)
                return go

            def fc1(u, at):
                for f in range(FT):
                    if f % 2 == 0:
                        ac.wait_ge(f1_ps[u], at(FT // 2, f // 2 + 1))
                    ins = ac.activation(hid[u][:, f, :], ps[u][:, 1 + f // 2, (f % 2) * TOK:(f % 2 + 1) * TOK],
                                        ACT.Gelu, bias=b_fc1[:, f:f + 1])
                    if f % 2:
                        ins.then_inc(hid_sb[u], 1)

            def step(f, g):
                if f:
                    channels("a", 0, 2)(*f)
                    queries("a")(*f)
                    high_keys("a", SCALE_A)(*f)
                if g:
                    channels("m", 4, 6)(*g)
                if f:
                    values_a(*f)
                if g:
                    fc1(*g)
                if f:
                    rel(*f)
                if g:
                    channels("b", None, None)(*g)
                    queries("b")(*g)
                    high_keys("b", SCALE_B)(*g)
                    values_b(*g)
                if f:
                    split(*f)
                if g:
                    max_rows("b")(*g)
                    exp_b(0)(*g)
                if f:
                    max_rows("a")(*f)
                if g:
                    exp_b(1)(*g)
                    exp_b(2)(*g)
                    exp_b(3)(*g)
                    exp_b(4)(*g)
                    exp_b(5)(*g)
                if f:
                    exp_a(0)(*f)
                    exp_a(1)(*f)
                    exp_a(2)(*f)
                    exp_a(3)(*f)
                    exp_a(4)(*f)
                if g:
                    channels("g", None, None)(*g)
                if f:
                    exp_a(5)(*f)

            run(ac, step, (1, 2, 3, 4, 12, 64))

        @block.vector
        def _(dv):
            def norm(u, at, k, src):
                for t in range(2):
                    ins = dv.bn_stats(stats[u][:, t, :], src[:, t * D:(t + 1) * D])
                ins.then_inc(st[u], 1)
                dv.wait_ge(st[u], at(4, NORM[k]))
                hold(dv)
                for t in range(2):
                    ins = dv.bn_aggr(mean_var[u][:, t, :], stats[u][:, t, :])
                ins.then_inc(ag[u], 1)
                dv.wait_ge(rs[u], at(4, NORM[k]))
                if k == "m":
                    dv.wait_ge(xn_out[u], at(16, 16))
                dst = x_na[u] if k == "a" else x_n[u]
                for t in range(2):
                    ins = dv.tensor_scalar(dst[:, t, :], src[:, t * D:(t + 1) * D],
                                           mean_var[u][:, t, 0:1], rstd[u][:, t:t + 1], ALU.subtract, ALU.mult)
                ins.then_inc(xn[u], 1)

            def norm_a(u, at):
                dv.wait_ge(x_loaded[u], at(16, 16))
                norm(u, at, "a", x_in[u][:, :, :].rearrange("p t d -> p (t d)"))

            def low_queries(u, at):
                dv.wait_ge(q_h[u], at(2, 2))
                dv.tensor_tensor(staged[u][:, 4:6, :].rearrange("p g n -> p (g n)").bitcast(F32R),
                                 ps[u][0:DC, 1, :], staged[u][:, 0:2, :].rearrange("p g n -> p (g n)"),
                                 ALU.subtract).then_inc(q_l[u], 1)

            def low_keys(k, scale):
                def go(u, at):
                    dv.wait_ge(k_h[u], at(2, ATT[k] + 1))
                    dv.scalar_tensor_tensor(out=staged[u][:, 6:8, :].rearrange("p g n -> p (g n)").bitcast(F32R),
                                            in0=ps[u][0:DC, 2, :], scalar=scale,
                                            in1=staged[u][:, 2:4, :].rearrange("p g n -> p (g n)"),
                                            op0=ALU.mult, op1=ALU.subtract).then_inc(k_l[u], 1)
                return go

            def rel(u, at):
                dv.wait_ge(ry_sb[u], at(2, 2))
                for half in range(2):
                    dv.wait_ge(rx_ps[u], at(2, half + 1))
                    for b in range(2):
                        x = 8 * half + 4 * b
                        part = yx(rel_sum[u])[:, :, :, x:x + 4].rearrange("p g y x -> p x g y")
                        ins = dv.tensor_tensor(
                            part, ps[u][:, 2 * half + b, 0:384].rearrange("p (x g y) -> p x g y", x=4, g=PAIRS),
                            part, ALU.add)
                ins.then_inc(rel_done[u], 1)

            def low_rows(u, rows, to, first):
                for dst, src, hi in zip(win_order(q_heads[u][to, first:HEADS:2, :]),
                                        window_pieces(yx(rel_sum[u][rows])),
                                        win_order(q_heads[u][rows, first:HEADS:2, :].bitcast(F32))):
                    ins = dv.tensor_tensor(dst, src, hi, ALU.subtract)
                return ins

            def split_odd(u, at):
                dv.wait_ge(rel_done[u], at(1, 1))
                for dst, src in zip(win_order(q_heads[u][SLOT:P, 1:HEADS:2, :]),
                                    window_pieces(yx(rel_sum[u][SLOT:P]))):
                    ins = dv.tensor_copy(dst, src)
                ins.then_inc(q_odd[u], 1)
                dv.wait_ge(q_odd[u], at(1, 1))
                low_rows(u, slice(SLOT, P), slice(0, SLOT), 1)

            def split_even(u, at):
                dv.wait_ge(q_even[u], at(1, 1))
                low_rows(u, slice(0, SLOT), slice(SLOT, P), 0).then_inc(q_done[u], 1)

            def max_a(p):
                def go(u, at):
                    dv.wait_ge(mw_ps[u], at(6, p + 1))
                    dv.tensor_reduce(neg_max[u][0:HALF, 0:2, 2 * p:2 * p + 2].rearrange("p q e -> p e q"),
                                     ps[u][0:HALF, 0:2, 0:2 * WIN].rearrange("p e (q k) -> p e q k", q=2),
                                     AX.X, ALU.max, negate=True).then_inc(mw_sb[u], 1)
                    dv.wait_ge(m_ps[u], at(12, p + 1))
                    dv.tensor_reduce(neg_max[u][0:OUT, 2, 2 * p:2 * p + 2], ps[u][0:OUT, 2:4, 0:TOK],
                                     AX.X, ALU.max, negate=True).then_inc(m_sb[u], 1)
                return go

            def max_b(p):
                def go(u, at):
                    bank = 2 * (p % 2)
                    dv.wait_ge(m_ps[u], at(12, PAIRS + p + 1))
                    dv.tensor_reduce(neg_max[u][:, 0, 2 * p:2 * p + 2], ps[u][:, bank:bank + 2, 0:P],
                                     AX.X, ALU.max, negate=True)
                    dv.tensor_reduce(neg_max[u][:, 1, 2 * p:2 * p + 2], ps[u][:, bank:bank + 2, P:3 * P],
                                     AX.X, ALU.max, negate=True).then_inc(m_sb[u], 1)
                return go

            def normalise(k, g):
                def go(u, at):
                    bank, done = 2 + g % 2, GROUPS * ATT[k] + g + 1
                    dv.wait_ge(av_ps[u], at(6, done))
                    if g:
                        dv.wait_ge(ot_sb[u], at(6, done - 1))
                    hold(dv)
                    dv.stream_shuffle(den[u][:, :], ps[u][:, bank, 0:TOK], [HD] * 32).then_inc(dn_sb[u], 1)
                    dv.wait_ge(dn_sb[u], at(6, done))
                    dv.reciprocal(den[u][:, :], den[u][:, :]).then_inc(rc_sb[u], 1)
                    dv.wait_ge(rc_sb[u], at(6, done))
                    if k == "a":
                        for dst, src, d in zip(window_pieces(yx(o_t[u][:, g:g + 1, :])),
                                               win_order(ps[u][:, bank:bank + 1, 0:TOK]),
                                               win_order(den[u][:, :].unsqueeze(1))):
                            ins = dv.tensor_tensor(dst[:, 0], src[:, 0], d[:, 0], ALU.mult)
                    else:
                        ins = dv.tensor_tensor(o_t[u][:, g, :], ps[u][:, bank, 0:TOK], den[u][:, :], ALU.mult)
                    ins.then_inc(ot_sb[u], 1)
                return go

            def out_a(u, at):
                dv.wait_ge(o_ps[u], at(2, 1))
                dv.wait_ge(t2_out[u], at(16, 16))
                dv.tensor_tensor(by_tile(x_2[u]), ps[u][:, 0:2, 0:D], x_in[u][:, :, :], ALU.add).then_inc(res[u], 1)

            def norm_m(u, at):
                dv.wait_ge(res[u], at(2, 1))
                norm(u, at, "m", x_2[u])

            def fc2(u, at):
                dv.wait_ge(f2_ps[u], at(1, 1))
                dv.wait_ge(x2b_done[u], at(1, 1))
                dv.tensor_tensor(by_tile(x_3[u]), ps[u][:, 0:2, 0:D], by_tile(x_2b[u]), ALU.add).then_inc(mlp_done[u], 1)

            def norm_b(u, at):
                dv.wait_ge(mlp_done[u], at(1, 1))
                norm(u, at, "b", x_3[u])

            def out_b(u, at):
                dv.wait_ge(o_ps[u], at(2, 2))
                dv.tensor_tensor(by_tile(x_2[u]), ps[u][:, 0:2, 0:D], by_tile(x_3[u]), ALU.add).then_inc(res[u], 1)

            def norm_g(u, at):
                dv.wait_ge(res[u], at(2, 2))
                norm(u, at, "g", x_2[u])

            def gate(u, at):
                dv.wait_ge(lg_ps[u], at(1, 1))
                dv.tensor_copy(logits[:, bass.ds(at(4, 2 * u), 2), :],
                               ps[u][:, 1, 0:2 * NE].rearrange("p (t e) -> p t e", t=2))

            def step(f, g):
                if f:
                    norm_a(*f)
                if g:
                    normalise("a", 2)(*g)
                    out_a(*g)
                    norm_m(*g)
                if f:
                    low_keys("a", SCALE_A)(*f)
                if g:
                    fc2(*g)
                    norm_b(*g)
                    low_queries(*g)
                    low_keys("b", SCALE_B)(*g)
                if f:
                    rel(*f)
                    split_odd(*f)
                    split_even(*f)
                    max_a(0)(*f)
                    max_a(1)(*f)
                if g:
                    max_b(0)(*g)
                    max_b(1)(*g)
                    max_b(2)(*g)
                    max_b(3)(*g)
                    max_b(4)(*g)
                    max_b(5)(*g)
                if f:
                    max_a(2)(*f)
                    max_a(3)(*f)
                    max_a(4)(*f)
                    max_a(5)(*f)
                if g:
                    normalise("b", 0)(*g)
                    normalise("b", 1)(*g)
                    normalise("b", 2)(*g)
                if f:
                    normalise("a", 0)(*f)
                if g:
                    out_b(*g)
                    norm_g(*g)
                if f:
                    normalise("a", 1)(*f)
                if g:
                    gate(*g)

            run(dv, step, (1, 2, 4, 6, 12, 16))

        @block.tensor
        def _(pe):
            def transpose_norm(k):
                def go(u, at):
                    src = x_na[u] if k == "a" else x_n[u]
                    pe.wait_ge(xn[u], at(4, NORM[k]))
                    for t in range(2):
                        for c in range(2):
                            ins = pe.transpose(ps[u][0:DC, 0, c * TOK + t * P:c * TOK + (t + 1) * P],
                                               src[:, t, c * DC:(c + 1) * DC], ident[:, :])
                    ins.then_inc(xt_ps[u], 1)
                return go

            def chunks(dst, w, cols, x, toks, ones):
                pe.matmul(dst, w[0:DC + ones, 0, cols], x[0:DC + ones, 0, toks], start=True, stop=False)
                return pe.matmul(dst, w[0:DC, 1, cols], x[0:DC, 1, toks], start=False, stop=True)

            def tokens(dst, x, toks, w, cols, ones):
                pe.matmul(dst, x[0:DC + ones, 0, toks], w[0:DC + ones, 0, cols], start=True, stop=False)
                return pe.matmul(dst, x[0:DC, 1, toks], w[0:DC, 1, cols], start=False, stop=True)

            def output(k, w):
                def go(u, at):
                    for g in range(GROUPS):
                        pe.wait_ge(ot_sb[u], at(6, GROUPS * ATT[k] + g + 1))
                        for t in range(2):
                            ins = pe.matmul(ps[u][:, t, 0:D], o_t[u][:, g, t * P:(t + 1) * P],
                                            w[:, g, :], start=(g == 0), stop=(g == GROUPS - 1))
                    ins.then_inc(o_ps[u], 1)
                return go

            def channel_rows(u, bank, w, first, x, ones, done):
                for g in range(2):
                    ins = chunks(ps[u][0:DC, bank, g * TOK:(g + 1) * TOK], w,
                                 slice(first + g * DC, first + (g + 1) * DC), x[u], slice(0, TOK), ones)
                ins.then_inc(done[u], 1)

            def q_a(u, at):
                pe.wait_ge(xt[u], at(4, NORM["a"]))
                channel_rows(u, 1, w_qkv_a, 0, x_t, 1, q_ps)

            def k_a(u, at):
                pe.wait_ge(xtw[u], at(1, 1))
                channel_rows(u, 2, w_qkv_a, D, x_tw, 1, k_ps)

            def v_a(u, at):
                for t in range(2):
                    tokens(ps[u][0:HALF, 3, t * D:(t + 1) * D], x_tw[u], slice(t * HALF, (t + 1) * HALF),
                           w_qkv_a, slice(2 * D, 3 * D), 1)
                tokens(ps[u][0:OUT, 0, 0:D], x_tw[u], slice(WIN, TOK), w_qkv_a,
                       slice(2 * D, 3 * D), 1).then_inc(v_ps[u], 1)

            def positions(u, bank, i, table, toks):
                dst = ps[u][:, bank, i * 96:(i + 1) * 96].rearrange("p (g x) -> p g x", g=PAIRS)
                return pe.matmul(dst, rel_w[:, table, :], toks, start=True, stop=True)

            def rows_of_queries(u, at):
                pe.wait_ge(q_slots[u], at(64, 32))
                pe.wait_ge(v_sb[u], at(2, 1))
                pe.wait_ge(k_l[u], at(2, 1))
                for half in range(2):
                    for y in range(8 * half, 8 * half + 8):
                        ins = positions(u, y // 4, y % 4, y % WS, s_q[u][:, :, y * S:(y + 1) * S])
                    ins.then_inc(ry_ps[u], 1)

            def columns_of_queries(u, at):
                for half in range(2):
                    pe.wait_ge(ry_sb[u], at(2, half + 1))
                    for x in range(8 * half, 8 * half + 8):
                        ins = positions(u, x // 4, x % 4, WS + x % WS, s_q[u][:, :, x:TOK:S])
                    ins.then_inc(rx_ps[u], 1)

            def max_a(p):
                def go(u, at):
                    if p == 0:
                        pe.wait_ge(q_done[u], at(1, 1))
                        pe.wait_ge(k_slots[u], at(64, 32))
                    else:
                        pe.wait_ge(mw_sb[u], at(6, p))
                    for h in (2 * p, 2 * p + 1):
                        for q in range(2):
                            ins = pe.matmul(ps[u][0:HALF, h % 2, q * WIN:(q + 1) * WIN],
                                            q_heads[u][:, h, q * HALF:(q + 1) * HALF], k_s[u][:, h, 0:WIN],
                                            start=True, stop=True)
                    ins.then_inc(mw_ps[u], 1)
                    if p:
                        pe.wait_ge(m_sb[u], at(12, p))
                    for e in range(2):
                        h = 2 * p + e
                        ins = pe.matmul(ps[u][0:WIDE, 2 + e, 0:TOK], q_s[u][:, h * TOK + WIN:h * TOK + WIN + WIDE],
                                        k_s[u][:, h, WIN:KEYS], start=True, stop=True)
                    ins.then_inc(m_ps[u], 1)
                return go

            def row_a(u, at):
                pe.wait_ge(m_sb[u], at(12, PAIRS))
                for t, (rows, first) in enumerate(((HALF, 0), (HALF, HALF), (OUT, WIN))):
                    ins = pe.transpose(ps[u][0:HEADS, 0, first:first + rows], neg_max[u][0:rows, t, :],
                                       ident[0:rows, 0:rows])
                ins.then_inc(mt_ps[u], 1)

            def scores_a(u, p, e):
                h = 2 * p + e
                for k in range(2):
                    pe.matmul(ps[u][0:HALF, e, k * WIN:(k + 1) * WIN],
                              k_s[u][:, h, k * HALF:(k + 1) * HALF], q_heads[u][:, h, 0:WIN],
                              start=True, stop=True)
                for k in range(2):
                    ins = pe.matmul(ps[u][:, e, 2 * WIN + k * OUT:2 * WIN + (k + 1) * OUT],
                                    k_s[u][:, h, WIN + k * P:WIN + (k + 1) * P], q_heads[u][:, h, WIN:TOK],
                                    start=True, stop=True)
                return ins

            def values_a(u, g):
                for k in range(2):
                    for i in range(4):
                        h = 4 * g + i
                        pe.matmul(ps[u][32 * i:32 * i + 32, 2 + g % 2, 0:WIN], v_s[u][0:HALF, k, h, :],
                                  probs[u][0:HALF, h // 2 % 4, h % 2, k * WIN:(k + 1) * WIN],
                                  start=(k == 0), stop=(k == 1))
                for k in range(2):
                    for i in range(4):
                        h = 4 * g + i
                        ins = pe.matmul(ps[u][32 * i:32 * i + 32, 2 + g % 2, WIN:TOK], v_s[u][:, 2 + k, h, :],
                                        probs[u][:, h // 2 % 4, h % 2, 2 * WIN + k * OUT:2 * WIN + (k + 1) * OUT],
                                        start=(k == 0), stop=(k == 1))
                ins.then_inc(av_ps[u], 1)

            def attend(k, p, scores, values):
                def go(u, at):
                    before = PAIRS * ATT[k] + p
                    if p == 0:
                        pe.wait_ge(max_row[u], at(32, 16 * (ATT[k] + 1)))
                    elif p < PAIRS:
                        pe.wait_ge(p1_sb[u], at(12, before))
                    if p < PAIRS:
                        scores(u, p, 0).then_inc(s1_ps[u], 1)
                    if p:
                        pe.wait_ge(pr_sb[u], at(12, before))
                    if p < PAIRS:
                        scores(u, p, 1).then_inc(sc_ps[u], 1)
                    if p and p % 2 == 0:
                        if p == PAIRS:
                            pe.wait_ge(ot_sb[u], at(6, GROUPS * ATT[k] + 1))
                        values(u, p // 2 - 1)
                return go

            def fc1(u, at):
                pe.wait_ge(xt[u], at(4, NORM["m"]))
                for f in range(FT):
                    ins = chunks(ps[u][:, 1 + f // 2, (f % 2) * TOK:(f % 2 + 1) * TOK], w_fc1,
                                 slice(f * P, (f + 1) * P), x_t[u], slice(0, TOK), 0)
                    if f % 2:
                        ins.then_inc(f1_ps[u], 1)

            def fc2(u, at):
                for f in range(FT):
                    if f % 2 == 0:
                        pe.wait_ge(hid_sb[u], at(FT // 2, f // 2 + 1))
                    for t in range(2):
                        ins = pe.matmul(ps[u][:, t, 0:D], hid[u][:, f, t * P:(t + 1) * P],
                                        w_fc2[:, f, :], start=(f == 0), stop=(f == FT - 1))
                ins.then_inc(f2_ps[u], 1)

            def q_b(u, at):
                pe.wait_ge(xt[u], at(4, NORM["b"]))
                channel_rows(u, 1, w_qkv_b, 0, x_t, 0, q_ps)

            def k_b(u, at):
                channel_rows(u, 2, w_qkv_b, D, x_t, 0, k_ps)

            def v_b(u, at):
                for t in range(2):
                    ins = tokens(ps[u][:, 3, t * D:(t + 1) * D], x_t[u], slice(t * P, (t + 1) * P),
                                 w_qkv_b, slice(2 * D, 3 * D), 0)
                ins.then_inc(v_ps[u], 1)

            def masked(u, bank, mask):
                pe.matmul(ps[u][:, bank, 0:512].rearrange("p (a k) -> p a k", a=2)[:, :, 0:P], ident16[:, :],
                          mask[:, :, :], start=True, stop=False, skip_group_check=True)

            def max_b(p):
                def go(u, at):
                    if p == 0:
                        pe.wait_ge(q_slots[u], at(64, 64))
                        pe.wait_ge(k_slots[u], at(64, 64))
                        pe.wait_ge(cleared[u], at(2, 2))
                        pe.wait_ge(v_sb[u], at(2, 2))
                        pe.wait_ge(k_l[u], at(2, 2))
                    if p >= 2:
                        pe.wait_ge(m_sb[u], at(12, PAIRS + p - 1))
                    for e in range(2):
                        h, bank = 2 * p + e, 2 * (p % 2) + e
                        masked(u, bank, mask_q)
                        pe.matmul(ps[u][:, bank, 0:P], q_heads[u][:, h, 0:P], k_s[u][:, h, 0:P],
                                  start=False, stop=True, skip_group_check=True)
                        ins = pe.matmul(ps[u][:, bank, P:3 * P], q_heads[u][:, h, P:2 * P], k_s[u][:, h, 0:2 * P],
                                        start=False, stop=True, skip_group_check=True)
                    ins.then_inc(m_ps[u], 1)
                return go

            def row_b(u, at):
                pe.wait_ge(m_sb[u], at(12, 2 * PAIRS))
                for t in range(2):
                    ins = pe.transpose(ps[u][0:HEADS, 0, t * P:(t + 1) * P], neg_max[u][:, t, :], ident[:, :])
                ins.then_inc(mt_ps[u], 1)

            def scores_b(u, p, e):
                h = 2 * p + e
                masked(u, e, mask_k)
                for k in range(2):
                    ins = pe.matmul(ps[u][:, e, k * TOK:TOK + k * P], k_s[u][:, h, k * P:(k + 1) * P],
                                    q_heads[u][:, h, k * P:TOK], start=False, stop=True, skip_group_check=True)
                return ins

            def values_b(u, g):
                for k in range(2):
                    for i in range(4):
                        h = 4 * g + i
                        ins = pe.matmul(ps[u][32 * i:32 * i + 32, 2 + g % 2, k * P:TOK], v_s[u][:, k, h, :],
                                        probs[u][:, h // 2 % 4, h % 2, k * TOK:k * TOK + TOK - k * P],
                                        start=(k == 0), stop=True, skip_group_check=(k == 1))
                ins.then_inc(av_ps[u], 1)

            def gate(u, at):
                pe.wait_ge(xt[u], at(4, NORM["g"]))
                for t in range(2):
                    ins = tokens(ps[u][:, 1, t * NE:(t + 1) * NE], x_t[u], slice(t * P, (t + 1) * P), w_gate,
                                 slice(0, NE), 1)
                ins.then_inc(lg_ps[u], 1)

            def step(f, g):
                if f:
                    transpose_norm("a")(*f)
                if g:
                    output("a", w_out_a)(*g)
                if f:
                    q_a(*f)
                    k_a(*f)
                if g:
                    transpose_norm("m")(*g)
                if f:
                    v_a(*f)
                if g:
                    fc1(*g)
                    fc2(*g)
                if f:
                    rows_of_queries(*f)
                if g:
                    transpose_norm("b")(*g)
                    q_b(*g)
                    k_b(*g)
                if f:
                    columns_of_queries(*f)
                if g:
                    v_b(*g)
                if f:
                    max_a(0)(*f)
                    max_a(1)(*f)
                if g:
                    max_b(0)(*g)
                    max_b(1)(*g)
                    max_b(2)(*g)
                    max_b(3)(*g)
                    max_b(4)(*g)
                    max_b(5)(*g)
                if f:
                    max_a(2)(*f)
                if g:
                    row_b(*g)
                if f:
                    max_a(3)(*f)
                    max_a(4)(*f)
                    max_a(5)(*f)
                if g:
                    attend("b", 0, scores_b, values_b)(*g)
                if f:
                    row_a(*f)
                if g:
                    attend("b", 1, scores_b, values_b)(*g)
                    attend("b", 2, scores_b, values_b)(*g)
                    attend("b", 3, scores_b, values_b)(*g)
                    attend("b", 4, scores_b, values_b)(*g)
                    attend("b", 5, scores_b, values_b)(*g)
                if f:
                    attend("a", 0, scores_a, values_a)(*f)
                if g:
                    attend("b", 6, scores_b, values_b)(*g)
                if f:
                    attend("a", 1, scores_a, values_a)(*f)
                    attend("a", 2, scores_a, values_a)(*f)
                if g:
                    output("b", w_out_b)(*g)
                if f:
                    attend("a", 3, scores_a, values_a)(*f)
                    attend("a", 4, scores_a, values_a)(*f)
                if g:
                    transpose_norm("g")(*g)
                if f:
                    attend("a", 5, scores_a, values_a)(*f)
                if g:
                    gate(*g)
                if f:
                    attend("a", 6, scores_a, values_a)(*f)

            run(pe, step, (1, 2, 3, 4, 6, 12, 32, 64))


def expert_phase(nc, a, t2_dram, xn_dram, xs_dram, ys_dram, logits, ident, ps, sem, out):
    with ExitStack() as ctx:
        def sb(name, shape, dt=F32):
            return ctx.enter_context(nc.sbuf_tensor(name, shape, dt))

        def two(name, shape, dt=F32):
            return [sb(f"{name}{u}", shape, dt) for u in range(2)]

        def sems(name, n=2):
            return [sem(f"{name}{i}") for i in range(n)]

        w1 = sb("w1", [DC + 1, NE, 2, MLP])
        w2 = sb("w2", [P, NE, FT, D])
        b2 = sb("b2", [P, NE, D])
        xn_all = sb("xn_all", [P, NT, D])
        t2_all = sb("t2_all", [P, NT, D])
        y_sel = sb("y_sel", [P, 2, NT, D])
        before = sb("before", [P, P])
        ones = sb("ones", [P, P])
        numbers = sb("numbers", [P, NTILE])
        starts = sb("starts", [P, NT])

        top = sb("top", [P, NT, 8])
        top_at = sb("top_at", [P, NT, 8], U32)
        row = sb("row", [P, NT])
        row2 = sb("row2", [P, NT])
        gates = sb("gates", [P, NT, NE])
        chosen = sb("chosen", [P, NT, 2])
        hot = sb("hot", [P, 2, NT, NE])
        both = sb("both", [P, NT, NE])
        counts = sb("counts", [P, 2, NT * NE])
        seen = sb("seen", [P, NT + 1, NE])
        full = sb("full", [P, NE, NT])
        tiles_of = sb("tiles_of", [P, NE])
        first = sb("first", [P, NE + 1])
        place = sb("place", [P, NT, NE])
        place_s = sb("place_s", [P, NT, NE])
        pos_f = sb("pos_f", [P, 2, NT])
        pos = sb("pos", [P, 2 * NT], U32)
        weight = sb("weight", [P, 2, NT])
        past = sb("past", [P, NTILE, NE - 1])
        expert_f = sb("expert_f", [P, NTILE])
        expert = sb("expert", [P, NTILE], I32)

        rows_in = two("rows_in", [P, D])
        rows_t = two("rows_t", [DC + 1, 2, P])
        hid_t = two("hid_t", [P, FT, P])
        w1_tile = two("w1_tile", [DC + 1, 2, MLP])
        y_out = two("y_out", [P, D])

        gathered = sems("gathered", NT // 4)
        c_in, w_loaded, xn_loaded, t2_loaded, pool_c, exp_in, exp_out, choice, counted, routed, experts_known = (
            sem(n) for n in ("c_in", "w_loaded", "xn_loaded", "t2_loaded", "pool_c", "exp_in", "exp_out", "choice",
                             "counted", "routed", "experts_known"))
        dve_c, scattered, mixed, stored = (sem(n) for n in ("dve_c", "scattered", "mixed", "stored"))
        in_loaded, in_ps, in_t, h_ps, h_sb, y_ps, y_sb, y_stored = (sems(n) for n in (
            "in_loaded", "in_ps", "in_t", "h_ps", "h_sb", "y_ps", "y_sb", "y_stored"))
        w1_first, w1_second = sems("w1_first"), sems("w1_second")
        STEPS = NTILE // 2

        def experts_of(eng, it, ahead):
            at = [eng.snap((it * 2 + 2 + u) % NTILE) if ahead else it * 2 + u for u in range(2)]
            return [eng.value_load(expert[0:1, bass.ds(at[u], 1)], min_val=0, max_val=NE - 1) for u in range(2)]

        block = ctx.enter_context(nc.Block("experts"))

        @block.sync
        def _(sp):
            for dst, name in ((before[:, :], "before"), (starts[:, :], "starts"), (numbers[:, :], "numbers")):
                sp.dma_start(dst, a[name]).then_inc(c_in, 16)
            sp.dma_start(xn_all[:, :, :], xn_dram.rearrange("t p d -> p t d")).then_inc(xn_loaded, 16)
            for e in range(NE):
                sp.dma_start(w1[:, e], a["e_w1"][:, e]).then_inc(w_loaded, 16)
                sp.dma_start(w2[:, e], a["e_w2"][:, e]).then_inc(w_loaded, 16)
            sp.dma_start(b2[:, :, :], a["e_b2"].to_broadcast([P, NE, D])).then_inc(w_loaded, 16)
            sp.dma_start(t2_all[:, :, :], t2_dram.rearrange("t p d -> p t d")).then_inc(t2_loaded, 16)
            sorted_rows = xs_dram.rearrange("(t p) d -> t p d", p=P)
            result = ys_dram.rearrange("(t p) d -> t p d", p=P)
            sp.wait_ge(scattered, 16 * 2 * NT)
            for u in range(2):
                sp.dma_start(rows_in[u][:, :], sorted_rows[u]).then_inc(in_loaded[u], 16)
                sp.sem_inc(y_stored[u], 16)
            with sp.Fori(0, STEPS) as it:
                done, two_done = sp.snap(it + 1), sp.snap(it + 2)
                tile = [sp.snap(it * 2 + u) for u in range(2)]
                nxt = [sp.snap((it * 2 + 2 + u) % NTILE) for u in range(2)]
                for u in range(2):
                    sp.wait_ge(in_ps[u], done)
                    sp.dma_start(rows_in[u][:, :], sorted_rows[nxt[u]]).then_inc(in_loaded[u], 16)
                for u in range(2):
                    sp.wait_ge(y_sb[u], two_done)
                    sp.dma_start(result[tile[u]], y_out[u][:, :]).then_inc(y_stored[u], 16)
            for u in range(2):
                sp.wait_ge(in_loaded[u], 16 * (STEPS + 1))
            for t in range(NT):
                sp.wait_ge(mixed, t + 1)
                sp.dma_start(out[t], t2_all[:, t, :]).then_inc(stored, 16)
            sp.wait_ge(stored, 16 * NT)

        @block.gpsimd
        def _(gp):
            gp.memset(ones[:, :], 1.0)
            for u in range(2):
                ins = gp.memset(rows_t[u][:, :, :], 1.0)
            ins.then_inc(pool_c, 1)
            gp.wait_ge(routed, 1)
            gp.wait_ge(xn_loaded, 16)
            for t in range(NT):
                for s in range(2):
                    gp.indirect_dma_start(
                        out=xs_dram, out_offset=bass.IndirectOffsetOnAxis(ap=pos[:, s * NT + t:s * NT + t + 1], axis=0),
                        in_=xn_all[:, t, :], in_offset=None).then_inc(scattered, 16)
            for u in range(2):
                gp.wait_ge(y_stored[u], 16 * (STEPS + 1))
            for t in range(NT):
                for s in range(2):
                    gp.indirect_dma_start(
                        out=y_sel[:, s, t, :], out_offset=None, in_=ys_dram,
                        in_offset=bass.IndirectOffsetOnAxis(ap=pos[:, s * NT + t:s * NT + t + 1], axis=0)
                        ).then_inc(gathered[t // 4], 16)

        @block.scalar
        def _(ac):
            ac.wait_ge(exp_in, 1)
            ac.activation(gates[:, :, :], place[:, :, :], ACT.Exp).then_inc(exp_out, 1)

            def copy_w1(u, e):
                ac.copy(w1_tile[u][:, 0, :], w1[:, bass.ds(e, 1), 0, :].rearrange("p e f -> p (e f)")
                        ).then_inc(w1_first[u], 1)

            ac.wait_ge(w_loaded, 16 * (2 * NE + 1))
            ac.wait_ge(experts_known, 1)
            for u, e in enumerate(experts_of(ac, 0, False)):
                copy_w1(u, e)
            with ac.Fori(0, STEPS) as it:
                done = ac.snap(it + 1)
                e = experts_of(ac, it, True)
                for u in range(2):
                    ac.wait_ge(h_ps[u], done)
                    ac.activation(hid_t[u][:, :, :].rearrange("p (b f) n -> p b (f n)", b=2),
                                  ps[u][:, 1:3, 0:FT // 2 * P], ACT.Gelu).then_inc(h_sb[u], 1)
                for u in range(2):
                    copy_w1(u, e[u])

        @block.vector
        def _(dv):
            count = [0]

            def step(ins):
                count[0] += 1
                ins.then_inc(dve_c, 1)
                dv.wait_ge(dve_c, count[0])

            def over(x, shape, axis):
                return x.unsqueeze(axis).to_broadcast(shape)

            TE = [P, NT, NE]
            dv.wait_ge(c_in, 48)
            step(dv.tensor_reduce(row[:, :], logits[:, :, :], AX.X, ALU.max))
            dv.tensor_tensor(place[:, :, :], logits[:, :, :], over(row[:, :], TE, 2), ALU.subtract).then_inc(exp_in, 1)
            dv.wait_ge(exp_out, 1)
            step(dv.tensor_reduce(row[:, :], gates[:, :, :], AX.X, ALU.add))
            step(dv.reciprocal(row[:, :], row[:, :]))
            step(dv.tensor_tensor(gates[:, :, :], gates[:, :, :], over(row[:, :], TE, 2), ALU.mult))
            for t in range(NT):
                ins = dv.max(top[:, t, :], gates[:, t, :])
            step(ins)
            for t in range(NT):
                ins = dv.max_index(top_at[:, t, :], top[:, t, :], gates[:, t, :])
            step(ins)
            step(dv.tensor_copy(chosen[:, :, :], top_at[:, :, 0:2]))
            for s in range(2):
                ins = dv.tensor_tensor(hot[:, s], numbers[:, 0:NE].unsqueeze(1).to_broadcast(TE),
                                       over(chosen[:, :, s], TE, 2), ALU.is_equal)
            step(ins)
            dv.tensor_tensor(both[:, :, :], hot[:, 0], hot[:, 1], ALU.add).then_inc(choice, 1)
            step(dv.tensor_tensor(row2[:, :], top[:, :, 0], top[:, :, 1], ALU.add))
            step(dv.tensor_scalar(row2[:, :], row2[:, :], 1e-9, None, ALU.add))
            step(dv.reciprocal(row2[:, :], row2[:, :]))
            for s in range(2):
                ins = dv.tensor_tensor(weight[:, s, :], top[:, :, s], row2[:, :], ALU.mult)
            step(ins)
            dv.wait_ge(counted, 1)
            step(dv.tensor_copy(counts[:, :, :], ps[0][:, 0:2, 0:NT * NE]))
            step(dv.memset(seen[:, 0, :], 0.0))
            total = counts[:, 1, :].rearrange("p (t e) -> p t e", e=NE)
            for t in range(NT):
                step(dv.tensor_tensor(seen[:, t + 1, :], seen[:, t, :], total[:, t, :], ALU.add))
            step(dv.tensor_tensor(full[:, :, :], over(seen[:, NT, :], [P, NE, NT], 2),
                                  starts[:, :].unsqueeze(1).to_broadcast([P, NE, NT]), ALU.is_gt))
            step(dv.tensor_reduce(tiles_of[:, :], full[:, :, :], AX.X, ALU.add))
            step(dv.memset(first[:, :], 0.0))
            for e in range(NE):
                step(dv.tensor_tensor(first[:, e + 1:e + 2], first[:, e:e + 1], tiles_of[:, e:e + 1], ALU.add))
            TL = [P, NTILE, NE - 1]
            step(dv.tensor_tensor(past[:, :, :], over(numbers[:, :], TL, 2),
                                  first[:, 1:NE].unsqueeze(1).to_broadcast(TL), ALU.is_ge))
            step(dv.tensor_reduce(expert_f[:, :], past[:, :, :], AX.X, ALU.add))
            dv.tensor_copy(expert[:, :], expert_f[:, :]).then_inc(experts_known, 1)
            step(dv.tensor_tensor(place[:, :, :], counts[:, 0, :].rearrange("p (t e) -> p t e", e=NE),
                                  seen[:, 0:NT, :], ALU.add))
            step(dv.scalar_tensor_tensor(out=place[:, :, :], in0=first[:, 0:NE].unsqueeze(1).to_broadcast(TE),
                                         scalar=float(P), in1=place[:, :, :], op0=ALU.mult, op1=ALU.add))
            for s in range(2):
                step(dv.tensor_tensor(place_s[:, :, :], place[:, :, :], hot[:, s], ALU.mult))
                step(dv.tensor_reduce(pos_f[:, s, :], place_s[:, :, :], AX.X, ALU.add))
            dv.tensor_copy(pos[:, :], pos_f[:, :, :].rearrange("p s t -> p (s t)")).then_inc(routed, 1)

            def rows_to_channels(u, reached):
                dv.wait_ge(in_ps[u], reached)
                dv.tensor_copy(rows_t[u][0:DC, :, :], ps[u][0:DC, 0, 0:2 * P].rearrange("p (c n) -> p c n", c=2)
                               ).then_inc(in_t[u], 1)

            dv.wait_ge(pool_c, 1)
            dv.wait_ge(w_loaded, 16 * (2 * NE + 1))
            dv.wait_ge(experts_known, 1)

            def copy_w1(u, e):
                dv.tensor_copy(w1_tile[u][0:DC, 1, :], w1[0:DC, bass.ds(e, 1), 1, :].rearrange("p e f -> p (e f)")
                               ).then_inc(w1_second[u], 1)

            for u, e in enumerate(experts_of(dv, 0, False)):
                copy_w1(u, e)
            for u in range(2):
                dv.sem_inc(y_sb[u], 1)
                rows_to_channels(u, 1)
            with dv.Fori(0, STEPS) as it:
                done, two_done, stored_before = dv.snap(it + 1), dv.snap(it + 2), dv.snap(it * 16 + 16)
                e, e_next = experts_of(dv, it, False), experts_of(dv, it, True)
                for u in range(2):
                    rows_to_channels(u, two_done)
                for u in range(2):
                    dv.wait_ge(h_ps[u], done)
                    copy_w1(u, e_next[u])
                for u in range(2):
                    dv.wait_ge(y_ps[u], done)
                    dv.wait_ge(y_stored[u], stored_before)
                    dv.tensor_tensor(y_out[u][:, :], ps[u][:, 3, 0:D],
                                     b2[:, bass.ds(e[u], 1), :].rearrange("p e d -> p (e d)"), ALU.add
                                     ).then_inc(y_sb[u], 1)
            dv.wait_ge(t2_loaded, 16)
            for t in range(NT):
                dv.wait_ge(gathered[t // 4], 16 * 8)
                step(dv.scalar_tensor_tensor(out=t2_all[:, t, :], in0=y_sel[:, 0, t, :], scalar=weight[:, 0, t:t + 1],
                                             in1=t2_all[:, t, :], op0=ALU.mult, op1=ALU.add))
                dv.scalar_tensor_tensor(out=t2_all[:, t, :], in0=y_sel[:, 1, t, :], scalar=weight[:, 1, t:t + 1],
                                        in1=t2_all[:, t, :], op0=ALU.mult, op1=ALU.add).then_inc(mixed, 1)

        @block.tensor
        def _(pe):
            pe.wait_ge(pool_c, 1)
            pe.wait_ge(c_in, 48)
            pe.wait_ge(choice, 1)
            pairs = both[:, :, :].rearrange("p t e -> p (t e)")
            pe.matmul(ps[0][:, 0, 0:NT * NE], before[:, :], pairs, start=True, stop=True)
            pe.matmul(ps[0][:, 1, 0:NT * NE], ones[:, :], pairs, start=True, stop=True).then_inc(counted, 1)
            pe.wait_ge(routed, 1)
            pe.wait_ge(w_loaded, 16 * (2 * NE + 1))
            pe.wait_ge(experts_known, 1)

            def transpose_rows(u, reached):
                pe.wait_ge(in_loaded[u], reached)
                for c in range(2):
                    ins = pe.transpose(ps[u][0:DC, 0, c * P:(c + 1) * P], rows_in[u][:, c * DC:(c + 1) * DC],
                                       ident[:, :])
                ins.then_inc(in_ps[u], 1)

            for u in range(2):
                transpose_rows(u, 16)
            with pe.Fori(0, STEPS) as it:
                done, loaded = pe.snap(it + 1), pe.snap(it * 16 + 32)
                e = experts_of(pe, it, False)
                for u in range(2):
                    pe.wait_ge(in_t[u], done)
                    pe.wait_ge(w1_first[u], done)
                    pe.wait_ge(w1_second[u], done)
                    for f in range(FT):
                        dst = ps[u][:, 1 + f // 3, f % 3 * P:(f % 3 + 1) * P]
                        cols = slice(f * P, (f + 1) * P)
                        pe.matmul(dst, w1_tile[u][:, 0, cols], rows_t[u][:, 0, :], start=True, stop=False)
                        ins = pe.matmul(dst, w1_tile[u][0:DC, 1, cols], rows_t[u][0:DC, 1, :],
                                        start=False, stop=True)
                    ins.then_inc(h_ps[u], 1)
                for u in range(2):
                    transpose_rows(u, loaded)
                for u in range(2):
                    pe.wait_ge(h_sb[u], done)
                    pe.wait_ge(y_sb[u], done)
                    for f in range(FT):
                        ins = pe.matmul(ps[u][:, 3, 0:D], hid_t[u][:, f, :], w2[:, bass.ds(e[u], 1), f, :],
                                        start=(f == 0), stop=(f == FT - 1))
                    ins.then_inc(y_ps[u], 1)


def _layouts(i):
    f = np.float32

    def rows(w, bias=None):
        out = np.zeros((DC + (bias is not None), 2, w.shape[1]), f)
        out[:DC, 0], out[:DC, 1] = w[:DC], w[DC:]
        if bias is not None:
            out[DC, 0] = bias
        return out

    def head_rows(w, bias):
        out = np.zeros((P, GROUPS, w.shape[1]), f)
        for h in range(HEADS):
            r = 32 * (h % 4)
            out[r:r + HD, h // 4] = w[h * HD:(h + 1) * HD]
        out[HD, 0] = bias
        return out

    tables = np.zeros((P, 2 * WS, P), f)
    for e in range(2):
        s = SLOT * e
        for at in range(WS):
            for c in range(HD):
                tables[s + c, at, s + 2 * c:s + 2 * c + 2] = 1.0
            for r in range(MAXROW + 1, SLOT):
                tables[s + r, at, s + r] = 1.0
            for key in range(WS):
                tables[s:s + HD, at, s + REL + key] = i["L0_conv_rel_pos_h"][at - key + WS - 1]
                tables[s:s + HD, WS + at, s + REL + WS + key] = i["L0_conv_rel_pos_w"][at - key + WS - 1]
    slot_rows = np.zeros((P, KEYS), f)
    slot_rows_q = np.zeros((P, TOK), f)
    for e in range(2):
        s = SLOT * e
        keys = [(y, x, -1) for y in range(WS) for x in range(WS)]
        keys += [(y, x - WS, 0) for y in range(WS) for x in range(WS, S)]
        keys += [(y - WS, x % WS, 1 + x // WS) for y in range(WS, S) for x in range(S)]
        keys += [(y, x, 3) for y in range(WS) for x in range(WS)]
        left = S - WS
        for n, (y, x, w) in enumerate(keys):
            slot_rows[s + REL + y, n] = 1.0
            slot_rows[s + REL + WS + x, n] = 1.0
            slot_rows[s + MAXROW, n] = 1.0
            if w >= 0:
                ok = (x >= left, y >= left, y >= left or x >= left) if w == 3 else (w == 0, w == 1, w == 2)
                for m in range(3):
                    slot_rows[s + MAXROW + 1 + m, n] = 0.0 if ok[m] else -BIG
        for y in range(S):
            for x in range(S):
                if y >= WS or x >= WS:
                    m = 0 if y < WS else 1 if x < WS else 2
                    slot_rows_q[s + MAXROW + 1 + m, y * S + x] = 1.0
    later = np.where(np.arange(P)[None, :] > np.arange(P)[:, None], f(-BIG), f(0))
    masks = np.stack([later, later, later.T, later.T], 1).reshape(P, 4 * P)
    qkv_b = i["L0_conv_qkv_b"]
    heads = [i[f"L1_attn_W_{n}"].transpose(1, 0, 2).reshape(D, D) for n in "qkv"]
    norms = np.zeros((DC, 8), f)
    for n, name in enumerate(("norm1_w", "norm1_b", "norm2_w", "norm2_b")):
        norms[:, 2 * n:2 * n + 2] = i[f"L0_conv_{name}"].reshape(2, DC).T
    e_w1 = np.zeros((DC + 1, NE, 2, MLP), f)
    e_w1[:DC] = i["L1_ffn_w1"].reshape(NE, 2, DC, MLP).transpose(2, 0, 1, 3)
    e_w1[DC, :, 0] = i["L1_ffn_b1"]
    return {
        "x": i["x"].reshape(B, 2, P, D).transpose(0, 2, 1, 3),
        "w_qkv_a": rows(i["L0_conv_qkv_w"], qkv_b),
        "w_qkv_b": rows(np.concatenate(heads, 1)),
        "w_out_a": head_rows(i["L0_conv_proj_w"], i["L0_conv_proj_b"]),
        "w_out_b": head_rows(i["L1_attn_lin_w"].T, i["L1_attn_lin_b"]),
        "w_fc1": rows(i["L0_conv_fc1_w"]),
        "w_fc2": i["L0_conv_fc2_w"].reshape(FT, P, D).transpose(1, 0, 2),
        "b_fc1": i["L0_conv_fc1_b"].reshape(FT, P).T,
        "b_fc2": np.tile(i["L0_conv_fc2_b"], (P, 2)),
        "norms": norms,
        "w_gate": rows(i["L1_ffn_gate_w"], i["L1_ffn_gate_b"]),
        "k_bias": qkv_b[D:2 * D].reshape(2, DC).T,
        "v_bias": np.tile(qkv_b[2 * D:], (P, 1)),
        "rel_tables": tables,
        "slot_rows": slot_rows,
        "slot_rows_q": slot_rows_q,
        "masks": masks,
        "ident": np.eye(P, dtype=f),
        "before": np.triu(np.ones((P, P), f), 1),
        "starts": np.tile(np.arange(NT, dtype=f) * P, (P, 1)),
        "numbers": np.tile(np.arange(NTILE, dtype=f), (P, 1)),
        "e_w1": e_w1,
        "e_w2": i["L1_ffn_w2"].reshape(NE, FT, P, D).transpose(2, 0, 1, 3),
        "e_b2": i["L1_ffn_b2"].reshape(1, NE, D),
    }


def kernel(**inputs):
    import concourse.bacc as bacc
    from concourse.bass_utils import run_bass_kernel_spmd

    nc = bacc.Bacc("TRN2", target_bir_lowering=False, num_devices=1)
    arrays, aps = {}, {}
    for name, value in _layouts({k: np.asarray(v) for k, v in inputs.items()}).items():
        value = np.ascontiguousarray(value)
        arrays[f"in_{name}"] = value
        aps[name] = nc.dram_tensor(f"in_{name}", value.shape, mybir.dt.from_np(value.dtype),
                                   kind="ExternalInput").ap()
    result = nc.dram_tensor("result", (NT, P, D), F32, kind="ExternalOutput").ap()
    build(nc, aps, result)
    run = run_bass_kernel_spmd(nc, [arrays], core_ids=[0])
    return run.results[0]["result"].reshape(B, S, S, D)
```
